# Optimizing a Trainium2 kernel written in Bass

```python
import numpy as np
import jax
import jax.numpy as jnp

def _softmax(x, axis=-1):
    return jax.nn.softmax(x, axis=axis)

def _gelu(x):
    return jax.nn.gelu(x, approximate=True)

def _silu(x):
    return jax.nn.silu(x)

def _sigmoid(x):
    return jax.nn.sigmoid(x)

def _layernorm(x, axis=-1, eps=1e-05):
    m = jnp.mean(x, axis=axis, keepdims=True)
    v = jnp.var(x, axis=axis, keepdims=True)
    return (x - m) / jnp.sqrt(v + eps)

def _scatter_add(tgt, idx, src, axis=0):
    return tgt.at[idx].add(src)

def _segment_sum(src, seg, n):
    return jax.ops.segment_sum(src, seg, n)
kernel_name = 'mk_xattn_ffn_d1_seqx_r4_efa178'

def setup_inputs(seed: int=0):
    np.random.seed(seed)
    _w = jnp.asarray

    def _rec_inputs():
        import jax
        import jax.numpy as jnp
        _rk = jax.random.key(seed)
        x = -0.0005146 + 1 * jax.random.normal(jax.random.fold_in(_rk, 1), (4, 1024, 256), jnp.float32)
        _lenS = 1024 - jax.random.randint(jax.random.fold_in(_rk, 7), (4,), 0, max(1, 1024 // 4) + 1, jnp.int32)
        _lenS2 = 77 - jax.random.randint(jax.random.fold_in(_rk, 8), (4,), 0, max(1, 77 // 4) + 1, jnp.int32)
        _ctx_1024P = jax.random.normal(jax.random.fold_in(_rk, 11), (4, 16, 256), jnp.float32)
        _ctx_1024c = jax.random.dirichlet(jax.random.fold_in(_rk, 511), 0.3 * jnp.ones((16,), jnp.float32), (4, 77))
        _ctx_1024t = jnp.einsum('bsk,bkd->bsd', _ctx_1024c, _ctx_1024P)
        _ctx_1024t = _ctx_1024t * jax.lax.rsqrt(jnp.mean(jnp.square(_ctx_1024t)) + 1e-12) * 0.953939
        ctx_1024 = -0.000392918 + 0.999932 * (_ctx_1024t + 0.3 * jax.random.normal(jax.random.fold_in(_rk, 611), (4, 77, 256), jnp.float32))
        _validS = jnp.arange(1024)[None, :] < _lenS[:, None]
        _validS2 = jnp.arange(77)[None, :] < _lenS2[:, None]
        _causal = jnp.tril(jnp.ones((1024, 1024), dtype=bool))
        mask_BxS2_bf1 = jnp.ones((4, 77), dtype=bool)
        return (x, ctx_1024, mask_BxS2_bf1)
    x, ctx_1024, mask_BxS2_bf1 = _rec_inputs()

    def _L0_xattn_setup():
        import jax, jax.numpy as jnp
        import numpy as np
        DIM = 256
        DIM_LATENT = 256
        DIM_HEAD = 64
        HEADS = 16
        INNER = HEADS * DIM_HEAD

        def layernorm(x, g, b, eps=1e-05):
            m = jnp.mean(x, axis=-1, keepdims=True)
            v = jnp.mean((x - m) ** 2, axis=-1, keepdims=True)
            return (x - m) / jnp.sqrt(v + eps) * g + b

        def rmsnorm(x, gamma, eps=1e-08):
            n = jnp.linalg.norm(x, axis=-1, keepdims=True) * x.shape[-1] ** (-0.5)
            return x / jnp.maximum(n, eps) * gamma
        key = jax.random.key(seed)
        ks = jax.random.split(key, 8)
        b, n, m = (4, 1024, 128)
        x = jax.random.normal(ks[0], (b, n, DIM), dtype=jnp.float32)
        latents = jax.random.normal(ks[1], (b, m, DIM_LATENT), dtype=jnp.float32)
        mask = jnp.ones((b, n), dtype=bool)
        s = 0.02
        return {'x': x, 'latents': latents, 'mask': mask, 'ln_x_g': jnp.ones((DIM,), jnp.float32), 'ln_x_b': jnp.zeros((DIM,), jnp.float32), 'ln_l_g': jnp.ones((DIM_LATENT,), jnp.float32), 'ln_l_b': jnp.zeros((DIM_LATENT,), jnp.float32), 'qn_g': jnp.ones((DIM_HEAD,), jnp.float32), 'kn_g': jnp.ones((DIM_HEAD,), jnp.float32), 'Wq': jax.random.normal(ks[2], (DIM_LATENT, INNER), jnp.float32) * s, 'Wkv': jax.random.normal(ks[3], (DIM, 2 * INNER), jnp.float32) * s, 'Wout': jax.random.normal(ks[4], (INNER, DIM_LATENT), jnp.float32) * s, 'bout': jnp.zeros((DIM_LATENT,), jnp.float32)}
    _L0_xattn_all = _L0_xattn_setup()
    _L0_xattn_in = {k: v for k, v in _L0_xattn_all.items() if k in ('ln_x_g', 'ln_x_b', 'ln_l_g', 'ln_l_b', 'qn_g', 'kn_g', 'Wq', 'Wkv', 'Wout', 'bout')}
    del _L0_xattn_all

    def _L0_ffn_setup():
        import jax, jax.numpy as jnp
        import numpy as np
        import math
        N_EMBD = 256
        HIDDEN = 4 * N_EMBD
        N_EXPERTS = 8
        TOP_K = 2
        B, T = (4, 512)

        def new_gelu(x):
            c = math.sqrt(2.0 / math.pi)
            return 0.5 * x * (1.0 + jnp.tanh(c * (x + 0.044715 * x * x * x)))

        def _moe_forward(x, Wfc_s, bfc_s, Wproj_s, bproj_s, Wr, Wfc, bfc, Wproj, bproj):
            Bb, Tt, C = x.shape
            xf = x.reshape(Bb * Tt, C)
            N = Bb * Tt
            shared = new_gelu(xf @ Wfc_s + bfc_s) @ Wproj_s + bproj_s
            logits = xf @ Wr
            probs = jax.nn.softmax(logits, axis=-1)
            topk_p, topk_i = jax.lax.top_k(probs, TOP_K)
            topk_p = topk_p / jnp.sum(topk_p, axis=-1, keepdims=True)
            gate = jnp.zeros((N, N_EXPERTS), dtype=xf.dtype)
            gate = gate.at[jnp.arange(N)[:, None], topk_i].add(topk_p)
            routed = jnp.zeros_like(xf)
            for e in range(N_EXPERTS):
                h = new_gelu(xf @ Wfc[e] + bfc[e]) @ Wproj[e] + bproj[e]
                routed = routed + h * gate[:, e:e + 1]
            return (shared + routed).reshape(Bb, Tt, C)
        key = jax.random.key(seed)
        ks = jax.random.split(key, 10)
        s = 0.02
        return {'x': jax.random.normal(ks[0], (B, T, N_EMBD), dtype=jnp.float32), 'Wfc_s': jax.random.normal(ks[1], (N_EMBD, HIDDEN), dtype=jnp.float32) * s, 'bfc_s': jnp.zeros((HIDDEN,), dtype=jnp.float32), 'Wproj_s': jax.random.normal(ks[2], (HIDDEN, N_EMBD), dtype=jnp.float32) * s, 'bproj_s': jnp.zeros((N_EMBD,), dtype=jnp.float32), 'Wr': jax.random.normal(ks[3], (N_EMBD, N_EXPERTS), dtype=jnp.float32) * s, 'Wfc': jax.random.normal(ks[4], (N_EXPERTS, N_EMBD, HIDDEN), dtype=jnp.float32) * s, 'bfc': jnp.zeros((N_EXPERTS, HIDDEN), dtype=jnp.float32), 'Wproj': jax.random.normal(ks[5], (N_EXPERTS, HIDDEN, N_EMBD), dtype=jnp.float32) * s, 'bproj': jnp.zeros((N_EXPERTS, N_EMBD), dtype=jnp.float32)}
    _L0_ffn_all = _L0_ffn_setup()
    _L0_ffn_in = {k: v for k, v in _L0_ffn_all.items() if k in ('Wfc_s', 'bfc_s', 'Wproj_s', 'bproj_s', 'Wr', 'Wfc', 'bfc', 'Wproj', 'bproj')}
    del _L0_ffn_all
    return {'x': x, 'ctx_1024': ctx_1024, 'mask_BxS2_bf1': mask_BxS2_bf1, 'L0_xattn_ln_x_g': _L0_xattn_in['ln_x_g'], 'L0_xattn_ln_x_b': _L0_xattn_in['ln_x_b'], 'L0_xattn_ln_l_g': _L0_xattn_in['ln_l_g'], 'L0_xattn_ln_l_b': _L0_xattn_in['ln_l_b'], 'L0_xattn_qn_g': _L0_xattn_in['qn_g'], 'L0_xattn_kn_g': _L0_xattn_in['kn_g'], 'L0_xattn_Wq': _L0_xattn_in['Wq'], 'L0_xattn_Wkv': _L0_xattn_in['Wkv'], 'L0_xattn_Wout': _L0_xattn_in['Wout'], 'L0_xattn_bout': _L0_xattn_in['bout'], 'L0_ffn_Wfc_s': _L0_ffn_in['Wfc_s'], 'L0_ffn_bfc_s': _L0_ffn_in['bfc_s'], 'L0_ffn_Wproj_s': _L0_ffn_in['Wproj_s'], 'L0_ffn_bproj_s': _L0_ffn_in['bproj_s'], 'L0_ffn_Wr': _L0_ffn_in['Wr'], 'L0_ffn_Wfc': _L0_ffn_in['Wfc'], 'L0_ffn_bfc': _L0_ffn_in['bfc'], 'L0_ffn_Wproj': _L0_ffn_in['Wproj'], 'L0_ffn_bproj': _L0_ffn_in['bproj']}

def reference(x, ctx_1024, mask_BxS2_bf1, L0_xattn_ln_x_g, L0_xattn_ln_x_b, L0_xattn_ln_l_g, L0_xattn_ln_l_b, L0_xattn_qn_g, L0_xattn_kn_g, L0_xattn_Wq, L0_xattn_Wkv, L0_xattn_Wout, L0_xattn_bout, L0_ffn_Wfc_s, L0_ffn_bfc_s, L0_ffn_Wproj_s, L0_ffn_bproj_s, L0_ffn_Wr, L0_ffn_Wfc, L0_ffn_bfc, L0_ffn_Wproj, L0_ffn_bproj):
    import jax
    import jax.numpy as jnp

    def _L0_xattn_ref(x, latents, mask, ln_x_g, ln_x_b, ln_l_g, ln_l_b, qn_g, kn_g, Wq, Wkv, Wout, bout):
        import jax, jax.numpy as jnp
        import numpy as np
        DIM = 256
        DIM_LATENT = 256
        DIM_HEAD = 64
        HEADS = 16
        INNER = HEADS * DIM_HEAD

        def layernorm(x, g, b, eps=1e-05):
            m = jnp.mean(x, axis=-1, keepdims=True)
            v = jnp.mean((x - m) ** 2, axis=-1, keepdims=True)
            return (x - m) / jnp.sqrt(v + eps) * g + b

        def rmsnorm(x, gamma, eps=1e-08):
            n = jnp.linalg.norm(x, axis=-1, keepdims=True) * x.shape[-1] ** (-0.5)
            return x / jnp.maximum(n, eps) * gamma
        b, n, _ = x.shape
        m = latents.shape[1]
        h, d = (HEADS, DIM_HEAD)
        scale = d ** (-0.5)
        xn = layernorm(x, ln_x_g, ln_x_b)
        ln = layernorm(latents, ln_l_g, ln_l_b)
        q = (ln @ Wq).reshape(b, m, h, d).transpose(0, 2, 1, 3)
        kv = jnp.concatenate([xn @ Wkv, ln @ Wkv], axis=1)
        kv = kv.reshape(b, n + m, 2, h, d)
        k = kv[:, :, 0].transpose(0, 2, 1, 3)
        v = kv[:, :, 1].transpose(0, 2, 1, 3)
        qn = rmsnorm(q, qn_g) * scale
        kn = rmsnorm(k, kn_g)
        sim = jnp.einsum('bhid,bhjd->bhij', qn, kn)
        max_neg = -jnp.finfo(sim.dtype).max
        padded_mask = jnp.concatenate([mask, jnp.ones((b, m), bool)], axis=1)
        sim = jnp.where(padded_mask[:, None, None, :], sim, max_neg)
        attn = jax.nn.softmax(sim.astype(jnp.float32), axis=-1).astype(sim.dtype)
        out = jnp.einsum('bhij,bhjd->bhid', attn, v)
        out = out.transpose(0, 2, 1, 3).reshape(b, m, h * d)
        return out @ Wout + bout

    def _L0_ffn_ref(x, Wfc_s, bfc_s, Wproj_s, bproj_s, Wr, Wfc, bfc, Wproj, bproj):
        import jax, jax.numpy as jnp
        import numpy as np
        import math
        N_EMBD = 256
        HIDDEN = 4 * N_EMBD
        N_EXPERTS = 8
        TOP_K = 2
        B, T = (4, 512)

        def new_gelu(x):
            c = math.sqrt(2.0 / math.pi)
            return 0.5 * x * (1.0 + jnp.tanh(c * (x + 0.044715 * x * x * x)))

        def _moe_forward(x, Wfc_s, bfc_s, Wproj_s, bproj_s, Wr, Wfc, bfc, Wproj, bproj):
            Bb, Tt, C = x.shape
            xf = x.reshape(Bb * Tt, C)
            N = Bb * Tt
            shared = new_gelu(xf @ Wfc_s + bfc_s) @ Wproj_s + bproj_s
            logits = xf @ Wr
            probs = jax.nn.softmax(logits, axis=-1)
            topk_p, topk_i = jax.lax.top_k(probs, TOP_K)
            topk_p = topk_p / jnp.sum(topk_p, axis=-1, keepdims=True)
            gate = jnp.zeros((N, N_EXPERTS), dtype=xf.dtype)
            gate = gate.at[jnp.arange(N)[:, None], topk_i].add(topk_p)
            routed = jnp.zeros_like(xf)
            for e in range(N_EXPERTS):
                h = new_gelu(xf @ Wfc[e] + bfc[e]) @ Wproj[e] + bproj[e]
                routed = routed + h * gate[:, e:e + 1]
            return (shared + routed).reshape(Bb, Tt, C)
        return _moe_forward(x, Wfc_s, bfc_s, Wproj_s, bproj_s, Wr, Wfc, bfc, Wproj, bproj)
    x = x + _L0_xattn_ref(ctx_1024, _layernorm(x, axis=-1), mask_BxS2_bf1, L0_xattn_ln_x_g, L0_xattn_ln_x_b, L0_xattn_ln_l_g, L0_xattn_ln_l_b, L0_xattn_qn_g, L0_xattn_kn_g, L0_xattn_Wq, L0_xattn_Wkv, L0_xattn_Wout, L0_xattn_bout)
    x = x + _L0_ffn_ref(_layernorm(x, axis=-1), L0_ffn_Wfc_s, L0_ffn_bfc_s, L0_ffn_Wproj_s, L0_ffn_bproj_s, L0_ffn_Wr, L0_ffn_Wfc, L0_ffn_bfc, L0_ffn_Wproj, L0_ffn_bproj)
    return x

_drawn_inputs = setup_inputs


def setup_inputs(seed=0):
    import zlib

    import numpy as np

    out = dict(_drawn_inputs(seed))
    spreads = {'L0_xattn_ln_x_g': (1.0, 0.6),
     'L0_xattn_ln_x_b': (0.0, 2.0),
     'L0_xattn_ln_l_g': (1.0, 0.6),
     'L0_xattn_ln_l_b': (0.0, 0.347),
     'L0_xattn_qn_g': (1.0, 0.6),
     'L0_xattn_kn_g': (1.0, 0.6),
     'L0_xattn_bout': (0.0, 0.1),
     'L0_ffn_bfc_s': (0.0, 0.1),
     'L0_ffn_bproj_s': (0.0, 0.1),
     'L0_ffn_bfc': (0.0, 0.323),
     'L0_ffn_bproj': (0.0, 0.1)}
    factors = {'ctx_1024': 13.637}
    for name, (base, spread) in spreads.items():
        noise = np.random.default_rng([zlib.crc32(name.encode()), seed]).standard_normal(out[name].shape)
        drawn = base * np.exp(spread * noise) if base else spread * noise
        out[name] = jnp.asarray(drawn.astype(out[name].dtype))
    for name, factor in factors.items():
        out[name] = (out[name] * factor).astype(out[name].dtype)
    return out
```

```python
from contextlib import ExitStack

import concourse.bass as bass
from concourse import mybir

F32 = mybir.dt.float32
F32R = mybir.dt.float32r
I32 = mybir.dt.int32
U32 = mybir.dt.uint32
U8 = mybir.dt.uint8
ALU = mybir.AluOpType
ACT = mybir.ActivationFunctionType
AX = mybir.AxisListType

P = 128
B, N, D = 4, 1024, 256
CTX = 77
H, DH = 16, 64
C = D // P
NT = N // P
KT = NT + 1
KEYS = KT * P
QB = N // 512
HEADS = B * H
LN_EPS, RMS_EPS = 1e-5, 1e-8
NEG = -1e30
TOKENS = B * N
TT = TOKENS // P
GT = 2
E = 8
HID = 4 * D
HC = HID // P
TS = 2 * P
SHARED = TOKENS // TS
ROUTED = (2 * TOKENS + E * (TS - 1)) // TS
ROUTED += ROUTED % 2
ROWS = (ROUTED + 1) * TS


class Tools:

    def __init__(self, nc, ctx):
        self.nc, self.ctx = nc, ctx

    def sb(self, name, shape, dt=F32):
        return self.ctx.enter_context(self.nc.sbuf_tensor(name, shape, dt))

    def ps(self, name, shape):
        return self.ctx.enter_context(self.nc.psum_tensor(name, shape, F32))

    def sem(self, name):
        return self.ctx.enter_context(self.nc.semaphore(name))


def step(eng, sem, count, ins):
    ins.then_inc(sem, 1)
    count[0] += 1
    eng.wait_ge(sem, count[0])


def prepare(nc, x, ctx_in, mask, ln_x_g, ln_x_b, ln_l_g, ln_l_b, Wq, Wkv, lnT, wHead, maskRow, maskCol):
    with ExitStack() as ctx:
        t = Tools(nc, ctx)
        ident = t.sb("ident", [P, P])
        xin = t.sb("xin", [P, 2, NT, D])
        z = t.sb("z", [P, NT, D])
        cz = t.sb("cz", [CTX, B, D])
        stats = t.sb("stats", [P, NT, 6])
        mv = t.sb("mv", [P, NT, 2])
        var_eps = t.sb("var_eps", [P, NT])
        rstd = t.sb("rstd", [P, NT])
        half = t.sb("half", [P, NT])
        gain = t.sb("gain", [P, 4, C])
        full = t.sb("full", [P, 2, 512])
        out = t.sb("out", [P, 2, C, KEYS], F32R)
        w = t.sb("w", [P, C, 3 * H * DH])
        wh = t.sb("wh", [P, H, 2, C, 3 * DH], F32R)
        mk8 = t.sb("mk8", [P, B], U8)
        mkf = t.sb("mkf", [P, B])
        mr8 = t.sb("mr8", [B, P], U8)
        mrf = t.sb("mrf", [B, P], F32R)
        tp = t.ps("tp", [P, 2, 512])
        s_x = [t.sem("s_x0"), t.sem("s_x1")]
        s_c, s_w, s_g, s_m = t.sem("s_c"), t.sem("s_w"), t.sem("s_g"), t.sem("s_m")
        s_id, s_ve, s_rs, s_z, s_cz = t.sem("s_id"), t.sem("s_ve"), t.sem("s_rs"), t.sem("s_z"), t.sem("s_cz")
        s_tp, s_full, s_fullfree, s_split = t.sem("s_tp"), t.sem("s_full"), t.sem("s_fullfree"), t.sem("s_split")
        s_out, s_whi, s_wlo, s_mk, s_wout = t.sem("s_out"), t.sem("s_whi"), t.sem("s_wlo"), t.sem("s_mk"), t.sem("s_wout")
        s_v, s_lnT = t.sem("s_v"), t.sem("s_lnT")
        block = ctx.enter_context(nc.Block())
        x_v = x.rearrange("b (t p) d -> b p t d", p=P)
        GROUPS = [(c, g) for c in range(C) for g in range(2)]
        JOBS = len(GROUPS) + C

        @block.sync
        def _(sp):
            sp.dma_start(xin[:, 0], x_v[0]).then_inc(s_x[0], 16)
            sp.dma_start(w[:, :, 0:H * DH], Wq.rearrange("(c p) n -> p c n", p=P)).then_inc(s_w, 16)
            sp.dma_start(w[:, :, H * DH:], Wkv.rearrange("(c p) n -> p c n", p=P)).then_inc(s_w, 16)
            for b in range(B):
                if b + 1 < B:
                    if b >= 1:
                        sp.wait_ge(s_z, b)
                    sp.dma_start(xin[:, (b + 1) % 2], x_v[b + 1]).then_inc(s_x[(b + 1) % 2], 16)
                sp.wait_ge(s_split, 2 * JOBS * (b + 1))
                sp.dma_start(lnT[b], out[:, :, :, :].bitcast(F32)).then_inc(s_lnT, 16)
                if b == 0:
                    sp.wait_ge(s_mk, 2)
                    sp.dma_start(maskRow, mrf[:, :].bitcast(F32)).then_inc(s_out, 16)
                    sp.dma_start(maskCol, mkf[:, :]).then_inc(s_out, 16)
                    sp.wait_ge(s_whi, 6)
                    sp.wait_ge(s_wlo, 6)
                    sp.dma_start(wHead.rearrange("h p s c n -> p h s c n"), wh[:, :, :, :, :].bitcast(F32)).then_inc(s_out, 16)
            sp.wait_ge(s_lnT, 16 * B)
            sp.wait_ge(s_out, 48)

        @block.gpsimd
        def _(pool):
            pool.dma_start(cz[:, :, :], ctx_in.rearrange("b k d -> k b d")).then_inc(s_c, 16)
            pool.memset(ident[:, :], 0.0).then_inc(s_id, 1)
            pool.memset(half[:, :], -0.5).then_inc(s_id, 1)
            pool.memset(mk8[:, :], 0).then_inc(s_id, 1)
            pool.memset(mr8[:, :], 0).then_inc(s_id, 1)
            pool.wait_ge(s_id, 4)
            pool.dma_start(mk8[0:CTX, :], mask.rearrange("b k -> k b"), allow_slow_non_contiguous=True).then_inc(s_m, 16)
            pool.dma_start(mr8[:, 0:CTX], mask).then_inc(s_m, 16)
            for i, v in enumerate((ln_l_g, ln_l_b, ln_x_g, ln_x_b)):
                pool.dma_start(gain[:, i, :], v.rearrange("(c p) -> p c", p=P), allow_slow_non_contiguous=True).then_inc(s_g, 16)
            pool.affine_select(out=ident[:, :], in_=ident[:, :], compare_op=ALU.not_equal, fill=1.0,
                               base=0, pattern=[[-1, P]], channel_multiplier=1).then_inc(s_id, 1)
            pool.wait_ge(s_ve, 1)
            pool.tensor_tensor(rstd[0:CTX, 0:B], var_eps[0:CTX, 0:B], half[0:CTX, 0:B], ALU.pow).then_inc(s_rs, 1)
            for k in range(2 * B):
                pool.wait_ge(s_ve, k + 2)
                pool.tensor_tensor(rstd[:, :], var_eps[:, :], half[:, :], ALU.pow).then_inc(s_rs, 1)

        @block.vector
        def _(dve):
            n = [0]
            v = nc.vector

            def statistics(src, rows, tiles):
                for i in range(tiles):
                    v.bn_stats(stats[0:rows, i, :], src(i)).then_inc(s_v, 1)
                n[0] += tiles
                dve.wait_ge(s_v, n[0])
                for i in range(tiles):
                    v.bn_aggr(mv[0:rows, i, :], stats[0:rows, i, :]).then_inc(s_v, 1)
                n[0] += tiles
                dve.wait_ge(s_v, n[0])
                v.tensor_scalar(var_eps[0:rows, 0:tiles], mv[0:rows, 0:tiles, 1], LN_EPS, None, ALU.add).then_inc(s_ve, 1)

            def normalise(dst, src, rows, tiles, k, done):
                dve.wait_ge(s_rs, k)
                for i in range(tiles):
                    ins = v.tensor_scalar(dst(i), src(i), mv[0:rows, i, 0:1], rstd[0:rows, i:i + 1],
                                          ALU.subtract, ALU.mult)
                    if done is not None and i == tiles - 1:
                        ins.then_inc(done, 1)
                    else:
                        ins.then_inc(s_v, 1)
                        n[0] += 1
                dve.wait_ge(s_v, n[0])

            dve.wait_ge(s_c, 16)
            statistics(lambda b: cz[:, b, :], CTX, B)
            normalise(lambda b: cz[:, b, :], lambda b: cz[:, b, :], CTX, B, 1, s_cz)
            dve.wait_ge(s_m, 32)
            dve.wait_ge(s_id, 4)
            v.tensor_scalar(mkf[:, :], mk8[:, :], -NEG, NEG, ALU.mult, ALU.add).then_inc(s_mk, 1)
            v.tensor_scalar(mrf[:, :], mr8[:, :], -NEG, NEG, ALU.mult, ALU.add).then_inc(s_mk, 1)
            v.memset(out[:, :, :, N + CTX:KEYS].bitcast(F32), 0.0).then_inc(s_v, 1)
            n[0] += 1
            dve.wait_ge(s_g, 64)
            for b in range(B):
                dve.wait_ge(s_x[b % 2], 16 * (b // 2 + 1))
                src = lambda i: xin[:, b % 2, i, :]
                dst = lambda i: z[:, i, :]
                statistics(src, P, NT)
                normalise(src, src, P, NT, 2 * b + 2, None)
                statistics(src, P, NT)
                if b:
                    dve.wait_ge(s_tp, JOBS * b)
                normalise(dst, src, P, NT, 2 * b + 3, s_z)
                if b:
                    dve.wait_ge(s_lnT, 16 * b)
                for j in range(JOBS):
                    jj = JOBS * b + j
                    c = GROUPS[j][0] if j < 4 else j - 4
                    lo, n_ = (512 * GROUPS[j][1], 512) if j < 4 else (N, CTX)
                    dve.wait_ge(s_full, jj + 1)
                    f = full[:, jj % 2, 0:n_]
                    v.tensor_copy(out[:, 0, c, lo:lo + n_], f).then_inc(s_split, 1)
                    dve.wait_ge(s_split, 2 * jj + 1)
                    v.tensor_tensor(out[:, 1, c, lo:lo + n_], f, out[:, 0, c, lo:lo + n_].bitcast(F32),
                                    ALU.subtract).then_inc(s_split, 1)
                if b == 0:
                    for k in range(6):
                        c, part = k // 3, k % 3
                        hi, lo_ = (wh[:, :, s, c, part * DH:(part + 1) * DH] for s in range(2))
                        src_w = w[:, c, part * H * DH:(part + 1) * H * DH].rearrange("p (h d) -> p h d", d=DH)
                        dve.wait_ge(s_whi, k + 1)
                        v.tensor_tensor(lo_, src_w, hi.bitcast(F32), ALU.subtract).then_inc(s_wlo, 1)

        @block.tensor
        def _(pe):
            pe.wait_ge(s_id, 5)
            for b in range(B):
                pe.wait_ge(s_z, b + 1)
                if b == 0:
                    pe.wait_ge(s_cz, 1)
                for j in range(JOBS):
                    jj = JOBS * b + j
                    if jj >= 2:
                        pe.wait_ge(s_full, jj - 1)
                    if j < 4:
                        c, g = GROUPS[j]
                        for i in range(4):
                            ins = nc.tensor.transpose(tp[:, jj % 2, i * P:(i + 1) * P],
                                                      z[:, 4 * g + i, c * P:(c + 1) * P], ident[:, :])
                    else:
                        c = j - 4
                        ins = nc.tensor.transpose(tp[:, jj % 2, 0:CTX], cz[:, b, c * P:(c + 1) * P],
                                                  ident[0:CTX, 0:CTX])
                    ins.then_inc(s_tp, 1)

        @block.scalar
        def _(act):
            act.wait_ge(s_w, 32)
            for k in range(6):
                c, part = k // 3, k % 3
                act.activation(wh[:, :, 0, c, part * DH:(part + 1) * DH],
                               w[:, c, part * H * DH:(part + 1) * H * DH].rearrange("p (h d) -> p h d", d=DH),
                               ACT.Copy).then_inc(s_whi, 1)
            act.wait_ge(s_g, 64)
            for jj in range(B * JOBS):
                j = jj % JOBS
                c = GROUPS[j][0] if j < 4 else j - 4
                n_, kind = (512, 0) if j < 4 else (CTX, 2)
                act.wait_ge(s_tp, jj + 1)
                if jj >= 2:
                    act.wait_ge(s_split, 2 * (jj - 1))
                act.activation(full[:, jj % 2, 0:n_], tp[:, jj % 2, 0:n_], ACT.Identity,
                               scale=gain[:, kind, c:c + 1], bias=gain[:, kind + 1, c:c + 1]).then_inc(s_full, 1)


PLAN = [["P0", "P1"], ["P2", "P3"], ["K10", "P4"], ["K11", "KK"], ["Q10", "P5"], ["Q11", "P6"],
        ["M00", "P7"], ["M01", "P8"], ["M10", "C0"], ["M11", "M20"], ["M21", "M30"], ["M31", "K20"], ["M40", "M41"],
        ["M50", "K21", "M51"], ["M60", "Q20", "M61"], ["M70", "C1", "M71"], [], ["Q21"]]
RING = 3
LAG = 2
UNITS = QB * KT
assert len(PLAN) == UNITS
MISC = [j for u in PLAN for j in u]
BANKS = 3
REDUCED = [j for j in MISC if j[0] in "MC"]
COPIES = [j for j in MISC if j[0] not in "MC"]
assert len(MISC) % BANKS == 0 and KT % BANKS == 0


class Window:

    PER = {"misc": len(MISC), "copy": len(COPIES), "reduce": len(REDUCED), "unit": UNITS, "block": QB,
           "proj": 1, "split": 1, "one": 1}
    PRE = {"misc": len(MISC) + KT, "copy": len(COPIES) + KT, "reduce": len(REDUCED), "unit": 0, "block": 0,
           "proj": 2, "split": 1, "one": 0}

    def __init__(self, v, s):
        self.v, self.s = v, s
        self.n = s if v is None else None
        self.slot, self.other = s % 2, (s + 1) % 2
        self.attend = v is not None
        self.turn = v is not None or s == -1
        self.first = v is not None and isinstance(v, int) and v == 0 and s == 0

    def count(self, kind, k=0, times=1):
        per, pre = self.PER[kind], self.PRE[kind]
        if self.v is None:
            before = 0 if self.s == -2 else {"misc": KT, "copy": KT, "proj": 1}.get(kind, 0)
            return times * (before + k)
        return self.v * (2 * per * times) + times * (pre + self.s * per + k)

    def here(self):
        return MISC if self.turn else [j for j in MISC if j[0] == "P"]

    def taken(self, name):
        kind = "reduce" if name in REDUCED else "copy"
        mine = [j for j in self.here() if (j in REDUCED) == (name in REDUCED)]
        return kind, self.count(kind, mine.index(name) + 1)

    def copied(self, name):
        return self.taken(name)[1]

    def freed(self, m):
        if m >= BANKS:
            return self.taken(self.here()[m - BANKS])
        if self.n == -2:
            return None
        before = MISC if self.n != -1 else [j for j in MISC if j[0] == "P"]
        name, after = before[m - BANKS], before[len(before) + m - BANKS + 1:]
        return ("reduce" if name in REDUCED else "copy",
                self.count("reduce" if name in REDUCED else "copy",
                           -sum((j in REDUCED) == (name in REDUCED) for j in after)))

    def jobs(self, u):
        here = self.here()
        return [(j, here.index(j)) for j in PLAN[u] if j in here]


def windows(eng, body, last=None):
    body(Window(None, -2))
    body(Window(None, -1))
    for s in range(2):
        body(Window(0, s))
    with eng.Fori(1, HEADS // 2) as v:
        for s in range(2):
            body(Window(v, s))
    if last is not None:
        last(Window(HEADS // 2, 0))


def attention(nc, qn_g, kn_g, lnT, wHead, maskRow, maskCol, attT, routed):
    with ExitStack() as ctx:
        t = Tools(nc, ctx)
        ident = t.sb("a_ident", [P, P])
        lnT_sb = t.sb("lnT_sb", [P, 2, C, KEYS], F32R)
        w_sb = t.sb("w_sb", [P, 2, 2, C, 3 * DH], F32R)
        raw = t.sb("raw", [P, 2, KT, 3 * DH])
        sq = t.sb("sq", [P, KT, 2 * DH])
        ss = t.sb("ss", [P, 2 * KT])
        rs = t.sb("rs", [P, 2 * KT])
        minus_half = t.sb("minus_half", [P, 2 * KT])
        nrm = t.sb("nrm", [P, KT, 2, DH])
        gq = t.sb("gq", [P, DH])
        gk = t.sb("gk", [P, DH])
        gqk = t.sb("gqk", [P, DH])
        k_st = t.sb("k_st", [P, 2, KT, 2 * DH + 2], F32R)
        q_st = t.sb("q_st", [P, 2, NT, 3 * DH + 2], F32R)
        kT1 = t.sb("kT1", [P, 2, KEYS], F32R)
        kT2 = t.sb("kT2", [P, 2, KEYS], F32R)
        qT1 = t.sb("qT1", [P, 2, N], F32R)
        qT2 = t.sb("qT2", [P, 2, N], F32R)
        vA = t.sb("vA", [P, 2, KT, 2 * DH], F32R)
        vC = t.sb("vC", [P, 2, KT, 2 * DH], F32R)
        one_row = t.sb("one_row", [P, P], F32R)
        mrow = t.sb("mrow", [P, 2, P], F32R)
        mcol = t.sb("mcol", [P, 2])
        pr = t.sb("pr", [P, RING, 512])
        pr_hi = t.sb("pr_hi", [P, RING, 512], F32R)
        pr_lo = t.sb("pr_lo", [P, RING, 512], F32R)
        maxima = t.sb("maxima", [P, NT, 3])
        o_sb = t.sb("o_sb", [DH + 1, 2, 512])
        zero = t.sb("zero", [P, D])
        ps_s = t.ps("ps_s", [P, RING, 512])
        ps_o = t.ps("ps_o", [P, QB, 512])
        ps_m = t.ps("ps_m", [P, BANKS, 512])
        s_id, s_g, s_gd, s_const = t.sem("a_id"), t.sem("a_g"), t.sem("a_gd"), t.sem("a_const")
        s_ln, s_lnready = t.sem("a_ln"), t.sem("a_lnready")
        s_w = [t.sem("a_w0"), t.sem("a_w1")]
        s_mask = [t.sem("a_mask0"), t.sem("a_mask1")]
        s_misc, s_copy, s_reduce, s_negmax = t.sem("a_misc"), t.sem("a_copy"), t.sem("a_reduce"), t.sem("a_negmax")
        s_sq, s_ss, s_nrm, s_hi, s_lo = t.sem("a_sq"), t.sem("a_ss"), t.sem("a_nrm"), t.sem("a_hi"), t.sem("a_lo")
        s_vhi, s_vlo, s_pool = t.sem("a_vhi"), t.sem("a_vlo"), t.sem("a_pool")
        s_scores, s_exp, s_prlo, s_pv = t.sem("a_scores"), t.sem("a_exp"), t.sem("a_prlo"), t.sem("a_pv")
        s_o = [t.sem("a_o0"), t.sem("a_o1")]
        s_store = [t.sem("a_store0"), t.sem("a_store1")]
        s_zero, s_clear = t.sem("a_zero"), t.sem("a_clear")
        block = ctx.enter_context(nc.Block())

        @block.sync
        def _(sp):
            def load_ln(b):
                sp.dma_start(lnT_sb[:, :, :, :].bitcast(F32).unsqueeze(1),
                             lnT[bass.ds(b, 1)].rearrange("b p s c k -> p b s c k")).then_inc(s_ln, 16)

            def load_w(head, slot):
                sp.dma_start(w_sb[:, slot:slot + 1].bitcast(F32),
                             wHead[bass.ds(head, 1)].rearrange("h p s c n -> p h s c n")).then_inc(s_w[slot], 16)

            def load_mask(b, slot):
                sp.dma_start(mrow[0:1, slot, :].bitcast(F32), maskRow[bass.ds(b, 1), :]).then_inc(s_mask[slot], 16)
                sp.dma_start(mcol[:, slot:slot + 1], maskCol[:, bass.ds(b, 1)], allow_slow_non_contiguous=True).then_inc(s_mask[slot], 16)

            load_ln(0)
            load_w(0, 0)
            load_w(1, 1)
            sp.wait_ge(s_ln, 16)
            sp.sem_inc(s_lnready, 1)
            sp.wait_ge(s_copy, KT)
            load_w(2, 0)
            sp.wait_ge(s_const, 3)
            load_mask(0, 0)
            sp.wait_ge(s_copy, Window(None, -1).copied("P8"))
            load_w(3, 1)

            def store(head, q):
                sp.wait_ge(s_o[q], head + 1)
                sp.dma_start(attT[bass.ds(head, 1), :, q * 512:(q + 1) * 512].rearrange("h d n -> d h n"),
                             o_sb[:, q:q + 1, :]).then_inc(s_store[q], 16)

            def pair(v, b=None):
                if b is not None:
                    sp.wait_ge(s_ln, b * 16 + 16)
                sp.sem_inc(s_lnready, 1)
                for s in range(2):
                    w = Window(v, s)
                    mb, head = (v + s) // 8 % B, (v * 2 + s + 4) % H
                    sp.wait_ge(s_exp, w.count("unit"))
                    load_mask(mb, w.other)
                    if not w.first:
                        store(v * 2 + s - 1, 1)
                    sp.wait_ge(s_copy, w.copied("P8"))
                    load_w(head, w.slot)
                    store(v * 2 + s, 0)

            pair(0)
            with sp.Fori(1, 7) as v:
                pair(v)
            with sp.Fori(1, B) as b:
                load_ln(b)
                with sp.Fori(0, 8) as k:
                    pair(b * 8 + k - 1, b)
            pair(HEADS // 2 - 1)
            store(HEADS - 1, 1)
            sp.wait_ge(s_clear, 16)
            for q in range(QB):
                sp.wait_ge(s_store[q], 16 * HEADS)
            for s in range(2):
                sp.wait_ge(s_w[s], 16 * (HEADS // 2 + 2))
                sp.wait_ge(s_mask[s], 32 * (HEADS // 2 + (s == 0)))

        @block.gpsimd
        def _(pool):
            g = nc.gpsimd
            pool.memset(ident[:, :], 0.0).then_inc(s_id, 1)
            pool.wait_ge(s_id, 1)
            pool.affine_select(out=ident[:, :], in_=ident[:, :], compare_op=ALU.not_equal, fill=1.0,
                               base=0, pattern=[[-1, P]], channel_multiplier=1).then_inc(s_id, 1)
            pool.memset(minus_half[:, :], -0.5).then_inc(s_pool, 1)
            pool.dma_start(gq[:, :], qn_g.rearrange("(a d) -> a d", a=1).broadcast_to([P, DH])).then_inc(s_g, 16)
            pool.dma_start(gk[:, :], kn_g.rearrange("(a d) -> a d", a=1).broadcast_to([P, DH])).then_inc(s_g, 16)
            pool.wait_ge(s_const, 4)

            def window(w):
                if w.turn:
                    pool.wait_ge(s_hi, w.count("split", 1, 2))
                    g.tensor_tensor(k_st[:, w.other, :, 0:DH], nrm[:, :, 1, :],
                                    k_st[:, w.other, :, DH:2 * DH].bitcast(F32), ALU.subtract).then_inc(s_lo, 1)
                    g.tensor_tensor(q_st[:, w.other, :, 2 * DH:3 * DH], nrm[:, 0:NT, 0, :],
                                    q_st[:, w.other, :, 0:DH].bitcast(F32), ALU.subtract).then_inc(s_lo, 1)
                    pool.wait_ge(s_vhi, w.count("split", 1))
                    g.tensor_tensor(vC[:, w.other, :, 0:DH], raw[:, w.other, :, 2 * DH:3 * DH],
                                    vA[:, w.other, :, 0:DH].bitcast(F32), ALU.subtract).then_inc(s_vlo, 1)
                pool.wait_ge(s_copy, w.copied("P8"))
                qk = raw[:, w.slot, :, 0:2 * DH]
                g.tensor_tensor(sq[:, :, :], qk, qk, ALU.mult).then_inc(s_sq, 1)
                pool.wait_ge(s_ss, w.count("proj", 1, 2))
                g.tensor_tensor(rs[:, :], ss[:, :], minus_half[:, :], ALU.pow).then_inc(s_pool, 1)
                pool.wait_ge(s_pool, w.count("proj", 0, 2) + 2)
                g.tensor_tensor(nrm[:, :, :, :], qk.rearrange("p t (j d) -> p t j d", d=DH),
                                rs[:, :].rearrange("p (t j) -> p t j", j=2).unsqueeze(3).broadcast_to([P, KT, 2, DH]),
                                ALU.mult).then_inc(s_pool, 1)
                pool.wait_ge(s_pool, w.count("proj", 0, 2) + 3)
                g.tensor_tensor(nrm[:, 0:NT, 0, :], nrm[:, 0:NT, 0, :],
                                gqk[:, :].unsqueeze(1).broadcast_to([P, NT, DH]), ALU.mult).then_inc(s_nrm, 1)

            windows(pool, window)

        @block.vector
        def _(dve):
            v = nc.vector
            v.memset(zero[:, :], 0.0).then_inc(s_zero, 1)
            v.memset(k_st[:, :, :, 2 * DH:2 * DH + 2].bitcast(F32), 1.0).then_inc(s_const, 1)
            v.memset(one_row[:, :].bitcast(F32), 0.0).then_inc(s_const, 1)
            v.memset(mrow[:, :, :].bitcast(F32), 0.0).then_inc(s_const, 1)
            dve.wait_ge(s_g, 32)
            dve.wait_ge(s_const, 3)
            v.scalar_tensor_tensor(gqk[:, :], gq[:, :], DH ** 0.5, gk[:, :], ALU.mult, ALU.mult).then_inc(s_const, 1)
            v.memset(one_row[0:1, :].bitcast(F32), 1.0).then_inc(s_const, 1)
            v.memset(vA[:, :, :, DH:2 * DH].bitcast(F32), 1.0).then_inc(s_const, 1)
            v.memset(vC[:, :, :, DH:2 * DH].bitcast(F32), 0.0).then_inc(s_const, 1)

            def negmax(w, half):
                a = slice(4 * half, 4 * half + 4)
                dve.wait_ge(s_reduce, w.taken("M71" if half else "M31")[1])
                v.tensor_reduce(q_st[:, w.other, a, 3 * DH], maxima[:, a, :], AX.X, ALU.min).then_inc(s_negmax, 1)

            def output(w, q, before=0):
                dve.wait_ge(s_pv, w.count("unit", KT * (q + 1) - before * UNITS))
                dve.wait_ge(s_store[q], w.count("one", -before, 16))
                v.tensor_copy(o_sb[:, q, :], ps_o[0:DH + 1, q, :]).then_inc(s_o[q], 1)

            def window(w):
                for u in range(UNITS):
                    for name, m in w.jobs(u):
                        if name not in REDUCED:
                            continue
                        dve.wait_ge(s_misc, w.count("misc", m + 1))
                        j, bank = int(name[1]), ps_m[:, m % BANKS, :]
                        if name[0] == "M":
                            g = int(name[2])
                            v.tensor_reduce(maxima[:, j, g:g + 1], bank, AX.X, ALU.max, negate=True).then_inc(s_reduce, 1)
                        else:
                            v.tensor_reduce(maxima[:, 4 * j:4 * j + 4, 2], bank.rearrange("p (t k) -> p t k", k=P),
                                            AX.X, ALU.max, negate=True).then_inc(s_reduce, 1)
                        if name in ("M31", "M71"):
                            negmax(w, name == "M71")
                    if w.attend:
                        dve.wait_ge(s_exp, w.count("unit", u + 1))
                        v.tensor_tensor(pr_lo[:, u % RING, :], pr[:, u % RING, :], pr_hi[:, u % RING, :].bitcast(F32),
                                        ALU.subtract).then_inc(s_prlo, 1)
                    if u == 0 and w.turn:
                        dve.wait_ge(s_nrm, w.count("proj"))
                        v.tensor_copy(k_st[:, w.other, :, DH:2 * DH], nrm[:, :, 1, :]).then_inc(s_hi, 1)
                        v.tensor_copy(q_st[:, w.other, :, 0:2 * DH].rearrange("p t (j d) -> p t j d", d=DH),
                                      nrm[:, 0:NT, 0, :].unsqueeze(2).broadcast_to([P, NT, 2, DH])).then_inc(s_hi, 1)
                    if u == 4 and w.turn:
                        if w.attend:
                            dve.wait_ge(s_pv, w.count("unit"))
                        dve.wait_ge(s_copy, w.count("copy"))
                        v.tensor_copy(vA[:, w.other, :, 0:DH], raw[:, w.other, :, 2 * DH:3 * DH]).then_inc(s_vhi, 1)
                    if u == 11:
                        dve.wait_ge(s_sq, w.count("proj", 1))
                        v.tensor_reduce(ss[:, :], sq[:, :, :].rearrange("p t (j d) -> p (t j) d", d=DH),
                                        AX.X, ALU.add).then_inc(s_ss, 1)
                        dve.wait_ge(s_ss, w.count("proj", 0, 2) + 1)
                        v.tensor_scalar(ss[:, :], ss[:, :], DH * RMS_EPS ** 2, None, ALU.max).then_inc(s_ss, 1)
                    if u == LAG and w.attend and not w.first:
                        output(w, 1, 1)
                    if u == KT + LAG and w.attend:
                        output(w, 0)

            windows(dve, window, lambda w: output(w, 1, 1))

        @block.scalar
        def _(act):
            def window(w):
                for u in range(UNITS):
                    if w.attend:
                        q, k = u // KT, u % KT
                        act.wait_ge(s_scores, w.count("unit", u + 1))
                        if k == KT - 1:
                            if q == 0:
                                act.wait_ge(s_mask[w.slot], w.v * 32 + 32)
                            bias = mcol[:, w.slot:w.slot + 1]
                        else:
                            bias = 0.0
                        act.activation(pr[:, u % RING, :], ps_s[:, u % RING, :], ACT.Exp, bias=bias)
                        act.activation(pr_hi[:, u % RING, :], ps_s[:, u % RING, :], ACT.Exp, bias=bias).then_inc(s_exp, 1)
                    for name, m in w.jobs(u):
                        if name in REDUCED:
                            continue
                        act.wait_ge(s_misc, w.count("misc", m + 1))
                        src = ps_m[:, m % BANKS, :]
                        if name[0] == "P":
                            if name == "P0" and w.attend:
                                act.wait_ge(s_vlo, w.count("split"))
                                act.wait_ge(s_nrm, w.count("proj"))
                            ins = act.activation(raw[:, w.slot, int(name[1]), :], src[:, 0:3 * DH], ACT.Copy)
                        elif name == "KK":
                            act.activation(kT1[:, w.other, N:KEYS], src[:, 0:P], ACT.Copy)
                            ins = act.activation(kT2[0:DH + 1, w.other, N:KEYS], src[0:DH + 1, P:2 * P], ACT.Copy)
                        else:
                            rows, dst = {"K1": (P, kT1), "K2": (DH + 1, kT2), "Q1": (P, qT1), "Q2": (DH + 1, qT2)}[name[:2]]
                            g = int(name[2])
                            ins = act.activation(dst[0:rows, w.other, 512 * g:512 * g + 512], src[0:rows, :], ACT.Copy)
                        ins.then_inc(s_copy, 1)

            act.wait_ge(s_zero, 1)
            act.dma_start(routed.rearrange("(t p) d -> p t d", p=P),
                          zero[:, :].unsqueeze(1).broadcast_to([P, ROWS // P, D])).then_inc(s_clear, 16)
            windows(act, window)

        @block.tensor
        def _(pe):
            mm = nc.tensor.matmul
            pe.wait_ge(s_id, 2)
            pe.wait_ge(s_const, 7)

            def project(w, tile, out):
                for k, (a, b, c) in enumerate((a, b, c) for a, b in ((0, 0), (0, 1), (1, 0)) for c in range(C)):
                    ins = mm(out[:, 0:3 * DH], lnT_sb[:, a, c, tile * P:(tile + 1) * P], w_sb[:, w.slot, b, c, :],
                             start=k == 0, stop=k == 3 * C - 1)
                return ins

            def values(w, u):
                slot = w.slot if u >= 0 else w.other
                q, k, r = u % UNITS // KT, u % KT, u % RING
                if k == 0:
                    pe.wait_ge(s_o[q], w.count("one"))
                pe.wait_ge(s_prlo, w.count("unit", u + 1))
                last = k == KT - 1
                mm(ps_o[:, q, :], vA[:, slot, k, :], pr_hi[:, r, :], start=k == 0, stop=False)
                mm(ps_o[:, q, :], vC[:, slot, k, :], pr_hi[:, r, :], start=False, stop=False)
                mm(ps_o[:, q, :], vA[:, slot, k, :], pr_lo[:, r, :], start=False, stop=last).then_inc(s_pv, 1)

            def transposes(w, out, src, tiles, lo, n_):
                for i, tile in enumerate(tiles):
                    ins = nc.tensor.transpose(out[0:n_, i * P:(i + 1) * P],
                                              src[:, w.other, tile, lo:lo + n_].bitcast(F32), ident[:, :])
                return ins

            def job(w, name, m):
                out = ps_m[:, m % BANKS, :]
                if w.freed(m):
                    kind, value = w.freed(m)
                    pe.wait_ge({"copy": s_copy, "reduce": s_reduce}[kind], value)
                if name[0] == "P":
                    if name == "P0":
                        if w.n is None:
                            pe.wait_ge(s_lnready, w.v + 2)
                            pe.wait_ge(s_w[w.slot], w.v * 16 + 32)
                        else:
                            pe.wait_ge(s_lnready, 1)
                            pe.wait_ge(s_w[w.slot], 16)
                    ins = project(w, int(name[1]), out)
                elif name[0] == "M":
                    j, g = int(name[1]), int(name[2])
                    if name in ("M00", "M40"):
                        pe.wait_ge(s_copy, w.copied("Q10" if j == 0 else "Q11"))
                    ins = mm(out, qT1[:, w.other, j * P:(j + 1) * P], kT1[:, w.other, 512 * g:512 * g + 512],
                             start=True, stop=True)
                elif name[0] == "C":
                    j = int(name[1])
                    if j == 0:
                        if w.n is None:
                            pe.wait_ge(s_mask[w.other], w.v * 32 + (32 if w.s == 0 else 64))
                        else:
                            pe.wait_ge(s_mask[w.other], 32)
                    pe.wait_ge(s_copy, w.copied("Q1%d" % j))
                    for i in range(4):
                        mm(out[:, i * P:(i + 1) * P], qT1[:, w.other, (4 * j + i) * P:(4 * j + i + 1) * P],
                           kT1[:, w.other, N:KEYS], start=True, stop=False)
                        ins = mm(out[:, i * P:(i + 1) * P], one_row[:, :], mrow[:, w.other, :], start=False, stop=True)
                elif name == "KK":
                    transposes(w, out, k_st, [KT - 1], 0, 2 * DH)
                    ins = transposes(w, out[:, P:2 * P], k_st, [KT - 1], DH, DH + 1)
                else:
                    g = int(name[2])
                    tiles = range(4 * g, 4 * g + 4)
                    if name in ("K10", "Q10"):
                        pe.wait_ge(s_lo, w.count("split", 1, 2) - (name == "K10"))
                    if name[:2] == "Q2":
                        pe.wait_ge(s_negmax, w.count("split", 0, 2) + g + 1)
                    src, lo, n_ = {"K1": (k_st, 0, 2 * DH), "K2": (k_st, DH, DH + 1),
                                   "Q1": (q_st, 0, 2 * DH), "Q2": (q_st, 2 * DH, DH + 1)}[name[:2]]
                    ins = transposes(w, out, src, tiles, lo, n_)
                ins.then_inc(s_misc, 1)

            def window(w):
                for u in range(UNITS):
                    if w.attend:
                        q, k = u // KT, u % KT
                        if u == 0:
                            pe.wait_ge(s_copy, w.count("copy"))
                            pe.wait_ge(s_vlo, w.count("split"))
                        mm(ps_s[:, u % RING, :], kT1[:, w.slot, k * P:(k + 1) * P],
                           qT1[:, w.slot, q * 512:(q + 1) * 512], start=True, stop=False)
                        mm(ps_s[:, u % RING, :], kT2[0:DH + 1, w.slot, k * P:(k + 1) * P],
                           qT2[0:DH + 1, w.slot, q * 512:(q + 1) * 512], start=False, stop=True).then_inc(s_scores, 1)
                    here = w.jobs(u)
                    for name, m in here[:1]:
                        job(w, name, m)
                    if w.attend and (u >= LAG or not w.first):
                        values(w, u - LAG)
                    for name, m in here[1:]:
                        job(w, name, m)

            def last(w):
                for u in range(LAG):
                    values(w, u - LAG)

            windows(pe, window, last)


def project_out(nc, x, Wout, bout, attT, rden, tokens, x2, l2):
    HP, G = H // 2, 4
    W = GT * P
    with ExitStack() as ctx:
        t = Tools(nc, ctx)
        dn = t.sb("dn", [HEADS, N])
        wo = t.sb("wo", [P, HP, D])
        wo_hi = t.sb("wo_hi", [P, HP, D], F32R)
        wo_lo = t.sb("wo_lo", [P, HP, D], F32R)
        bo = t.sb("bo", [P, D])
        a = t.sb("a", [P, 2, HP, W])
        rb = t.sb("rb", [P, 2, HP, W])
        a_hi = t.sb("a_hi", [P, 2, HP, W], F32R)
        a_lo = t.sb("a_lo", [P, 2, HP, W], F32R)
        xg = t.sb("xg", [P, 2, GT, D])
        stats = t.sb("o_stats", [P, GT, 6])
        mv = t.sb("o_mv", [P, GT, 2])
        var_eps = t.sb("o_var", [P, GT])
        rstd = t.sb("o_rstd", [P, GT])
        half = t.sb("o_half", [P, GT])
        marker = t.sb("marker", [P, 1])
        ps_y = t.ps("ps_y", [P, G * GT, 512])
        s_dn, s_rd, s_w, s_whi, s_wlo, s_bo, s_half = (t.sem("o_" + n) for n in ("dn", "rd", "w", "whi", "wlo", "bo", "half"))
        s_a, s_x, s_prod, s_xb, s_y, s_l2, s_lov, s_lop = ([t.sem("o_%s_%d" % (n, q)) for q in range(G)] for n in
                                                            ("a", "x", "prod", "xb", "y", "l2", "lov", "lop"))
        s_hi, s_x2, s_v, s_ve, s_rs, s_st = (t.sem("o_" + n) for n in ("hi", "x2", "v", "ve", "rs", "st"))
        block = ctx.enter_context(nc.Block())
        att_v = attT.rearrange("(b k r) d n -> b r d k n", b=B, r=2)
        rden_v = rden.rearrange("(b k r) n -> b r k n", b=B, r=2)
        x_v = x.rearrange("b (g t p) d -> (b g) p t d", t=GT, p=P)
        tokens_v = tokens.rearrange("(g t p) d -> g p t d", t=GT, p=P)
        HH = HP // 2

        def before(q, b):
            return (q - 2, b + 1) if q >= 2 else (q + 2, b)

        def batches(eng, batch):
            batch(0)
            with eng.Fori(1, B) as b:
                batch(b)

        @block.sync
        def _(sp):
            sp.dma_start(dn[:, :], attT[:, DH, :]).then_inc(s_dn, 16)
            sp.dma_start(wo[:, :, :], Wout.rearrange("(k p) n -> p k n", p=P)).then_inc(s_w, 16)
            sp.wait_ge(s_rd, 1)
            sp.dma_start(rden, dn[:, :]).then_inc(s_dn, 16)
            sp.wait_ge(s_dn, 32)
            def batch(b):
                for q in range(G):
                    g, done = before(q, b)
                    sp.wait_ge(s_lov[g], done)
                    sp.wait_ge(s_lop[g], done)
                    cols = slice(W * q, W * q + W)
                    for r in range(2):
                        p = slice(DH * r, DH * r + DH)
                        sp.dma_start(a[p, q % 2:q % 2 + 1], att_v[bass.ds(b, 1), r, 0:DH, :, cols]
                                     .rearrange("b d k n -> d b k n")).then_inc(s_a[q], 16)
                        sp.dma_start(rb[p, q % 2:q % 2 + 1], rden_v[bass.ds(b, 1), r, :, cols]
                                     .unsqueeze(0).broadcast_to([DH, 1, HP, W])).then_inc(s_a[q], 16)
                    sp.wait_ge(s_l2[g], done)
                    sp.dma_start(xg[:, q % 2:q % 2 + 1], x_v[bass.ds(b * G + q, 1)]
                                 .rearrange("g p t d -> p g t d")).then_inc(s_x[q], 16)

            batches(sp, batch)

        @block.gpsimd
        def _(pool):
            pool.dma_start(bo[:, :], bout.rearrange("(a d) -> a d", a=1).broadcast_to([P, D])).then_inc(s_bo, 16)
            pool.memset(half[:, :], -0.5).then_inc(s_half, 1)
            pool.wait_ge(s_half, 1)
            pool.wait_ge(s_bo, 16)
            def batch(b):
                for q in range(G):
                    pool.wait_ge(s_x[q], b * 16 + 16)
                    nc.gpsimd.tensor_tensor(xg[:, q % 2], xg[:, q % 2], bo[:, :].unsqueeze(1).broadcast_to([P, GT, D]),
                                            ALU.add).then_inc(s_xb[q], 1)
                    pool.wait_ge(s_hi, b * (2 * G) + 2 * q + 2)
                    nc.gpsimd.tensor_tensor(a_lo[:, q % 2, HH:, :], a[:, q % 2, HH:, :],
                                            a_hi[:, q % 2, HH:, :].bitcast(F32), ALU.subtract).then_inc(s_lop[q], 1)
                    pool.wait_ge(s_ve, b * G + q + 1)
                    nc.gpsimd.tensor_tensor(rstd[:, :], var_eps[:, :], half[:, :], ALU.pow).then_inc(s_rs, 1)
                    pool.wait_ge(s_l2[q], b + 1)
                    pool.dma_start(tokens_v[bass.ds(b * G + q, 1)].rearrange("g p t d -> p g t d"),
                                   l2[:, bass.ds((b * G + q) * GT, GT), :].unsqueeze(1)).then_inc(s_st, 16)

            batches(pool, batch)
            pool.wait_ge(s_st, 16 * G * B)

        @block.scalar
        def _(act):
            act.wait_ge(s_w, 16)
            act.activation(wo_hi[:, :, :], wo[:, :, :], ACT.Copy).then_inc(s_whi, 1)
            def batch(b):
                for q in range(G):
                    g, done = before(q, b)
                    act.wait_ge(s_y[g], done * GT)
                    for k in range(2):
                        act.wait_ge(s_prod[q], b * 2 + k + 1)
                        h = slice(HH * k, HH * k + HH)
                        act.activation(a_hi[:, q % 2, h, :], a[:, q % 2, h, :], ACT.Copy).then_inc(s_hi, 1)

            batches(act, batch)

        @block.vector
        def _(dve):
            v = nc.vector
            dve.wait_ge(s_dn, 16)
            v.reciprocal(dn[:, :], dn[:, :]).then_inc(s_rd, 1)
            dve.wait_ge(s_whi, 1)
            v.tensor_tensor(wo_lo[:, :, :], wo[:, :, :], wo_hi[:, :, :].bitcast(F32), ALU.subtract).then_inc(s_wlo, 1)

            def product(b, q):
                dve.wait_ge(s_a[q], b * 64 + 64)
                for k in range(2):
                    h = slice(HH * k, HH * k + HH)
                    v.tensor_tensor(a[:, q % 2, h, :], a[:, q % 2, h, :], rb[:, q % 2, h, :], ALU.mult).then_inc(s_prod[q], 1)
                dve.wait_ge(s_hi, b * (2 * G) + 2 * q + 1)
                v.tensor_tensor(a_lo[:, q % 2, 0:HH, :], a[:, q % 2, 0:HH, :], a_hi[:, q % 2, 0:HH, :].bitcast(F32),
                                ALU.subtract).then_inc(s_lov[q], 1)

            def batch(b):
                for q in range(G):
                    product(b, q)
                    dve.wait_ge(s_xb[q], b + 1)
                    group = b * G + q
                    for i in range(GT):
                        dve.wait_ge(s_y[q], b * GT + i + 1)
                        v.tensor_tensor(x2[:, bass.ds(group * GT + i, 1), :], ps_y[:, q * GT + i, 0:D].unsqueeze(1),
                                        xg[:, q % 2, i:i + 1, :], ALU.add).then_inc(s_x2, 1)
                    dve.wait_ge(s_x2, group * (2 * GT) + GT)
                    v.memset(marker[:, :], 0.0)
                    for i in range(GT):
                        v.bn_stats(stats[:, i, :], x2[:, bass.ds(group * GT + i, 1), :].rearrange("p a d -> p (a d)")).then_inc(s_x2, 1)
                    dve.wait_ge(s_x2, group * (2 * GT) + 2 * GT)
                    v.memset(marker[:, :], 0.0)
                    for i in range(GT):
                        ins = v.bn_aggr(mv[:, i, :], stats[:, i, :])
                    ins.then_inc(s_v, 1)
                    dve.wait_ge(s_v, group + 1)
                    v.tensor_scalar(var_eps[:, :], mv[:, :, 1], LN_EPS, None, ALU.add).then_inc(s_ve, 1)
                    dve.wait_ge(s_rs, group + 1)
                    for i in range(GT):
                        tile = bass.ds(group * GT + i, 1)
                        ins = v.tensor_scalar(l2[:, tile, :], x2[:, tile, :], mv[:, i, 0:1], rstd[:, i:i + 1],
                                              ALU.subtract, ALU.mult)
                    ins.then_inc(s_l2[q], 1)

            batches(dve, batch)

        @block.tensor
        def _(pe):
            pe.wait_ge(s_wlo, 1)
            def batch(b):
                for q in range(G):
                    pe.wait_ge(s_lov[q], b + 1)
                    pe.wait_ge(s_lop[q], b + 1)
                    pe.wait_ge(s_l2[q], b)
                    for i in range(GT):
                        n = 0
                        for k in range(HP):
                            for lhs, rhs in ((a_hi, wo_hi), (a_hi, wo_lo), (a_lo, wo_hi)):
                                ins = nc.tensor.matmul(ps_y[:, q * GT + i, 0:D], lhs[:, q % 2, k, i * P:(i + 1) * P],
                                                       rhs[:, k, :], start=n == 0, stop=n == 3 * HP - 1)
                                n += 1
                        ins.then_inc(s_y[q], 1)

            batches(pe, batch)


def route(nc, Wr, l2, slots, gates, expert):
    with ExitStack() as ctx:
        t = Tools(nc, ctx)
        ident = t.sb("r_ident", [P, P])
        before = t.sb("before", [P, P])
        ones = t.sb("ones", [P, P])
        wr = t.sb("wr", [P, C, E])
        l2T = t.sb("l2T", [P, 2, 2, C, P])
        eight = t.sb("eight", [P, TT, E])
        tiles = t.sb("tiles", [P, ROUTED + 2, E])
        logit = t.sb("logit", [P, TT, E])
        top = t.sb("top", [P, TT])
        prob = t.sb("prob", [P, TT, E])
        total = t.sb("total", [P, TT])
        best = t.sb("best", [P, TT, 8])
        index = t.sb("index", [P, TT, 8], U32)
        index_f = t.sb("index_f", [P, TT, 2])
        hot = t.sb("hot", [P, 2, TT, E])
        both = t.sb("both", [P, TT, E])
        cum = t.sb("cum", [P, 2, TT, E])
        base = t.sb("base", [P, TT, E])
        filled = t.sb("filled", [P, E])
        filled_i = t.sb("filled_i", [P, E], I32)
        end = t.sb("end", [P, E])
        start = t.sb("start", [P, E])
        pick = t.sb("pick", [P, 2, TT, E])
        slot_f = t.sb("slot_f", [P, 2, TT])
        reached = t.sb("reached", [P, ROUTED + 2, E])
        expert_f = t.sb("expert_f", [P, ROUTED + 2])
        ps_t = t.ps("r_ps_t", [P, 2, 512])
        ps_l = t.ps("r_ps_l", [P, 512])
        ps_c = t.ps("r_ps_c", [P, 2, 512])
        s_c, s_wr, s_t, s_tc, s_lg, s_v, s_e, s_cnt = (t.sem("r_" + n) for n in ("c", "wr", "t", "tc", "lg", "v", "e", "cnt"))
        s_in = t.sem("r_in")
        block = ctx.enter_context(nc.Block())

        @block.gpsimd
        def _(pool):
            pool.dma_start(wr[:, :, :], Wr.rearrange("(c p) e -> p c e", p=P)).then_inc(s_wr, 16)
            pool.memset(ident[:, :], 0.0).then_inc(s_c, 1)
            pool.memset(before[:, :], 1.0).then_inc(s_c, 1)
            pool.memset(ones[:, :], 1.0).then_inc(s_c, 1)
            pool.iota(eight[:, :, :], pattern=[[0, TT], [1, E]], base=0, channel_multiplier=0,
                      allow_small_or_imprecise_dtypes=True).then_inc(s_c, 1)
            pool.iota(tiles[:, :, :], pattern=[[1, ROUTED + 2], [0, E]], base=0, channel_multiplier=0,
                      allow_small_or_imprecise_dtypes=True).then_inc(s_c, 1)
            pool.wait_ge(s_c, 5)
            pool.affine_select(out=ident[:, :], in_=ident[:, :], compare_op=ALU.not_equal, fill=1.0,
                               base=0, pattern=[[-1, P]], channel_multiplier=1).then_inc(s_c, 1)
            pool.affine_select(out=before[:, :], in_=before[:, :], compare_op=ALU.is_gt, fill=0.0,
                               base=0, pattern=[[1, P]], channel_multiplier=-1).then_inc(s_c, 1)

        @block.tensor
        def _(pe):
            pe.wait_ge(s_c, 7)
            pe.wait_ge(s_wr, 16)
            for j in range(TT // 2 + 1):
                if j < TT // 2:
                    if j >= 2:
                        pe.wait_ge(s_tc, j - 1)
                    for i in range(2):
                        for c in range(C):
                            ins = nc.tensor.transpose(ps_t[:, j % 2, (2 * i + c) * P:(2 * i + c + 1) * P],
                                                      l2[:, 2 * j + i, c * P:(c + 1) * P], ident[:, :])
                    ins.then_inc(s_t, 1)
                if j:
                    pe.wait_ge(s_tc, j)
                    for i in range(2):
                        tile = 2 * (j - 1) + i
                        for c in range(C):
                            ins = nc.tensor.matmul(ps_l[:, tile * E:(tile + 1) * E], l2T[:, (j - 1) % 2, i, c, :],
                                                   wr[:, c, :], start=c == 0, stop=c == C - 1)
                    ins.then_inc(s_lg, 1)
            pe.wait_ge(s_cnt, 1)
            nc.tensor.matmul(ps_c[:, 0, 0:TT * E], before[:, :], both[:, :, :], start=True, stop=True)
            nc.tensor.matmul(ps_c[:, 1, 0:TT * E], ones[:, :], both[:, :, :], start=True, stop=True).then_inc(s_cnt, 1)

        @block.scalar
        def _(act):
            for j in range(TT // 2):
                act.wait_ge(s_t, j + 1)
                if j >= 2:
                    act.wait_ge(s_lg, j - 1)
                act.activation(l2T[:, j % 2], ps_t[:, j % 2, :].rearrange("p (i c n) -> p i c n", i=2, c=C),
                               ACT.Copy).then_inc(s_tc, 1)
            act.wait_ge(s_in, 1)
            act.activation(prob[:, :, :], logit[:, :, :], ACT.Exp).then_inc(s_e, 1)

        @block.vector
        def _(dve):
            v = nc.vector
            n = [0]

            def do(ins):
                step(dve, s_v, n, ins)

            tb = lambda ap: ap.unsqueeze(2).broadcast_to([P, TT, E])
            dve.wait_ge(s_lg, TT // 2)
            dve.wait_ge(s_c, 7)
            do(v.tensor_copy(logit[:, :, :], ps_l[:, 0:TT * E].rearrange("p (t e) -> p t e", e=E)))
            do(v.tensor_reduce(top[:, :], logit[:, :, :], AX.X, ALU.max))
            v.tensor_tensor(logit[:, :, :], logit[:, :, :], tb(top[:, :]), ALU.subtract).then_inc(s_in, 1)
            dve.wait_ge(s_e, 1)
            do(v.tensor_reduce(total[:, :], prob[:, :, :], AX.X, ALU.add))
            do(v.reciprocal(total[:, :], total[:, :]))
            do(v.tensor_tensor(prob[:, :, :], prob[:, :, :], tb(total[:, :]), ALU.mult))
            for i in range(TT):
                v.max(best[:, i, :], prob[:, i, :]).then_inc(s_v, 1)
            n[0] += TT
            dve.wait_ge(s_v, n[0])
            for i in range(TT):
                v.max_index(index[:, i, :], best[:, i, :], prob[:, i, :]).then_inc(s_v, 1)
            n[0] += TT
            dve.wait_ge(s_v, n[0])
            do(v.tensor_tensor(total[:, :], best[:, :, 0], best[:, :, 1], ALU.add))
            do(v.reciprocal(total[:, :], total[:, :]))
            do(v.tensor_tensor(gates[:, :, :], best[:, :, 0:2], total[:, :].unsqueeze(2).broadcast_to([P, TT, 2]), ALU.mult))
            do(v.tensor_copy(index_f[:, :, :], index[:, :, 0:2]))
            for k in range(2):
                do(v.tensor_tensor(hot[:, k], eight[:, :, :], tb(index_f[:, :, k]), ALU.is_equal))
            v.tensor_tensor(both[:, :, :], hot[:, 0], hot[:, 1], ALU.add).then_inc(s_cnt, 1)
            dve.wait_ge(s_cnt, 2)
            do(v.tensor_copy(cum[:, 0], ps_c[:, 1, 0:TT * E].rearrange("p (t e) -> p t e", e=E)))
            k, s = 0, 1
            while s < TT:
                do(v.tensor_copy(cum[:, 1 - k, 0:s, :], cum[:, k, 0:s, :]))
                do(v.tensor_tensor(cum[:, 1 - k, s:, :], cum[:, k, s:, :], cum[:, k, 0:TT - s, :], ALU.add))
                k, s = 1 - k, 2 * s
            do(v.tensor_scalar(filled[:, :], cum[:, k, TT - 1, :], float(TS - 1), None, ALU.add))
            do(v.tensor_copy(filled_i[:, :], filled[:, :]))
            do(v.tensor_scalar(filled_i[:, :], filled_i[:, :], TS.bit_length() - 1, None, ALU.logical_shift_right))
            do(v.tensor_copy(filled[:, :], filled_i[:, :]))
            do(v.tensor_copy(end[:, 0:1], filled[:, 0:1]))
            for e in range(1, E):
                do(v.tensor_tensor(end[:, e:e + 1], end[:, e - 1:e], filled[:, e:e + 1], ALU.add))
            do(v.tensor_tensor(start[:, :], end[:, :], filled[:, :], ALU.subtract))
            do(v.tensor_scalar(start[:, :], start[:, :], float(TS), None, ALU.mult))
            do(v.tensor_tensor(base[:, :, :], ps_c[:, 0, 0:TT * E].rearrange("p (t e) -> p t e", e=E),
                               start[:, :].unsqueeze(1).broadcast_to([P, TT, E]), ALU.add))
            do(v.tensor_tensor(base[:, 1:, :], base[:, 1:, :], cum[:, k, 0:TT - 1, :], ALU.add))
            for j in range(2):
                do(v.tensor_tensor(pick[:, j], hot[:, j], base[:, :, :], ALU.mult))
            do(v.tensor_reduce(slot_f[:, :, :], pick[:, :, :, :], AX.X, ALU.add))
            do(v.tensor_copy(slots[:, :, :], slot_f[:, :, :]))
            do(v.tensor_tensor(reached[:, :, :], tiles[:, :, :], end[:, :].unsqueeze(1).broadcast_to([P, ROUTED + 2, E]), ALU.is_ge))
            do(v.tensor_reduce(expert_f[:, :], reached[:, :, :], AX.X, ALU.add))
            do(v.tensor_scalar(expert_f[:, :], expert_f[:, :], float(E - 1), None, ALU.min))
            do(v.tensor_copy(expert[:, :], expert_f[:, :]))


def experts(nc, weights_s, weights, expert, slots, tokens, routed, x2, ys):
    Wfc, bfc, Wproj, bproj = weights
    with ExitStack() as ctx:
        t = Tools(nc, ctx)
        ident = t.sb("f_ident", [P, P])
        moved = t.sb("moved", [P, 4, D])
        xt = t.sb("xt", [P, 2, 2, D])
        xT_hi = t.sb("xT_hi", [P, 2, C, TS], F32R)
        xT_lo = t.sb("xT_lo", [P, 2, C, TS], F32R)
        w1 = t.sb("w1", [P, 2, C, HID])
        w2 = t.sb("w2", [P, 2, HC, D])
        b1 = t.sb("b1", [P, 2, HC])
        b2 = t.sb("b2", [P, 2, D])
        w1_hi = t.sb("w1_hi", [P, 2, C, HC, P], F32R)
        w1_lo = t.sb("w1_lo", [P, 2, C, HC, P], F32R)
        w2_hi = t.sb("w2_hi", [P, 2, HC, D], F32R)
        w2_lo = t.sb("w2_lo", [P, 2, HC, D], F32R)
        b1_use = t.sb("b1_use", [P, 2, HC])
        b2_use = t.sb("b2_use", [P, 2, D])
        ht = t.sb("ht", [P, 4, 2, TS])
        h_hi = t.sb("h_hi", [P, 2, HC, TS], F32R)
        h_lo = t.sb("h_lo", [P, 2, HC, TS], F32R)
        y = t.sb("y", [P, 2, 2, D])
        ps_t = t.ps("f_ps_t", [P, C, TS])
        ps_h = t.ps("f_ps_h", [P, 4, 2, TS])
        ps_y = t.ps("f_ps_y", [P, 2, 512])
        s_id = t.sem("f_id")
        s_wl, s_xl, s_ys = ([t.sem("f_%s%d" % (n, i)) for i in range(2)] for n in ("wl", "xl", "ys"))
        s_wh, s_w1l, s_w2l, s_xt, s_xh, s_xlo, s_h, s_y, s_yv = (t.sem("f_" + n) for n in
                                                                  ("wh", "w1l", "w2l", "xt", "xh", "xlo", "h", "y", "yv"))
        s_g, s_hh, s_hl = ([t.sem("f_%s%d" % (n, i)) for i in range(4)] for n in ("g", "hh", "hl"))
        s_b2, s_sum = t.sem("f_b2"), t.sem("f_sum")
        s_mv = [t.sem("f_mv%d" % i) for i in range(4)]
        s_sc = [t.sem("f_sc%d" % i) for i in range(4)]
        block = ctx.enter_context(nc.Block())
        tokens_v = tokens.rearrange("(t r p) d -> t p r d", r=2, p=P)
        routed_v = routed.rearrange("(t r p) d -> t p r d", r=2, p=P)
        ys_v = ys.rearrange("(t r p) d -> t p r d", r=2, p=P)

        def shared_pair(tile, u):
            for s in range(2):
                tile(u * 2, s, None, u)

        def routed_pair(tile, u):
            for s in range(2):
                tile(u * 2 + SHARED, s, u * 2, u + SHARED // 2)

        def loops(eng, tile):
            shared_pair(tile, 0)
            with eng.Fori(1, SHARED // 2) as u:
                shared_pair(tile, u)
            routed_pair(tile, 0)
            with eng.Fori(1, ROUTED // 2) as u:
                routed_pair(tile, u)

        def weights_done(eng, R, s):
            eng.wait_ge(s_wh, (R + s) * 2 + 4)
            eng.wait_ge(s_w1l, R + (s + 2))
            eng.wait_ge(s_w2l, R + (s + 2))
            eng.wait_ge(s_b2, R + (s + 2))

        @block.sync
        def _(sp):
            def load_w(slot, e):
                if e is None:
                    f, bf, pr, bp = weights_s
                    srcs = (f.rearrange("(c p) n -> p c n", p=P), pr.rearrange("(p c) n -> p c n", c=HC),
                            bf.rearrange("(p c) -> p c", c=HC), bp.rearrange("(a n) -> a n", a=1).broadcast_to([P, D]))
                    dsts = (w1[:, slot], w2[:, slot], b1[:, slot], b2[:, slot])
                else:
                    srcs = (Wfc[bass.ds(e, 1)].rearrange("e (c p) n -> p e c n", p=P),
                            Wproj[bass.ds(e, 1)].rearrange("e (p c) n -> p e c n", c=HC),
                            bfc[bass.ds(e, 1)].rearrange("e (p c) -> p e c", c=HC),
                            bproj[bass.ds(e, 1)].broadcast_to([P, D]))
                    dsts = (w1[:, slot:slot + 1], w2[:, slot:slot + 1], b1[:, slot:slot + 1], b2[:, slot])
                for d, s_ in zip(dsts, srcs):
                    sp.dma_start(d, s_).then_inc(s_wl[slot], 16)

            def expert_of(j):
                return sp.value_load(expert[0:1, bass.ds(j, 1)], min_val=0, max_val=E - 1)

            def load_x(T, parity, src=tokens_v):
                sp.dma_start(xt[:, parity:parity + 1], src[bass.ds(T, 1)].rearrange("t p r d -> p t r d")).then_inc(s_xl[parity], 16)

            load_w(1, None)
            load_x(0, 0)
            load_w(0, expert_of(0))
            sp.wait_ge(s_wh, 2)
            sp.wait_ge(s_w1l, 1)
            sp.wait_ge(s_w2l, 1)
            sp.wait_ge(s_b2, 1)
            load_w(1, expert_of(1))

            def tile(T, s, R, U):
                if R is not None:
                    e = expert_of(R + (s + 2))
                    weights_done(sp, R, s)
                    load_w(s, e)
                sp.wait_ge(s_xt, T + s)
                if R is not None:
                    load_x(R + (s + 1), 1 - s, routed_v)
                elif U is None and s == 1:
                    load_x(0, 1 - s, routed_v)
                else:
                    load_x(T + (s + 1), 1 - s)
                if R is None:
                    return
                sp.wait_ge(s_yv, T + (s + 1))
                sp.dma_start(ys_v[bass.ds(R + s, 1)].rearrange("t p r d -> p t r d"), y[:, s:s + 1]).then_inc(s_ys[s], 16)

            shared_pair(tile, 0)
            with sp.Fori(1, SHARED // 2 - 1) as u:
                shared_pair(tile, u)
            tile(SHARED - 2, 0, None, None)
            for i in range(4):
                sp.wait_ge(s_sc[i], 16 * 2 * TT // 4)
            tile(SHARED - 2, 1, None, None)
            with sp.Fori(0, ROUTED // 2) as u:
                routed_pair(tile, u)
            for s in range(2):
                sp.wait_ge(s_ys[s], 16 * ROUTED // 2)
            sp.wait_ge(s_wl[0], 64 * (1 + ROUTED // 2))
            sp.wait_ge(s_wl[1], 64 * (2 + ROUTED // 2))

        @block.gpsimd
        def _(pool):
            g = nc.gpsimd
            pool.memset(ident[:, :], 0.0).then_inc(s_id, 1)
            pool.wait_ge(s_id, 1)
            pool.affine_select(out=ident[:, :], in_=ident[:, :], compare_op=ALU.not_equal, fill=1.0,
                               base=0, pattern=[[-1, P]], channel_multiplier=1).then_inc(s_id, 1)

            def split(slot):
                g.tensor_tensor(w2_lo[:, slot], w2[:, slot], w2_hi[:, slot].bitcast(F32), ALU.subtract).then_inc(s_w2l, 1)

            pool.wait_ge(s_wh, 2)
            split(1)
            pool.wait_ge(s_wh, 4)
            split(0)
            moved_v = tokens.rearrange("(t p) d -> t p d", p=P)
            for tile in range(TT + 3):
                if tile < TT:
                    i = tile % 4
                    if tile >= 4:
                        pool.wait_ge(s_sc[i], 32 * (tile // 4))
                    pool.dma_start(moved[:, i, :], moved_v[tile]).then_inc(s_mv[i], 16)
                if tile >= 3:
                    back = tile - 3
                    i = back % 4
                    pool.wait_ge(s_mv[i], 16 * (back // 4 + 1))
                    for k in range(2):
                        pool.indirect_dma_start(out=routed[:, :], out_offset=bass.IndirectOffsetOnAxis(ap=slots[:, k, back:back + 1], axis=0),
                                                in_=moved[:, i, :], in_offset=None).then_inc(s_sc[i], 16)
            with pool.Fori(0, ROUTED // 2) as u:
                for s in range(2):
                    pool.wait_ge(s_wh, u * 4 + (2 * s + 6))
                    split(1 - s)

        @block.tensor
        def _(pe):
            mm = nc.tensor.matmul
            pe.wait_ge(s_id, 2)

            def transpose(T, parity):
                for r in range(2):
                    for c in range(C):
                        ins = nc.tensor.transpose(ps_t[:, c, r * P:(r + 1) * P], xt[:, parity, r, c * P:(c + 1) * P], ident[:, :])
                ins.then_inc(s_xt, 1)

            pe.wait_ge(s_xl[0], 16)
            transpose(0, 0)

            def tile(T, s, R, U):
                slot = 1 if R is None else s
                pe.wait_ge(s_xlo, T + (s + 1))
                if R is not None:
                    weights_done(pe, R, s)
                elif s == 0:
                    pe.wait_ge(s_wh, 2)
                    pe.wait_ge(s_w1l, 1)
                for p in range(4):
                    pe.wait_ge(s_g[p], T + s)
                    for i in range(2):
                        c = 2 * p + i
                        n = 0
                        for k in range(C):
                            for w, x_ in ((w1_hi, xT_hi), (w1_hi, xT_lo), (w1_lo, xT_hi)):
                                ins = mm(ps_h[:, p, i, :], w[:, slot, k, c, :], x_[:, s, k, :], start=n == 0, stop=n == 3 * C - 1)
                                n += 1
                    ins.then_inc(s_h, 1)
                pe.wait_ge(s_xl[1 - s], U * 16 + 16 * (s + 1))
                transpose(None, 1 - s)
                pe.wait_ge(s_yv, T + s)
                if R is None and s == 0:
                    pe.wait_ge(s_w2l, 1)
                for c in range(HC):
                    if c % 2 == 0:
                        pe.wait_ge(s_hl[c // 2], T + (s + 1))
                    for r in range(2):
                        for n, (h, w) in enumerate(((h_hi, w2_hi), (h_hi, w2_lo), (h_lo, w2_hi))):
                            ins = mm(ps_y[:, r, 0:D], h[:, s, c, r * P:(r + 1) * P], w[:, slot, c, :],
                                     start=c == 0 and n == 0, stop=c == HC - 1 and n == 2)
                ins.then_inc(s_y, 1)

            loops(pe, tile)

        @block.scalar
        def _(act):
            def split(slot):
                act.activation(w1_hi[:, slot], w1[:, slot].rearrange("p k (m c) -> p k c m", c=HC), ACT.Copy).then_inc(s_wh, 1)
                act.activation(w2_hi[:, slot], w2[:, slot], ACT.Copy)
                act.activation(b1_use[:, slot], b1[:, slot], ACT.Copy).then_inc(s_wh, 1)

            def upper_x(parity):
                act.activation(xT_hi[:, parity], ps_t[:, :, :], ACT.Copy).then_inc(s_xh, 1)

            act.wait_ge(s_wl[1], 64)
            split(1)
            act.wait_ge(s_xt, 1)
            upper_x(0)
            act.wait_ge(s_wl[0], 64)
            split(0)

            def tile(T, s, R, U):
                slot = 1 if R is None else s
                for p in range(4):
                    act.wait_ge(s_h, (T + s) * 4 + (p + 1))
                    act.wait_ge(s_hl[p], T + s)
                    if p == 0 and s == 0:
                        act.wait_ge(s_wh, 2 if R is None else R * 2 + 4)
                    if p == 0 and s == 1 and R is not None:
                        act.wait_ge(s_wh, R * 2 + 6)
                    for i in range(2):
                        c = 2 * p + i
                        ins = act.activation(ht[:, p, i, :], ps_h[:, p, i, :], ACT.Gelu_apprx_tanh, bias=b1_use[:, slot, c:c + 1])
                    ins.then_inc(s_g[p], 1)
                act.wait_ge(s_xt, T + (s + 2))
                upper_x(1 - s)
                if R is not None:
                    act.wait_ge(s_wl[1 - s], (U - SHARED // 2) * 64 + 128)
                    split(1 - s)

            loops(act, tile)

        @block.vector
        def _(dve):
            v = nc.vector

            def split(slot):
                v.tensor_tensor(w1_lo[:, slot], w1[:, slot].rearrange("p k (m c) -> p k c m", c=HC),
                                w1_hi[:, slot].bitcast(F32), ALU.subtract).then_inc(s_w1l, 1)
                v.tensor_copy(b2_use[:, slot], b2[:, slot]).then_inc(s_b2, 1)

            def lower_x(parity):
                v.tensor_tensor(xT_lo[:, parity], ps_t[:, :, :], xT_hi[:, parity].bitcast(F32), ALU.subtract).then_inc(s_xlo, 1)

            dve.wait_ge(s_wh, 1)
            split(1)
            dve.wait_ge(s_xh, 1)
            lower_x(0)
            dve.wait_ge(s_wh, 3)
            split(0)

            def tile(T, s, R, U):
                slot = 1 if R is None else s
                for p in range(4):
                    dve.wait_ge(s_g[p], T + (s + 1))
                    v.tensor_copy(h_hi[:, s, 2 * p:2 * p + 2, :], ht[:, p]).then_inc(s_hh[p], 1)
                    dve.wait_ge(s_hh[p], T + (s + 1))
                    v.tensor_tensor(h_lo[:, s, 2 * p:2 * p + 2, :], ht[:, p], h_hi[:, s, 2 * p:2 * p + 2, :].bitcast(F32),
                                    ALU.subtract).then_inc(s_hl[p], 1)
                dve.wait_ge(s_xh, T + (s + 2))
                lower_x(1 - s)
                if R is not None:
                    dve.wait_ge(s_wh, R * 2 + (2 * s + 5))
                    split(1 - s)
                    dve.wait_ge(s_b2, R + (s + 2))
                else:
                    dve.wait_ge(s_b2, 1)
                dve.wait_ge(s_y, T + (s + 1))
                if R is not None:
                    dve.wait_ge(s_ys[s], (U - SHARED // 2) * 16)
                v.tensor_tensor(y[:, s], ps_y[:, :, 0:D], b2_use[:, slot].unsqueeze(1).broadcast_to([P, 2, D]),
                                ALU.add).then_inc(s_yv, 1)
                if R is None:
                    dve.wait_ge(s_yv, T + (s + 1))
                    x2_tile = x2[:, bass.ds(T * 2 + 2 * s, 2), :]
                    v.tensor_tensor(x2_tile, x2_tile, y[:, s], ALU.add).then_inc(s_sum, 1)

            loops(dve, tile)


def combine(nc, x2, slots, gates, ys, out):
    NB, PAIRS = 4, TT // 2
    with ExitStack() as ctx:
        t = Tools(nc, ctx)
        y = t.sb("c_y", [P, NB, 2, 2, D])
        s_y = [t.sem("c_y%d" % i) for i in range(NB)]
        s_half, s_sum, s_out = t.sem("c_half"), t.sem("c_sum"), t.sem("c_out")
        block = ctx.enter_context(nc.Block())
        out_v = out.rearrange("b (g t p) d -> (b g) p t d", t=2, p=P)

        @block.gpsimd
        def _(pool):
            for k in range(PAIRS):
                i = k % NB
                if k >= NB:
                    pool.wait_ge(s_y[i], 64 * (k // NB))
                    pool.wait_ge(s_sum, 2 * (k - NB + 1))
                for tile in range(2):
                    for j in range(2):
                        pool.indirect_dma_start(out=y[:, i, tile, j, :], out_offset=None, in_=ys[:, :],
                                                in_offset=bass.IndirectOffsetOnAxis(ap=slots[:, j, 2 * k + tile:2 * k + tile + 1], axis=0)
                                                ).then_inc(s_y[i], 16)

        @block.vector
        def _(dve):
            for k in range(PAIRS):
                i = k % NB
                dve.wait_ge(s_y[i], 64 * (k // NB + 1))
                for j, done in enumerate((s_half, s_sum)):
                    if j:
                        dve.wait_ge(s_half, 2 * k + 2)
                    for tile in range(2):
                        n = 2 * k + tile
                        nc.vector.scalar_tensor_tensor(x2[:, n, :], y[:, i, tile, j, :], gates[:, n, j:j + 1], x2[:, n, :],
                                                       ALU.mult, ALU.add).then_inc(done, 1)

        @block.sync
        def _(sp):
            for k in range(PAIRS):
                sp.wait_ge(s_sum, 2 * k + 2)
                sp.dma_start(out_v[k], x2[:, 2 * k:2 * k + 2, :]).then_inc(s_out, 16)
            sp.wait_ge(s_out, 16 * PAIRS)


NAMES = ["x", "ctx_1024", "mask_BxS2_bf1"] + ["L0_xattn_" + n for n in (
    "ln_x_g", "ln_x_b", "ln_l_g", "ln_l_b", "qn_g", "kn_g", "Wq", "Wkv", "Wout", "bout")] + ["L0_ffn_" + n for n in (
    "Wfc_s", "bfc_s", "Wproj_s", "bproj_s", "Wr", "Wfc", "bfc", "Wproj", "bproj")]


def cross_attention_moe(nc, x, ctx_in, mask, ln_x_g, ln_x_b, ln_l_g, ln_l_b, qn_g, kn_g, Wq, Wkv, Wout, bout,
                        Wfc_s, bfc_s, Wproj_s, bproj_s, Wr, Wfc, bfc, Wproj, bproj, out):
    def dram(name, *shape):
        return nc.dram_tensor(name + "_dram", shape, F32, kind="Internal").ap()

    lnT = dram("lnT", B, P, 2, C, KEYS)
    wHead = dram("wHead", H, P, 2, C, 3 * DH)
    maskRow, maskCol = dram("maskRow", B, P), dram("maskCol", P, B)
    attT = dram("attT", HEADS, DH + 1, N)
    rden = dram("rden", HEADS, N)
    tokens = dram("tokens", TOKENS, D)
    routed = dram("routed", ROWS, D)
    ys = dram("ys", ROUTED * TS, D)
    prepare(nc, x, ctx_in, mask, ln_x_g, ln_x_b, ln_l_g, ln_l_b, Wq, Wkv, lnT, wHead, maskRow, maskCol)
    attention(nc, qn_g, kn_g, lnT, wHead, maskRow, maskCol, attT, routed)
    with ExitStack() as ctx:
        t = Tools(nc, ctx)
        x2 = t.sb("x2", [P, TT, D])
        slots = t.sb("slots", [P, 2, TT], U32)
        gates = t.sb("gates", [P, TT, 2])
        expert = t.sb("expert", [P, ROUTED + 2], I32)
        with nc.sbuf_tensor("l2", [P, TT, D], F32) as l2:
            project_out(nc, x, Wout, bout, attT, rden, tokens, x2, l2)
            route(nc, Wr, l2, slots, gates, expert)
        experts(nc, [Wfc_s, bfc_s, Wproj_s, bproj_s], [Wfc, bfc, Wproj, bproj], expert, slots, tokens, routed, x2, ys)
        combine(nc, x2, slots, gates, ys, out)


def kernel(**inputs):
    import numpy as np
    import concourse.bacc as bacc
    from concourse.bass_utils import run_bass_kernel_spmd

    nc = bacc.Bacc("TRN2", target_bir_lowering=False, num_devices=1)
    arrays, args = {}, []
    for name in NAMES:
        a = np.ascontiguousarray(inputs[name])
        if a.dtype == np.bool_:
            a = a.view(np.uint8)
        arrays["in_" + name] = a
        args.append(nc.dram_tensor("in_" + name, a.shape, mybir.dt.from_np(a.dtype), kind="ExternalInput").ap())
    args.append(nc.dram_tensor("out_dram", (B, N, D), F32, kind="ExternalOutput").ap())
    cross_attention_moe(nc, *args)
    r = run_bass_kernel_spmd(nc, [arrays], core_ids=[0])
    return r.results[0]["out_dram"]
```

```python
from contextlib import ExitStack

import concourse.bass as bass
from concourse import mybir

F32 = mybir.dt.float32
F32R = mybir.dt.float32r
I32 = mybir.dt.int32
U32 = mybir.dt.uint32
U8 = mybir.dt.uint8
ALU = mybir.AluOpType
ACT = mybir.ActivationFunctionType
AX = mybir.AxisListType

P = 128
B, N, D = 4, 1024, 256
CTX = 77
H, DH = 16, 64
C = D // P
NT = N // P
KT = NT + 1
KEYS = KT * P
QB = N // 512
HEADS = B * H
LN_EPS, RMS_EPS = 1e-5, 1e-8
NEG = -1e30
TOKENS = B * N
TT = TOKENS // P
GT = 2
E = 8
HID = 4 * D
HC = HID // P
TS = 2 * P
SHARED = TOKENS // TS
ROUTED = (2 * TOKENS + E * (TS - 1)) // TS
ROUTED += ROUTED % 2
ROWS = (ROUTED + 1) * TS


class Tools:

    def __init__(self, nc, ctx):
        self.nc, self.ctx = nc, ctx

    def sb(self, name, shape, dt=F32):
        return self.ctx.enter_context(self.nc.sbuf_tensor(name, shape, dt))

    def ps(self, name, shape):
        return self.ctx.enter_context(self.nc.psum_tensor(name, shape, F32))

    def sem(self, name):
        return self.ctx.enter_context(self.nc.semaphore(name))


def step(eng, sem, count, ins):
    ins.then_inc(sem, 1)
    count[0] += 1
    eng.wait_ge(sem, count[0])


def prepare(nc, x, ctx_in, mask, ln_x_g, ln_x_b, ln_l_g, ln_l_b, Wq, Wkv, lnT, wHead, maskRow, maskCol):
    with ExitStack() as ctx:
        t = Tools(nc, ctx)
        ident = t.sb("ident", [P, P])
        xin = t.sb("xin", [P, 2, NT, D])
        z = t.sb("z", [P, NT, D])
        cz = t.sb("cz", [CTX, B, D])
        stats = t.sb("stats", [P, NT, 6])
        mv = t.sb("mv", [P, NT, 2])
        var_eps = t.sb("var_eps", [P, NT])
        rstd = t.sb("rstd", [P, NT])
        half = t.sb("half", [P, NT])
        gain = t.sb("gain", [P, 4, C])
        full = t.sb("full", [P, 2, 512])
        out = t.sb("out", [P, 2, C, KEYS], F32R)
        w = t.sb("w", [P, C, 3 * H * DH])
        wh = t.sb("wh", [P, H, 2, C, 3 * DH], F32R)
        mk8 = t.sb("mk8", [P, B], U8)
        mkf = t.sb("mkf", [P, B])
        mr8 = t.sb("mr8", [B, P], U8)
        mrf = t.sb("mrf", [B, P], F32R)
        tp = t.ps("tp", [P, 2, 512])
        s_x = [t.sem("s_x0"), t.sem("s_x1")]
        s_c, s_w, s_g, s_m = t.sem("s_c"), t.sem("s_w"), t.sem("s_g"), t.sem("s_m")
        s_id, s_ve, s_rs, s_z, s_cz = t.sem("s_id"), t.sem("s_ve"), t.sem("s_rs"), t.sem("s_z"), t.sem("s_cz")
        s_tp, s_full, s_fullfree, s_split = t.sem("s_tp"), t.sem("s_full"), t.sem("s_fullfree"), t.sem("s_split")
        s_out, s_whi, s_wlo, s_mk, s_wout = t.sem("s_out"), t.sem("s_whi"), t.sem("s_wlo"), t.sem("s_mk"), t.sem("s_wout")
        s_v, s_lnT = t.sem("s_v"), t.sem("s_lnT")
        block = ctx.enter_context(nc.Block())
        x_v = x.rearrange("b (t p) d -> b p t d", p=P)
        GROUPS = [(c, g) for c in range(C) for g in range(2)]
        JOBS = len(GROUPS) + C

        @block.sync
        def _(sp):
            sp.dma_start(xin[:, 0], x_v[0]).then_inc(s_x[0], 16)
            sp.dma_start(w[:, :, 0:H * DH], Wq.rearrange("(c p) n -> p c n", p=P)).then_inc(s_w, 16)
            sp.dma_start(w[:, :, H * DH:], Wkv.rearrange("(c p) n -> p c n", p=P)).then_inc(s_w, 16)
            for b in range(B):
                if b + 1 < B:
                    if b >= 1:
                        sp.wait_ge(s_z, b)
                    sp.dma_start(xin[:, (b + 1) % 2], x_v[b + 1]).then_inc(s_x[(b + 1) % 2], 16)
                sp.wait_ge(s_split, 2 * JOBS * (b + 1))
                sp.dma_start(lnT[b], out[:, :, :, :].bitcast(F32)).then_inc(s_lnT, 16)
                if b == 0:
                    sp.wait_ge(s_mk, 2)
                    sp.dma_start(maskRow, mrf[:, :].bitcast(F32)).then_inc(s_out, 16)
                    sp.dma_start(maskCol, mkf[:, :]).then_inc(s_out, 16)
                    sp.wait_ge(s_whi, 6)
                    sp.wait_ge(s_wlo, 6)
                    sp.dma_start(wHead.rearrange("h p s c n -> p h s c n"), wh[:, :, :, :, :].bitcast(F32)).then_inc(s_out, 16)
            sp.wait_ge(s_lnT, 16 * B)
            sp.wait_ge(s_out, 48)

        @block.gpsimd
        def _(pool):
            pool.dma_start(cz[:, :, :], ctx_in.rearrange("b k d -> k b d")).then_inc(s_c, 16)
            pool.memset(ident[:, :], 0.0).then_inc(s_id, 1)
            pool.memset(half[:, :], -0.5).then_inc(s_id, 1)
            pool.memset(mk8[:, :], 0).then_inc(s_id, 1)
            pool.memset(mr8[:, :], 0).then_inc(s_id, 1)
            pool.wait_ge(s_id, 4)
            pool.dma_start(mk8[0:CTX, :], mask.rearrange("b k -> k b"), allow_slow_non_contiguous=True).then_inc(s_m, 16)
            pool.dma_start(mr8[:, 0:CTX], mask).then_inc(s_m, 16)
            for i, v in enumerate((ln_l_g, ln_l_b, ln_x_g, ln_x_b)):
                pool.dma_start(gain[:, i, :], v.rearrange("(c p) -> p c", p=P), allow_slow_non_contiguous=True).then_inc(s_g, 16)
            pool.affine_select(out=ident[:, :], in_=ident[:, :], compare_op=ALU.not_equal, fill=1.0,
                               base=0, pattern=[[-1, P]], channel_multiplier=1).then_inc(s_id, 1)
            pool.wait_ge(s_ve, 1)
            pool.tensor_tensor(rstd[0:CTX, 0:B], var_eps[0:CTX, 0:B], half[0:CTX, 0:B], ALU.pow).then_inc(s_rs, 1)
            for k in range(2 * B):
                pool.wait_ge(s_ve, k + 2)
                pool.tensor_tensor(rstd[:, :], var_eps[:, :], half[:, :], ALU.pow).then_inc(s_rs, 1)

        @block.vector
        def _(dve):
            n = [0]
            v = nc.vector

            def statistics(src, rows, tiles):
                for i in range(tiles):
                    v.bn_stats(stats[0:rows, i, :], src(i)).then_inc(s_v, 1)
                n[0] += tiles
                dve.wait_ge(s_v, n[0])
                for i in range(tiles):
                    v.bn_aggr(mv[0:rows, i, :], stats[0:rows, i, :]).then_inc(s_v, 1)
                n[0] += tiles
                dve.wait_ge(s_v, n[0])
                v.tensor_scalar(var_eps[0:rows, 0:tiles], mv[0:rows, 0:tiles, 1], LN_EPS, None, ALU.add).then_inc(s_ve, 1)

            def normalise(dst, src, rows, tiles, k, done):
                dve.wait_ge(s_rs, k)
                for i in range(tiles):
                    ins = v.tensor_scalar(dst(i), src(i), mv[0:rows, i, 0:1], rstd[0:rows, i:i + 1],
                                          ALU.subtract, ALU.mult)
                    if done is not None and i == tiles - 1:
                        ins.then_inc(done, 1)
                    else:
                        ins.then_inc(s_v, 1)
                        n[0] += 1
                dve.wait_ge(s_v, n[0])

            dve.wait_ge(s_c, 16)
            statistics(lambda b: cz[:, b, :], CTX, B)
            normalise(lambda b: cz[:, b, :], lambda b: cz[:, b, :], CTX, B, 1, s_cz)
            dve.wait_ge(s_m, 32)
            dve.wait_ge(s_id, 4)
            v.tensor_scalar(mkf[:, :], mk8[:, :], -NEG, NEG, ALU.mult, ALU.add).then_inc(s_mk, 1)
            v.tensor_scalar(mrf[:, :], mr8[:, :], -NEG, NEG, ALU.mult, ALU.add).then_inc(s_mk, 1)
            v.memset(out[:, :, :, N + CTX:KEYS].bitcast(F32), 0.0).then_inc(s_v, 1)
            n[0] += 1
            dve.wait_ge(s_g, 64)
            for b in range(B):
                dve.wait_ge(s_x[b % 2], 16 * (b // 2 + 1))
                src = lambda i: xin[:, b % 2, i, :]
                dst = lambda i: z[:, i, :]
                statistics(src, P, NT)
                normalise(src, src, P, NT, 2 * b + 2, None)
                statistics(src, P, NT)
                if b:
                    dve.wait_ge(s_tp, JOBS * b)
                normalise(dst, src, P, NT, 2 * b + 3, s_z)
                if b:
                    dve.wait_ge(s_lnT, 16 * b)
                for j in range(JOBS):
                    jj = JOBS * b + j
                    c = GROUPS[j][0] if j < 4 else j - 4
                    lo, n_ = (512 * GROUPS[j][1], 512) if j < 4 else (N, CTX)
                    dve.wait_ge(s_full, jj + 1)
                    f = full[:, jj % 2, 0:n_]
                    v.tensor_copy(out[:, 0, c, lo:lo + n_], f).then_inc(s_split, 1)
                    dve.wait_ge(s_split, 2 * jj + 1)
                    v.tensor_tensor(out[:, 1, c, lo:lo + n_], f, out[:, 0, c, lo:lo + n_].bitcast(F32),
                                    ALU.subtract).then_inc(s_split, 1)
                if b == 0:
                    for k in range(6):
                        c, part = k // 3, k % 3
                        hi, lo_ = (wh[:, :, s, c, part * DH:(part + 1) * DH] for s in range(2))
                        src_w = w[:, c, part * H * DH:(part + 1) * H * DH].rearrange("p (h d) -> p h d", d=DH)
                        dve.wait_ge(s_whi, k + 1)
                        v.tensor_tensor(lo_, src_w, hi.bitcast(F32), ALU.subtract).then_inc(s_wlo, 1)

        @block.tensor
        def _(pe):
            pe.wait_ge(s_id, 5)
            for b in range(B):
                pe.wait_ge(s_z, b + 1)
                if b == 0:
                    pe.wait_ge(s_cz, 1)
                for j in range(JOBS):
                    jj = JOBS * b + j
                    if jj >= 2:
                        pe.wait_ge(s_full, jj - 1)
                    if j < 4:
                        c, g = GROUPS[j]
                        for i in range(4):
                            ins = nc.tensor.transpose(tp[:, jj % 2, i * P:(i + 1) * P],
                                                      z[:, 4 * g + i, c * P:(c + 1) * P], ident[:, :])
                    else:
                        c = j - 4
                        ins = nc.tensor.transpose(tp[:, jj % 2, 0:CTX], cz[:, b, c * P:(c + 1) * P],
                                                  ident[0:CTX, 0:CTX])
                    ins.then_inc(s_tp, 1)

        @block.scalar
        def _(act):
            act.wait_ge(s_w, 32)
            for k in range(6):
                c, part = k // 3, k % 3
                act.activation(wh[:, :, 0, c, part * DH:(part + 1) * DH],
                               w[:, c, part * H * DH:(part + 1) * H * DH].rearrange("p (h d) -> p h d", d=DH),
                               ACT.Copy).then_inc(s_whi, 1)
            act.wait_ge(s_g, 64)
            for jj in range(B * JOBS):
                j = jj % JOBS
                c = GROUPS[j][0] if j < 4 else j - 4
                n_, kind = (512, 0) if j < 4 else (CTX, 2)
                act.wait_ge(s_tp, jj + 1)
                if jj >= 2:
                    act.wait_ge(s_split, 2 * (jj - 1))
                act.activation(full[:, jj % 2, 0:n_], tp[:, jj % 2, 0:n_], ACT.Identity,
                               scale=gain[:, kind, c:c + 1], bias=gain[:, kind + 1, c:c + 1]).then_inc(s_full, 1)


PLAN = [["P0", "P1"], ["P2", "P3"], ["K10", "P4"], ["K11", "KK"], ["Q10", "P5"], ["Q11", "P6"],
        ["M00", "P7"], ["M01", "P8"], ["M10", "C0"], ["M11", "M20"], ["M21", "M30"], ["M31", "K20"], ["M40", "M41"],
        ["M50", "K21", "M51"], ["M60", "Q20", "M61"], ["M70", "C1", "M71"], [], ["Q21"]]
RING = 3
LAG = 2
UNITS = QB * KT
assert len(PLAN) == UNITS
MISC = [j for u in PLAN for j in u]
BANKS = 3
REDUCED = [j for j in MISC if j[0] in "MC"]
COPIES = [j for j in MISC if j[0] not in "MC"]
assert len(MISC) % BANKS == 0 and KT % BANKS == 0


class Window:

    PER = {"misc": len(MISC), "copy": len(COPIES), "reduce": len(REDUCED), "unit": UNITS, "block": QB,
           "proj": 1, "split": 1, "one": 1}
    PRE = {"misc": len(MISC) + KT, "copy": len(COPIES) + KT, "reduce": len(REDUCED), "unit": 0, "block": 0,
           "proj": 2, "split": 1, "one": 0}

    def __init__(self, v, s):
        self.v, self.s = v, s
        self.n = s if v is None else None
        self.slot, self.other = s % 2, (s + 1) % 2
        self.attend = v is not None
        self.turn = v is not None or s == -1
        self.first = v is not None and isinstance(v, int) and v == 0 and s == 0

    def count(self, kind, k=0, times=1):
        per, pre = self.PER[kind], self.PRE[kind]
        if self.v is None:
            before = 0 if self.s == -2 else {"misc": KT, "copy": KT, "proj": 1}.get(kind, 0)
            return times * (before + k)
        return self.v * (2 * per * times) + times * (pre + self.s * per + k)

    def here(self):
        return MISC if self.turn else [j for j in MISC if j[0] == "P"]

    def taken(self, name):
        kind = "reduce" if name in REDUCED else "copy"
        mine = [j for j in self.here() if (j in REDUCED) == (name in REDUCED)]
        return kind, self.count(kind, mine.index(name) + 1)

    def copied(self, name):
        return self.taken(name)[1]

    def freed(self, m):
        if m >= BANKS:
            return self.taken(self.here()[m - BANKS])
        if self.n == -2:
            return None
        before = MISC if self.n != -1 else [j for j in MISC if j[0] == "P"]
        name, after = before[m - BANKS], before[len(before) + m - BANKS + 1:]
        return ("reduce" if name in REDUCED else "copy",
                self.count("reduce" if name in REDUCED else "copy",
                           -sum((j in REDUCED) == (name in REDUCED) for j in after)))

    def jobs(self, u):
        here = self.here()
        return [(j, here.index(j)) for j in PLAN[u] if j in here]


def windows(eng, body, last=None):
    body(Window(None, -2))
    body(Window(None, -1))
    for s in range(2):
        body(Window(0, s))
    with eng.Fori(1, HEADS // 2) as v:
        for s in range(2):
            body(Window(v, s))
    if last is not None:
        last(Window(HEADS // 2, 0))


def attention(nc, qn_g, kn_g, lnT, wHead, maskRow, maskCol, attT, routed):
    with ExitStack() as ctx:
        t = Tools(nc, ctx)
        ident = t.sb("a_ident", [P, P])
        lnT_sb = t.sb("lnT_sb", [P, 2, C, KEYS], F32R)
        w_sb = t.sb("w_sb", [P, 2, 2, C, 3 * DH], F32R)
        raw = t.sb("raw", [P, 2, KT, 3 * DH])
        sq = t.sb("sq", [P, KT, 2 * DH])
        ss = t.sb("ss", [P, 2 * KT])
        rs = t.sb("rs", [P, 2 * KT])
        minus_half = t.sb("minus_half", [P, 2 * KT])
        nrm = t.sb("nrm", [P, KT, 2, DH])
        gq = t.sb("gq", [P, DH])
        gk = t.sb("gk", [P, DH])
        gqk = t.sb("gqk", [P, DH])
        k_st = t.sb("k_st", [P, 2, KT, 2 * DH + 2], F32R)
        q_st = t.sb("q_st", [P, 2, NT, 3 * DH + 2], F32R)
        kT1 = t.sb("kT1", [P, 2, KEYS], F32R)
        kT2 = t.sb("kT2", [P, 2, KEYS], F32R)
        qT1 = t.sb("qT1", [P, 2, N], F32R)
        qT2 = t.sb("qT2", [P, 2, N], F32R)
        vA = t.sb("vA", [P, 2, KT, 2 * DH], F32R)
        vC = t.sb("vC", [P, 2, KT, 2 * DH], F32R)
        one_row = t.sb("one_row", [P, P], F32R)
        mrow = t.sb("mrow", [P, 2, P], F32R)
        mcol = t.sb("mcol", [P, 2])
        pr = t.sb("pr", [P, RING, 512])
        pr_hi = t.sb("pr_hi", [P, RING, 512], F32R)
        pr_lo = t.sb("pr_lo", [P, RING, 512], F32R)
        maxima = t.sb("maxima", [P, NT, 3])
        o_sb = t.sb("o_sb", [DH + 1, 2, 512])
        zero = t.sb("zero", [P, D])
        ps_s = t.ps("ps_s", [P, RING, 512])
        ps_o = t.ps("ps_o", [P, QB, 512])
        ps_m = t.ps("ps_m", [P, BANKS, 512])
        s_id, s_g, s_gd, s_const = t.sem("a_id"), t.sem("a_g"), t.sem("a_gd"), t.sem("a_const")
        s_ln, s_lnready = t.sem("a_ln"), t.sem("a_lnready")
        s_w = [t.sem("a_w0"), t.sem("a_w1")]
        s_mask = [t.sem("a_mask0"), t.sem("a_mask1")]
        s_misc, s_copy, s_reduce, s_negmax = t.sem("a_misc"), t.sem("a_copy"), t.sem("a_reduce"), t.sem("a_negmax")
        s_sq, s_ss, s_nrm, s_hi, s_lo = t.sem("a_sq"), t.sem("a_ss"), t.sem("a_nrm"), t.sem("a_hi"), t.sem("a_lo")
        s_vhi, s_vlo, s_pool = t.sem("a_vhi"), t.sem("a_vlo"), t.sem("a_pool")
        s_scores, s_exp, s_prlo, s_pv = t.sem("a_scores"), t.sem("a_exp"), t.sem("a_prlo"), t.sem("a_pv")
        s_o = [t.sem("a_o0"), t.sem("a_o1")]
        s_store = [t.sem("a_store0"), t.sem("a_store1")]
        s_zero, s_clear = t.sem("a_zero"), t.sem("a_clear")
        block = ctx.enter_context(nc.Block())

        @block.sync
        def _(sp):
            def load_ln(b):
                sp.dma_start(lnT_sb[:, :, :, :].bitcast(F32).unsqueeze(1),
                             lnT[bass.ds(b, 1)].rearrange("b p s c k -> p b s c k")).then_inc(s_ln, 16)

            def load_w(head, slot):
                sp.dma_start(w_sb[:, slot:slot + 1].bitcast(F32),
                             wHead[bass.ds(head, 1)].rearrange("h p s c n -> p h s c n")).then_inc(s_w[slot], 16)

            def load_mask(b, slot):
                sp.dma_start(mrow[0:1, slot, :].bitcast(F32), maskRow[bass.ds(b, 1), :]).then_inc(s_mask[slot], 16)
                sp.dma_start(mcol[:, slot:slot + 1], maskCol[:, bass.ds(b, 1)], allow_slow_non_contiguous=True).then_inc(s_mask[slot], 16)

            load_ln(0)
            load_w(0, 0)
            load_w(1, 1)
            sp.wait_ge(s_ln, 16)
            sp.sem_inc(s_lnready, 1)
            sp.wait_ge(s_copy, KT)
            load_w(2, 0)
            sp.wait_ge(s_const, 3)
            load_mask(0, 0)
            sp.wait_ge(s_copy, Window(None, -1).copied("P8"))
            load_w(3, 1)

            def store(head, q):
                sp.wait_ge(s_o[q], head + 1)
                sp.dma_start(attT[bass.ds(head, 1), :, q * 512:(q + 1) * 512].rearrange("h d n -> d h n"),
                             o_sb[:, q:q + 1, :]).then_inc(s_store[q], 16)

            def pair(v, b=None):
                if b is not None:
                    sp.wait_ge(s_ln, b * 16 + 16)
                sp.sem_inc(s_lnready, 1)
                for s in range(2):
                    w = Window(v, s)
                    mb, head = (v + s) // 8 % B, (v * 2 + s + 4) % H
                    sp.wait_ge(s_exp, w.count("unit"))
                    load_mask(mb, w.other)
                    if not w.first:
                        store(v * 2 + s - 1, 1)
                    sp.wait_ge(s_copy, w.copied("P8"))
                    load_w(head, w.slot)
                    store(v * 2 + s, 0)

            pair(0)
            with sp.Fori(1, 7) as v:
                pair(v)
            with sp.Fori(1, B) as b:
                load_ln(b)
                with sp.Fori(0, 8) as k:
                    pair(b * 8 + k - 1, b)
            pair(HEADS // 2 - 1)
            store(HEADS - 1, 1)
            sp.wait_ge(s_clear, 16)
            for q in range(QB):
                sp.wait_ge(s_store[q], 16 * HEADS)
            for s in range(2):
                sp.wait_ge(s_w[s], 16 * (HEADS // 2 + 2))
                sp.wait_ge(s_mask[s], 32 * (HEADS // 2 + (s == 0)))

        @block.gpsimd
        def _(pool):
            g = nc.gpsimd
            pool.memset(ident[:, :], 0.0).then_inc(s_id, 1)
            pool.wait_ge(s_id, 1)
            pool.affine_select(out=ident[:, :], in_=ident[:, :], compare_op=ALU.not_equal, fill=1.0,
                               base=0, pattern=[[-1, P]], channel_multiplier=1).then_inc(s_id, 1)
            pool.memset(minus_half[:, :], -0.5).then_inc(s_pool, 1)
            pool.dma_start(gq[:, :], qn_g.rearrange("(a d) -> a d", a=1).broadcast_to([P, DH])).then_inc(s_g, 16)
            pool.dma_start(gk[:, :], kn_g.rearrange("(a d) -> a d", a=1).broadcast_to([P, DH])).then_inc(s_g, 16)
            pool.wait_ge(s_const, 4)

            def window(w):
                if w.turn:
                    pool.wait_ge(s_hi, w.count("split", 1, 2))
                    g.tensor_tensor(k_st[:, w.other, :, 0:DH], nrm[:, :, 1, :],
                                    k_st[:, w.other, :, DH:2 * DH].bitcast(F32), ALU.subtract).then_inc(s_lo, 1)
                    g.tensor_tensor(q_st[:, w.other, :, 2 * DH:3 * DH], nrm[:, 0:NT, 0, :],
                                    q_st[:, w.other, :, 0:DH].bitcast(F32), ALU.subtract).then_inc(s_lo, 1)
                    pool.wait_ge(s_vhi, w.count("split", 1))
                    g.tensor_tensor(vC[:, w.other, :, 0:DH], raw[:, w.other, :, 2 * DH:3 * DH],
                                    vA[:, w.other, :, 0:DH].bitcast(F32), ALU.subtract).then_inc(s_vlo, 1)
                pool.wait_ge(s_copy, w.copied("P8"))
                qk = raw[:, w.slot, :, 0:2 * DH]
                g.tensor_tensor(sq[:, :, :], qk, qk, ALU.mult).then_inc(s_sq, 1)
                pool.wait_ge(s_ss, w.count("proj", 1, 2))
                g.tensor_tensor(rs[:, :], ss[:, :], minus_half[:, :], ALU.pow).then_inc(s_pool, 1)
                pool.wait_ge(s_pool, w.count("proj", 0, 2) + 2)
                g.tensor_tensor(nrm[:, :, :, :], qk.rearrange("p t (j d) -> p t j d", d=DH),
                                rs[:, :].rearrange("p (t j) -> p t j", j=2).unsqueeze(3).broadcast_to([P, KT, 2, DH]),
                                ALU.mult).then_inc(s_pool, 1)
                pool.wait_ge(s_pool, w.count("proj", 0, 2) + 3)
                g.tensor_tensor(nrm[:, 0:NT, 0, :], nrm[:, 0:NT, 0, :],
                                gqk[:, :].unsqueeze(1).broadcast_to([P, NT, DH]), ALU.mult).then_inc(s_nrm, 1)

            windows(pool, window)

        @block.vector
        def _(dve):
            v = nc.vector
            v.memset(zero[:, :], 0.0).then_inc(s_zero, 1)
            v.memset(k_st[:, :, :, 2 * DH:2 * DH + 2].bitcast(F32), 1.0).then_inc(s_const, 1)
            v.memset(one_row[:, :].bitcast(F32), 0.0).then_inc(s_const, 1)
            v.memset(mrow[:, :, :].bitcast(F32), 0.0).then_inc(s_const, 1)
            dve.wait_ge(s_g, 32)
            dve.wait_ge(s_const, 3)
            v.scalar_tensor_tensor(gqk[:, :], gq[:, :], DH ** 0.5, gk[:, :], ALU.mult, ALU.mult).then_inc(s_const, 1)
            v.memset(one_row[0:1, :].bitcast(F32), 1.0).then_inc(s_const, 1)
            v.memset(vA[:, :, :, DH:2 * DH].bitcast(F32), 1.0).then_inc(s_const, 1)
            v.memset(vC[:, :, :, DH:2 * DH].bitcast(F32), 0.0).then_inc(s_const, 1)

            def negmax(w, half):
                a = slice(4 * half, 4 * half + 4)
                dve.wait_ge(s_reduce, w.taken("M71" if half else "M31")[1])
                v.tensor_reduce(q_st[:, w.other, a, 3 * DH], maxima[:, a, :], AX.X, ALU.min).then_inc(s_negmax, 1)

            def output(w, q, before=0):
                dve.wait_ge(s_pv, w.count("unit", KT * (q + 1) - before * UNITS))
                dve.wait_ge(s_store[q], w.count("one", -before, 16))
                v.tensor_copy(o_sb[:, q, :], ps_o[0:DH + 1, q, :]).then_inc(s_o[q], 1)

            def window(w):
                for u in range(UNITS):
                    for name, m in w.jobs(u):
                        if name not in REDUCED:
                            continue
                        dve.wait_ge(s_misc, w.count("misc", m + 1))
                        j, bank = int(name[1]), ps_m[:, m % BANKS, :]
                        if name[0] == "M":
                            g = int(name[2])
                            v.tensor_reduce(maxima[:, j, g:g + 1], bank, AX.X, ALU.max, negate=True).then_inc(s_reduce, 1)
                        else:
                            v.tensor_reduce(maxima[:, 4 * j:4 * j + 4, 2], bank.rearrange("p (t k) -> p t k", k=P),
                                            AX.X, ALU.max, negate=True).then_inc(s_reduce, 1)
                        if name in ("M31", "M71"):
                            negmax(w, name == "M71")
                    if w.attend:
                        dve.wait_ge(s_exp, w.count("unit", u + 1))
                        v.tensor_tensor(pr_lo[:, u % RING, :], pr[:, u % RING, :], pr_hi[:, u % RING, :].bitcast(F32),
                                        ALU.subtract).then_inc(s_prlo, 1)
                    if u == 0 and w.turn:
                        dve.wait_ge(s_nrm, w.count("proj"))
                        v.tensor_copy(k_st[:, w.other, :, DH:2 * DH], nrm[:, :, 1, :]).then_inc(s_hi, 1)
                        v.tensor_copy(q_st[:, w.other, :, 0:2 * DH].rearrange("p t (j d) -> p t j d", d=DH),
                                      nrm[:, 0:NT, 0, :].unsqueeze(2).broadcast_to([P, NT, 2, DH])).then_inc(s_hi, 1)
                    if u == 4 and w.turn:
                        if w.attend:
                            dve.wait_ge(s_pv, w.count("unit"))
                        dve.wait_ge(s_copy, w.count("copy"))
                        v.tensor_copy(vA[:, w.other, :, 0:DH], raw[:, w.other, :, 2 * DH:3 * DH]).then_inc(s_vhi, 1)
                    if u == 11:
                        dve.wait_ge(s_sq, w.count("proj", 1))
                        v.tensor_reduce(ss[:, :], sq[:, :, :].rearrange("p t (j d) -> p (t j) d", d=DH),
                                        AX.X, ALU.add).then_inc(s_ss, 1)
                        dve.wait_ge(s_ss, w.count("proj", 0, 2) + 1)
                        v.tensor_scalar(ss[:, :], ss[:, :], DH * RMS_EPS ** 2, None, ALU.max).then_inc(s_ss, 1)
                    if u == LAG and w.attend and not w.first:
                        output(w, 1, 1)
                    if u == KT + LAG and w.attend:
                        output(w, 0)

            windows(dve, window, lambda w: output(w, 1, 1))

        @block.scalar
        def _(act):
            def window(w):
                for u in range(UNITS):
                    if w.attend:
                        q, k = u // KT, u % KT
                        act.wait_ge(s_scores, w.count("unit", u + 1))
                        if k == KT - 1:
                            if q == 0:
                                act.wait_ge(s_mask[w.slot], w.v * 32 + 32)
                            bias = mcol[:, w.slot:w.slot + 1]
                        else:
                            bias = 0.0
                        act.activation(pr[:, u % RING, :], ps_s[:, u % RING, :], ACT.Exp, bias=bias)
                        act.activation(pr_hi[:, u % RING, :], ps_s[:, u % RING, :], ACT.Exp, bias=bias).then_inc(s_exp, 1)
                    for name, m in w.jobs(u):
                        if name in REDUCED:
                            continue
                        act.wait_ge(s_misc, w.count("misc", m + 1))
                        src = ps_m[:, m % BANKS, :]
                        if name[0] == "P":
                            if name == "P0" and w.attend:
                                act.wait_ge(s_vlo, w.count("split"))
                                act.wait_ge(s_nrm, w.count("proj"))
                            ins = act.activation(raw[:, w.slot, int(name[1]), :], src[:, 0:3 * DH], ACT.Copy)
                        elif name == "KK":
                            act.activation(kT1[:, w.other, N:KEYS], src[:, 0:P], ACT.Copy)
                            ins = act.activation(kT2[0:DH + 1, w.other, N:KEYS], src[0:DH + 1, P:2 * P], ACT.Copy)
                        else:
                            rows, dst = {"K1": (P, kT1), "K2": (DH + 1, kT2), "Q1": (P, qT1), "Q2": (DH + 1, qT2)}[name[:2]]
                            g = int(name[2])
                            ins = act.activation(dst[0:rows, w.other, 512 * g:512 * g + 512], src[0:rows, :], ACT.Copy)
                        ins.then_inc(s_copy, 1)

            act.wait_ge(s_zero, 1)
            act.dma_start(routed.rearrange("(t p) d -> p t d", p=P),
                          zero[:, :].unsqueeze(1).broadcast_to([P, ROWS // P, D])).then_inc(s_clear, 16)
            windows(act, window)

        @block.tensor
        def _(pe):
            mm = nc.tensor.matmul
            pe.wait_ge(s_id, 2)
            pe.wait_ge(s_const, 7)

            def project(w, tile, out):
                for k, (a, b, c) in enumerate((a, b, c) for a, b in ((0, 0), (0, 1), (1, 0)) for c in range(C)):
                    ins = mm(out[:, 0:3 * DH], lnT_sb[:, a, c, tile * P:(tile + 1) * P], w_sb[:, w.slot, b, c, :],
                             start=k == 0, stop=k == 3 * C - 1)
                return ins

            def values(w, u):
                slot = w.slot if u >= 0 else w.other
                q, k, r = u % UNITS // KT, u % KT, u % RING
                if k == 0:
                    pe.wait_ge(s_o[q], w.count("one"))
                pe.wait_ge(s_prlo, w.count("unit", u + 1))
                last = k == KT - 1
                mm(ps_o[:, q, :], vA[:, slot, k, :], pr_hi[:, r, :], start=k == 0, stop=False)
                mm(ps_o[:, q, :], vC[:, slot, k, :], pr_hi[:, r, :], start=False, stop=False)
                mm(ps_o[:, q, :], vA[:, slot, k, :], pr_lo[:, r, :], start=False, stop=last).then_inc(s_pv, 1)

            def transposes(w, out, src, tiles, lo, n_):
                for i, tile in enumerate(tiles):
                    ins = nc.tensor.transpose(out[0:n_, i * P:(i + 1) * P],
                                              src[:, w.other, tile, lo:lo + n_].bitcast(F32), ident[:, :])
                return ins

            def job(w, name, m):
                out = ps_m[:, m % BANKS, :]
                if w.freed(m):
                    kind, value = w.freed(m)
                    pe.wait_ge({"copy": s_copy, "reduce": s_reduce}[kind], value)
                if name[0] == "P":
                    if name == "P0":
                        if w.n is None:
                            pe.wait_ge(s_lnready, w.v + 2)
                            pe.wait_ge(s_w[w.slot], w.v * 16 + 32)
                        else:
                            pe.wait_ge(s_lnready, 1)
                            pe.wait_ge(s_w[w.slot], 16)
                    ins = project(w, int(name[1]), out)
                elif name[0] == "M":
                    j, g = int(name[1]), int(name[2])
                    if name in ("M00", "M40"):
                        pe.wait_ge(s_copy, w.copied("Q10" if j == 0 else "Q11"))
                    ins = mm(out, qT1[:, w.other, j * P:(j + 1) * P], kT1[:, w.other, 512 * g:512 * g + 512],
                             start=True, stop=True)
                elif name[0] == "C":
                    j = int(name[1])
                    if j == 0:
                        if w.n is None:
                            pe.wait_ge(s_mask[w.other], w.v * 32 + (32 if w.s == 0 else 64))
                        else:
                            pe.wait_ge(s_mask[w.other], 32)
                    pe.wait_ge(s_copy, w.copied("Q1%d" % j))
                    for i in range(4):
                        mm(out[:, i * P:(i + 1) * P], qT1[:, w.other, (4 * j + i) * P:(4 * j + i + 1) * P],
                           kT1[:, w.other, N:KEYS], start=True, stop=False)
                        ins = mm(out[:, i * P:(i + 1) * P], one_row[:, :], mrow[:, w.other, :], start=False, stop=True)
                elif name == "KK":
                    transposes(w, out, k_st, [KT - 1], 0, 2 * DH)
                    ins = transposes(w, out[:, P:2 * P], k_st, [KT - 1], DH, DH + 1)
                else:
                    g = int(name[2])
                    tiles = range(4 * g, 4 * g + 4)
                    if name in ("K10", "Q10"):
                        pe.wait_ge(s_lo, w.count("split", 1, 2) - (name == "K10"))
                    if name[:2] == "Q2":
                        pe.wait_ge(s_negmax, w.count("split", 0, 2) + g + 1)
                    src, lo, n_ = {"K1": (k_st, 0, 2 * DH), "K2": (k_st, DH, DH + 1),
                                   "Q1": (q_st, 0, 2 * DH), "Q2": (q_st, 2 * DH, DH + 1)}[name[:2]]
                    ins = transposes(w, out, src, tiles, lo, n_)
                ins.then_inc(s_misc, 1)

            def window(w):
                for u in range(UNITS):
                    if w.attend:
                        q, k = u // KT, u % KT
                        if u == 0:
                            pe.wait_ge(s_copy, w.count("copy"))
                            pe.wait_ge(s_vlo, w.count("split"))
                        mm(ps_s[:, u % RING, :], kT1[:, w.slot, k * P:(k + 1) * P],
                           qT1[:, w.slot, q * 512:(q + 1) * 512], start=True, stop=False)
                        mm(ps_s[:, u % RING, :], kT2[0:DH + 1, w.slot, k * P:(k + 1) * P],
                           qT2[0:DH + 1, w.slot, q * 512:(q + 1) * 512], start=False, stop=True).then_inc(s_scores, 1)
                    here = w.jobs(u)
                    for name, m in here[:1]:
                        job(w, name, m)
                    if w.attend and (u >= LAG or not w.first):
                        values(w, u - LAG)
                    for name, m in here[1:]:
                        job(w, name, m)

            def last(w):
                for u in range(LAG):
                    values(w, u - LAG)

            windows(pe, window, last)


def project_out(nc, x, Wout, bout, attT, rden, tokens, x2, l2):
    HP, G = H // 2, 4
    W = GT * P
    with ExitStack() as ctx:
        t = Tools(nc, ctx)
        dn = t.sb("dn", [HEADS, N])
        wo = t.sb("wo", [P, HP, D])
        wo_hi = t.sb("wo_hi", [P, HP, D], F32R)
        wo_lo = t.sb("wo_lo", [P, HP, D], F32R)
        bo = t.sb("bo", [P, D])
        a = t.sb("a", [P, 2, HP, W])
        rb = t.sb("rb", [P, 2, HP, W])
        a_hi = t.sb("a_hi", [P, 2, HP, W], F32R)
        a_lo = t.sb("a_lo", [P, 2, HP, W], F32R)
        xg = t.sb("xg", [P, G, GT, D])
        stats = t.sb("o_stats", [P, GT, 6])
        mv = t.sb("o_mv", [P, GT, 2])
        var_eps = t.sb("o_var", [P, GT])
        rstd = t.sb("o_rstd", [P, GT])
        half = t.sb("o_half", [P, GT])
        marker = t.sb("marker", [P, 1])
        ps_y = t.ps("ps_y", [P, G * GT, 512])
        s_dn, s_rd, s_w, s_whi, s_wlo, s_bo, s_half = (t.sem("o_" + n) for n in ("dn", "rd", "w", "whi", "wlo", "bo", "half"))
        s_a, s_x, s_prod, s_xb, s_y, s_l2, s_lov, s_lop = ([t.sem("o_%s_%d" % (n, q)) for q in range(G)] for n in
                                                            ("a", "x", "prod", "xb", "y", "l2", "lov", "lop"))
        s_hi, s_x2, s_v, s_ve, s_rs, s_st = (t.sem("o_" + n) for n in ("hi", "x2", "v", "ve", "rs", "st"))
        block = ctx.enter_context(nc.Block())
        att_v = attT.rearrange("(b k r) d n -> b r d k n", b=B, r=2)
        rden_v = rden.rearrange("(b k r) n -> b r k n", b=B, r=2)
        x_v = x.rearrange("b (g t p) d -> (b g) p t d", t=GT, p=P)
        tokens_v = tokens.rearrange("(g t p) d -> g p t d", t=GT, p=P)
        HH = HP // 2

        def before(q, b):
            return (q - 2, b + 1) if q >= 2 else (q + 2, b)

        def batches(eng, batch):
            batch(0)
            with eng.Fori(1, B) as b:
                batch(b)

        def ahead(eng, batch):
            batch(0)
            with eng.Fori(1, B - 1) as b:
                batch(b)
            batch(B - 1, last=True)

        @block.sync
        def _(sp):
            sp.dma_start(dn[:, :], attT[:, DH, :]).then_inc(s_dn, 16)
            sp.dma_start(wo[:, :, :], Wout.rearrange("(k p) n -> p k n", p=P)).then_inc(s_w, 16)
            sp.wait_ge(s_rd, 1)
            sp.dma_start(rden, dn[:, :]).then_inc(s_dn, 16)
            sp.wait_ge(s_dn, 32)
            def batch(b):
                for q in range(G):
                    g, done = before(q, b)
                    sp.wait_ge(s_lov[g], done)
                    sp.wait_ge(s_lop[g], done)
                    cols = slice(W * q, W * q + W)
                    for r in range(2):
                        p = slice(DH * r, DH * r + DH)
                        sp.dma_start(a[p, q % 2:q % 2 + 1], att_v[bass.ds(b, 1), r, 0:DH, :, cols]
                                     .rearrange("b d k n -> d b k n")).then_inc(s_a[q], 16)
                        sp.dma_start(rb[p, q % 2:q % 2 + 1], rden_v[bass.ds(b, 1), r, :, cols]
                                     .unsqueeze(0).broadcast_to([DH, 1, HP, W])).then_inc(s_a[q], 16)
                    sp.wait_ge(s_l2[q], b)
                    sp.dma_start(xg[:, q:q + 1], x_v[bass.ds(b * G + q, 1)]
                                 .rearrange("g p t d -> p g t d")).then_inc(s_x[q], 16)

            batches(sp, batch)

        @block.gpsimd
        def _(pool):
            pool.dma_start(bo[:, :], bout.rearrange("(a d) -> a d", a=1).broadcast_to([P, D])).then_inc(s_bo, 16)
            pool.memset(half[:, :], -0.5).then_inc(s_half, 1)
            pool.wait_ge(s_half, 1)
            pool.wait_ge(s_bo, 16)

            def lower(b, q):
                pool.wait_ge(s_hi, b * (2 * G) + 2 * q + 2)
                nc.gpsimd.tensor_tensor(a_lo[:, q % 2, HH:, :], a[:, q % 2, HH:, :],
                                        a_hi[:, q % 2, HH:, :].bitcast(F32), ALU.subtract).then_inc(s_lop[q], 1)

            lower(0, 0)

            def batch(b, last=False):
                for q in range(G):
                    pool.wait_ge(s_x[q], b * 16 + 16)
                    nc.gpsimd.tensor_tensor(xg[:, q], xg[:, q], bo[:, :].unsqueeze(1).broadcast_to([P, GT, D]),
                                            ALU.add).then_inc(s_xb[q], 1)
                    if q + 1 < G:
                        lower(b, q + 1)
                    elif not last:
                        lower(b + 1, 0)
                    pool.wait_ge(s_ve, b * G + q + 1)
                    nc.gpsimd.tensor_tensor(rstd[:, :], var_eps[:, :], half[:, :], ALU.pow).then_inc(s_rs, 1)
                    pool.wait_ge(s_l2[q], b + 1)
                    pool.dma_start(tokens_v[bass.ds(b * G + q, 1)].rearrange("g p t d -> p g t d"),
                                   l2[:, bass.ds((b * G + q) * GT, GT), :].unsqueeze(1)).then_inc(s_st, 16)

            ahead(pool, batch)
            pool.wait_ge(s_st, 16 * G * B)

        @block.scalar
        def _(act):
            act.wait_ge(s_w, 16)
            act.activation(wo_hi[:, :, :], wo[:, :, :], ACT.Copy).then_inc(s_whi, 1)
            def batch(b):
                for q in range(G):
                    g, done = before(q, b)
                    act.wait_ge(s_y[g], done * GT)
                    for k in range(2):
                        act.wait_ge(s_prod[q], b * 2 + k + 1)
                        h = slice(HH * k, HH * k + HH)
                        act.activation(a_hi[:, q % 2, h, :], a[:, q % 2, h, :], ACT.Copy).then_inc(s_hi, 1)

            batches(act, batch)

        @block.vector
        def _(dve):
            v = nc.vector
            dve.wait_ge(s_dn, 16)
            v.reciprocal(dn[:, :], dn[:, :]).then_inc(s_rd, 1)
            dve.wait_ge(s_whi, 1)
            v.tensor_tensor(wo_lo[:, :, :], wo[:, :, :], wo_hi[:, :, :].bitcast(F32), ALU.subtract).then_inc(s_wlo, 1)

            def product(b, q):
                dve.wait_ge(s_a[q], b * 64 + 64)
                for k in range(2):
                    h = slice(HH * k, HH * k + HH)
                    v.tensor_tensor(a[:, q % 2, h, :], a[:, q % 2, h, :], rb[:, q % 2, h, :], ALU.mult).then_inc(s_prod[q], 1)
                dve.wait_ge(s_hi, b * (2 * G) + 2 * q + 1)
                v.tensor_tensor(a_lo[:, q % 2, 0:HH, :], a[:, q % 2, 0:HH, :], a_hi[:, q % 2, 0:HH, :].bitcast(F32),
                                ALU.subtract).then_inc(s_lov[q], 1)

            product(0, 0)

            def batch(b, last=False):
                for q in range(G):
                    if q + 1 < G:
                        product(b, q + 1)
                    elif not last:
                        product(b + 1, 0)
                    dve.wait_ge(s_xb[q], b + 1)
                    group = b * G + q
                    for i in range(GT):
                        dve.wait_ge(s_y[q], b * GT + i + 1)
                        v.tensor_tensor(x2[:, bass.ds(group * GT + i, 1), :], ps_y[:, q * GT + i, 0:D].unsqueeze(1),
                                        xg[:, q, i:i + 1, :], ALU.add).then_inc(s_x2, 1)
                    dve.wait_ge(s_x2, group * (2 * GT) + GT)
                    v.memset(marker[:, :], 0.0)
                    for i in range(GT):
                        v.bn_stats(stats[:, i, :], x2[:, bass.ds(group * GT + i, 1), :].rearrange("p a d -> p (a d)")).then_inc(s_x2, 1)
                    dve.wait_ge(s_x2, group * (2 * GT) + 2 * GT)
                    v.memset(marker[:, :], 0.0)
                    for i in range(GT):
                        ins = v.bn_aggr(mv[:, i, :], stats[:, i, :])
                    ins.then_inc(s_v, 1)
                    dve.wait_ge(s_v, group + 1)
                    v.tensor_scalar(var_eps[:, :], mv[:, :, 1], LN_EPS, None, ALU.add).then_inc(s_ve, 1)
                    dve.wait_ge(s_rs, group + 1)
                    for i in range(GT):
                        tile = bass.ds(group * GT + i, 1)
                        ins = v.tensor_scalar(l2[:, tile, :], x2[:, tile, :], mv[:, i, 0:1], rstd[:, i:i + 1],
                                              ALU.subtract, ALU.mult)
                    ins.then_inc(s_l2[q], 1)

            ahead(dve, batch)

        @block.tensor
        def _(pe):
            pe.wait_ge(s_wlo, 1)
            def batch(b):
                for q in range(G):
                    pe.wait_ge(s_lov[q], b + 1)
                    pe.wait_ge(s_lop[q], b + 1)
                    pe.wait_ge(s_l2[q], b)
                    for i in range(GT):
                        n = 0
                        for k in range(HP):
                            for lhs, rhs in ((a_hi, wo_hi), (a_hi, wo_lo), (a_lo, wo_hi)):
                                ins = nc.tensor.matmul(ps_y[:, q * GT + i, 0:D], lhs[:, q % 2, k, i * P:(i + 1) * P],
                                                       rhs[:, k, :], start=n == 0, stop=n == 3 * HP - 1)
                                n += 1
                        ins.then_inc(s_y[q], 1)

            batches(pe, batch)


def route(nc, Wr, l2, slots, gates, expert):
    with ExitStack() as ctx:
        t = Tools(nc, ctx)
        ident = t.sb("r_ident", [P, P])
        before = t.sb("before", [P, P])
        ones = t.sb("ones", [P, P])
        wr = t.sb("wr", [P, C, E])
        l2T = t.sb("l2T", [P, 2, 2, C, P])
        eight = t.sb("eight", [P, TT, E])
        tiles = t.sb("tiles", [P, ROUTED + 2, E])
        logit = t.sb("logit", [P, TT, E])
        top = t.sb("top", [P, TT])
        prob = t.sb("prob", [P, TT, E])
        total = t.sb("total", [P, TT])
        best = t.sb("best", [P, TT, 8])
        index = t.sb("index", [P, TT, 8], U32)
        index_f = t.sb("index_f", [P, TT, 2])
        hot = t.sb("hot", [P, 2, TT, E])
        both = t.sb("both", [P, TT, E])
        cum = t.sb("cum", [P, 2, TT, E])
        base = t.sb("base", [P, TT, E])
        filled = t.sb("filled", [P, E])
        filled_i = t.sb("filled_i", [P, E], I32)
        end = t.sb("end", [P, E])
        start = t.sb("start", [P, E])
        pick = t.sb("pick", [P, 2, TT, E])
        slot_f = t.sb("slot_f", [P, 2, TT])
        reached = t.sb("reached", [P, ROUTED + 2, E])
        expert_f = t.sb("expert_f", [P, ROUTED + 2])
        ps_t = t.ps("r_ps_t", [P, 2, 512])
        ps_l = t.ps("r_ps_l", [P, 512])
        ps_c = t.ps("r_ps_c", [P, 2, 512])
        s_c, s_wr, s_t, s_tc, s_lg, s_v, s_e, s_cnt = (t.sem("r_" + n) for n in ("c", "wr", "t", "tc", "lg", "v", "e", "cnt"))
        s_in = t.sem("r_in")
        block = ctx.enter_context(nc.Block())

        @block.gpsimd
        def _(pool):
            pool.dma_start(wr[:, :, :], Wr.rearrange("(c p) e -> p c e", p=P)).then_inc(s_wr, 16)
            pool.memset(ident[:, :], 0.0).then_inc(s_c, 1)
            pool.memset(before[:, :], 1.0).then_inc(s_c, 1)
            pool.memset(ones[:, :], 1.0).then_inc(s_c, 1)
            pool.iota(eight[:, :, :], pattern=[[0, TT], [1, E]], base=0, channel_multiplier=0,
                      allow_small_or_imprecise_dtypes=True).then_inc(s_c, 1)
            pool.iota(tiles[:, :, :], pattern=[[1, ROUTED + 2], [0, E]], base=0, channel_multiplier=0,
                      allow_small_or_imprecise_dtypes=True).then_inc(s_c, 1)
            pool.wait_ge(s_c, 5)
            pool.affine_select(out=ident[:, :], in_=ident[:, :], compare_op=ALU.not_equal, fill=1.0,
                               base=0, pattern=[[-1, P]], channel_multiplier=1).then_inc(s_c, 1)
            pool.affine_select(out=before[:, :], in_=before[:, :], compare_op=ALU.is_gt, fill=0.0,
                               base=0, pattern=[[1, P]], channel_multiplier=-1).then_inc(s_c, 1)

        @block.tensor
        def _(pe):
            pe.wait_ge(s_c, 7)
            pe.wait_ge(s_wr, 16)
            for j in range(TT // 2 + 1):
                if j < TT // 2:
                    if j >= 2:
                        pe.wait_ge(s_tc, j - 1)
                    for i in range(2):
                        for c in range(C):
                            ins = nc.tensor.transpose(ps_t[:, j % 2, (2 * i + c) * P:(2 * i + c + 1) * P],
                                                      l2[:, 2 * j + i, c * P:(c + 1) * P], ident[:, :])
                    ins.then_inc(s_t, 1)
                if j:
                    pe.wait_ge(s_tc, j)
                    for i in range(2):
                        tile = 2 * (j - 1) + i
                        for c in range(C):
                            ins = nc.tensor.matmul(ps_l[:, tile * E:(tile + 1) * E], l2T[:, (j - 1) % 2, i, c, :],
                                                   wr[:, c, :], start=c == 0, stop=c == C - 1)
                    ins.then_inc(s_lg, 1)
            pe.wait_ge(s_cnt, 1)
            nc.tensor.matmul(ps_c[:, 0, 0:TT * E], before[:, :], both[:, :, :], start=True, stop=True)
            nc.tensor.matmul(ps_c[:, 1, 0:TT * E], ones[:, :], both[:, :, :], start=True, stop=True).then_inc(s_cnt, 1)

        @block.scalar
        def _(act):
            for j in range(TT // 2):
                act.wait_ge(s_t, j + 1)
                if j >= 2:
                    act.wait_ge(s_lg, j - 1)
                act.activation(l2T[:, j % 2], ps_t[:, j % 2, :].rearrange("p (i c n) -> p i c n", i=2, c=C),
                               ACT.Copy).then_inc(s_tc, 1)
            act.wait_ge(s_in, 1)
            act.activation(prob[:, :, :], logit[:, :, :], ACT.Exp).then_inc(s_e, 1)

        @block.vector
        def _(dve):
            v = nc.vector
            n = [0]

            def do(ins):
                step(dve, s_v, n, ins)

            tb = lambda ap: ap.unsqueeze(2).broadcast_to([P, TT, E])
            dve.wait_ge(s_lg, TT // 2)
            dve.wait_ge(s_c, 7)
            do(v.tensor_copy(logit[:, :, :], ps_l[:, 0:TT * E].rearrange("p (t e) -> p t e", e=E)))
            do(v.tensor_reduce(top[:, :], logit[:, :, :], AX.X, ALU.max))
            v.tensor_tensor(logit[:, :, :], logit[:, :, :], tb(top[:, :]), ALU.subtract).then_inc(s_in, 1)
            dve.wait_ge(s_e, 1)
            do(v.tensor_reduce(total[:, :], prob[:, :, :], AX.X, ALU.add))
            do(v.reciprocal(total[:, :], total[:, :]))
            do(v.tensor_tensor(prob[:, :, :], prob[:, :, :], tb(total[:, :]), ALU.mult))
            for i in range(TT):
                v.max(best[:, i, :], prob[:, i, :]).then_inc(s_v, 1)
            n[0] += TT
            dve.wait_ge(s_v, n[0])
            for i in range(TT):
                v.max_index(index[:, i, :], best[:, i, :], prob[:, i, :]).then_inc(s_v, 1)
            n[0] += TT
            dve.wait_ge(s_v, n[0])
            do(v.tensor_tensor(total[:, :], best[:, :, 0], best[:, :, 1], ALU.add))
            do(v.reciprocal(total[:, :], total[:, :]))
            do(v.tensor_tensor(gates[:, :, :], best[:, :, 0:2], total[:, :].unsqueeze(2).broadcast_to([P, TT, 2]), ALU.mult))
            do(v.tensor_copy(index_f[:, :, :], index[:, :, 0:2]))
            for k in range(2):
                do(v.tensor_tensor(hot[:, k], eight[:, :, :], tb(index_f[:, :, k]), ALU.is_equal))
            v.tensor_tensor(both[:, :, :], hot[:, 0], hot[:, 1], ALU.add).then_inc(s_cnt, 1)
            dve.wait_ge(s_cnt, 2)
            do(v.tensor_copy(cum[:, 0], ps_c[:, 1, 0:TT * E].rearrange("p (t e) -> p t e", e=E)))
            k, s = 0, 1
            while s < TT:
                do(v.tensor_copy(cum[:, 1 - k, 0:s, :], cum[:, k, 0:s, :]))
                do(v.tensor_tensor(cum[:, 1 - k, s:, :], cum[:, k, s:, :], cum[:, k, 0:TT - s, :], ALU.add))
                k, s = 1 - k, 2 * s
            do(v.tensor_scalar(filled[:, :], cum[:, k, TT - 1, :], float(TS - 1), None, ALU.add))
            do(v.tensor_copy(filled_i[:, :], filled[:, :]))
            do(v.tensor_scalar(filled_i[:, :], filled_i[:, :], TS.bit_length() - 1, None, ALU.logical_shift_right))
            do(v.tensor_copy(filled[:, :], filled_i[:, :]))
            do(v.tensor_copy(end[:, 0:1], filled[:, 0:1]))
            for e in range(1, E):
                do(v.tensor_tensor(end[:, e:e + 1], end[:, e - 1:e], filled[:, e:e + 1], ALU.add))
            do(v.tensor_tensor(start[:, :], end[:, :], filled[:, :], ALU.subtract))
            do(v.tensor_scalar(start[:, :], start[:, :], float(TS), None, ALU.mult))
            do(v.tensor_tensor(base[:, :, :], ps_c[:, 0, 0:TT * E].rearrange("p (t e) -> p t e", e=E),
                               start[:, :].unsqueeze(1).broadcast_to([P, TT, E]), ALU.add))
            do(v.tensor_tensor(base[:, 1:, :], base[:, 1:, :], cum[:, k, 0:TT - 1, :], ALU.add))
            for j in range(2):
                do(v.tensor_tensor(pick[:, j], hot[:, j], base[:, :, :], ALU.mult))
            do(v.tensor_reduce(slot_f[:, :, :], pick[:, :, :, :], AX.X, ALU.add))
            do(v.tensor_copy(slots[:, :, :], slot_f[:, :, :]))
            do(v.tensor_tensor(reached[:, :, :], tiles[:, :, :], end[:, :].unsqueeze(1).broadcast_to([P, ROUTED + 2, E]), ALU.is_ge))
            do(v.tensor_reduce(expert_f[:, :], reached[:, :, :], AX.X, ALU.add))
            do(v.tensor_scalar(expert_f[:, :], expert_f[:, :], float(E - 1), None, ALU.min))
            do(v.tensor_copy(expert[:, :], expert_f[:, :]))


def experts(nc, weights_s, weights, expert, slots, tokens, routed, x2, ys):
    Wfc, bfc, Wproj, bproj = weights
    with ExitStack() as ctx:
        t = Tools(nc, ctx)
        ident = t.sb("f_ident", [P, P])
        moved = t.sb("moved", [P, 4, D])
        xt = t.sb("xt", [P, 2, 2, D])
        xT_hi = t.sb("xT_hi", [P, 2, C, TS], F32R)
        xT_lo = t.sb("xT_lo", [P, 2, C, TS], F32R)
        w1 = t.sb("w1", [P, 2, C, HID])
        w2 = t.sb("w2", [P, 2, HC, D])
        b1 = t.sb("b1", [P, 2, HC])
        b2 = t.sb("b2", [P, 2, D])
        w1_hi = t.sb("w1_hi", [P, 2, C, HC, P], F32R)
        w1_lo = t.sb("w1_lo", [P, 2, C, HC, P], F32R)
        w2_hi = t.sb("w2_hi", [P, 2, HC, D], F32R)
        w2_lo = t.sb("w2_lo", [P, 2, HC, D], F32R)
        b1_use = t.sb("b1_use", [P, 2, HC])
        b2_use = t.sb("b2_use", [P, 2, D])
        ht = t.sb("ht", [P, 4, 2, TS])
        h_hi = t.sb("h_hi", [P, 2, HC, TS], F32R)
        h_lo = t.sb("h_lo", [P, 2, HC, TS], F32R)
        y = t.sb("y", [P, 2, 2, D])
        ps_t = t.ps("f_ps_t", [P, C, TS])
        ps_h = t.ps("f_ps_h", [P, 4, 2, TS])
        ps_y = t.ps("f_ps_y", [P, 2, 512])
        s_id = t.sem("f_id")
        s_xl, s_raw1, s_raw2, s_ys = ([t.sem("f_%s_%d" % (n, i)) for i in range(2)] for n in ("xl", "raw1", "raw2", "ys"))
        s_w1h, s_w1l, s_b1, s_w2h, s_w2l, s_b2 = (t.sem("f_" + n) for n in ("w1h", "w1l", "b1", "w2h", "w2l", "b2"))
        s_xt, s_xh, s_xlo, s_h, s_y, s_yv, s_sum = (t.sem("f_" + n) for n in ("xt", "xh", "xlo", "h", "y", "yv", "sum"))
        s_g, s_hh, s_hl = ([t.sem("f_%s_%d" % (n, i)) for i in range(4)] for n in ("g", "hh", "hl"))
        s_mv, s_sc = ([t.sem("f_%s_%d" % (n, i)) for i in range(4)] for n in ("mv", "sc"))
        block = ctx.enter_context(nc.Block())
        tokens_v = tokens.rearrange("(t r p) d -> t p r d", r=2, p=P)
        routed_v = routed.rearrange("(t r p) d -> t p r d", r=2, p=P)
        ys_v = ys.rearrange("(t r p) d -> t p r d", r=2, p=P)
        S2, LAST = SHARED // 2, (SHARED + ROUTED) // 2 - 1

        def loops(eng, step, first=0):
            def pair(U, shared, left=9):
                for s in range(2):
                    step(U, s, shared, left - s)

            pair(0, True)
            with eng.Fori(1, S2 - 1) as u:
                pair(u, True)
            pair(S2 - 1, True)
            for u in range(first):
                pair(S2 + u, False)
            with eng.Fori(S2 + first, LAST) as u:
                pair(u, False)
            pair(LAST, False, 1)

        def slot_of(U, s, shared, ahead):
            m = U * 2 + (s + ahead)
            if shared and not (isinstance(U, int) and m >= SHARED):
                return 1, 1
            return (s + ahead) % 2, m - (SHARED - 2)

        def last_shared(U, s):
            return isinstance(U, int) and U * 2 + s == SHARED - 1

        @block.sync
        def _(sp):
            def load1(slot, e):
                if e is None:
                    f, bf = weights_s[:2]
                    sp.dma_start(w1[:, slot], f.rearrange("(c p) n -> p c n", p=P)).then_inc(s_raw1[slot], 16)
                    sp.dma_start(b1[:, slot], bf.rearrange("(p c) -> p c", c=HC)).then_inc(s_raw1[slot], 16)
                else:
                    sp.dma_start(w1[:, slot:slot + 1], Wfc[bass.ds(e, 1)].rearrange("e (c p) n -> p e c n", p=P)).then_inc(s_raw1[slot], 16)
                    sp.dma_start(b1[:, slot:slot + 1], bfc[bass.ds(e, 1)].rearrange("e (p c) -> p e c", c=HC)).then_inc(s_raw1[slot], 16)

            def load2(slot, e):
                if e is None:
                    pr, bp = weights_s[2:]
                    sp.dma_start(w2[:, slot], pr.rearrange("(p c) n -> p c n", c=HC)).then_inc(s_raw2[slot], 16)
                    sp.dma_start(b2[:, slot], bp.rearrange("(a n) -> a n", a=1).broadcast_to([P, D])).then_inc(s_raw2[slot], 16)
                else:
                    sp.dma_start(w2[:, slot:slot + 1], Wproj[bass.ds(e, 1)].rearrange("e (p c) n -> p e c n", c=HC)).then_inc(s_raw2[slot], 16)
                    sp.dma_start(b2[:, slot], bproj[bass.ds(e, 1)].broadcast_to([P, D])).then_inc(s_raw2[slot], 16)

            def expert_of(j):
                return sp.value_load(expert[0:1, bass.ds(j, 1)], min_val=0, max_val=E - 1)

            def split1(n):
                sp.wait_ge(s_w1h, n)
                sp.wait_ge(s_w1l, n)
                sp.wait_ge(s_b1, n)

            def split2(n):
                sp.wait_ge(s_w2h, n)
                sp.wait_ge(s_w2l, n)
                sp.wait_ge(s_b2, n)

            def load_x(src, tile, parity):
                sp.dma_start(xt[:, parity:parity + 1], src[bass.ds(tile, 1)].rearrange("t p r d -> p t r d")).then_inc(s_xl[parity], 16)

            load1(1, None)
            load_x(tokens_v, 0, 0)
            load_x(tokens_v, 1, 1)
            load2(1, None)
            e0, e1, e2 = expert_of(0), expert_of(1), expert_of(2)
            load1(0, e0)
            load2(0, e0)
            split1(1)
            load1(1, e1)
            split2(1)
            load2(1, e1)
            split1(2)
            load1(0, e2)

            def step(U, s, shared, left):
                m = U * 2 + s
                if left >= 2:
                    sp.wait_ge(s_xt, m + 1)
                    if shared and isinstance(U, int) and m + 2 >= SHARED:
                        if s == 0:
                            for i in range(4):
                                sp.wait_ge(s_sc[i], 16 * 2 * TT // 4)
                        load_x(routed_v, m + 2 - SHARED, s)
                    elif shared:
                        load_x(tokens_v, m + 2, s)
                    else:
                        load_x(routed_v, m + (2 - SHARED), s)
                if not shared and left >= 2:
                    e = expert_of(m + (2 - SHARED))
                    split2(m - (SHARED - 2))
                    load2(s, e)
                    if left >= 3:
                        e = expert_of(m + (3 - SHARED))
                        split1(m - (SHARED - 3))
                        load1(1 - s, e)
                if not shared:
                    sp.wait_ge(s_yv, m + 1)
                    sp.dma_start(ys_v[bass.ds(m - SHARED, 1)].rearrange("t p r d -> p t r d"), y[:, s:s + 1]).then_inc(s_ys[s], 16)

            loops(sp, step)
            for s in range(2):
                sp.wait_ge(s_ys[s], 16 * ROUTED // 2)

        @block.gpsimd
        def _(pool):
            g = nc.gpsimd
            pool.memset(ident[:, :], 0.0).then_inc(s_id, 1)
            pool.wait_ge(s_id, 1)
            pool.affine_select(out=ident[:, :], in_=ident[:, :], compare_op=ALU.not_equal, fill=1.0,
                               base=0, pattern=[[-1, P]], channel_multiplier=1).then_inc(s_id, 1)

            def lower_w2(slot):
                g.tensor_tensor(w2_lo[:, slot], w2[:, slot], w2_hi[:, slot].bitcast(F32), ALU.subtract).then_inc(s_w2l, 1)

            pool.wait_ge(s_w2h, 1)
            lower_w2(1)
            pool.wait_ge(s_w2h, 2)
            lower_w2(0)
            moved_v = tokens.rearrange("(t p) d -> t p d", p=P)
            for tile in range(TT + 3):
                if tile < TT:
                    i = tile % 4
                    if tile >= 4:
                        pool.wait_ge(s_sc[i], 32 * (tile // 4))
                    pool.dma_start(moved[:, i, :], moved_v[tile]).then_inc(s_mv[i], 16)
                if tile >= 3:
                    back = tile - 3
                    i = back % 4
                    pool.wait_ge(s_mv[i], 16 * (back // 4 + 1))
                    for k in range(2):
                        pool.indirect_dma_start(out=routed[:, :], out_offset=bass.IndirectOffsetOnAxis(ap=slots[:, k, back:back + 1], axis=0),
                                                in_=moved[:, i, :], in_offset=None).then_inc(s_sc[i], 16)

            def pair(U, last=False):
                for s in range(1 if last else 2):
                    pool.wait_ge(s_w2h, U * 2 + (s + 3 - SHARED))
                    lower_w2(1 - s)

            with pool.Fori(S2, LAST) as u:
                pair(u)
            pair(LAST, True)

        @block.tensor
        def _(pe):
            mm = nc.tensor.matmul
            pe.wait_ge(s_id, 2)

            def transpose(parity):
                for r in range(2):
                    for c in range(C):
                        ins = nc.tensor.transpose(ps_t[:, c, r * P:(r + 1) * P], xt[:, parity, r, c * P:(c + 1) * P], ident[:, :])
                ins.then_inc(s_xt, 1)

            def fc(m, p, parity, slot):
                pe.wait_ge(s_g[p], m)
                for i in range(2):
                    n = 0
                    for k in range(C):
                        for w, x_ in ((w1_hi, xT_hi), (w1_hi, xT_lo), (w1_lo, xT_hi)):
                            ins = mm(ps_h[:, p, i, :], w[:, slot, k, 2 * p + i, :], x_[:, parity, k, :],
                                     start=n == 0, stop=n == 3 * C - 1)
                            n += 1
                ins.then_inc(s_h, 1)

            def proj(m, p, parity, slot):
                pe.wait_ge(s_hl[p], m + 1)
                for c in (2 * p, 2 * p + 1):
                    for r in range(2):
                        for n, (h, w) in enumerate(((h_hi, w2_hi), (h_hi, w2_lo), (h_lo, w2_hi))):
                            ins = mm(ps_y[:, r, 0:D], h[:, parity, c, r * P:(r + 1) * P], w[:, slot, c, :],
                                     start=c == 0 and n == 0, stop=c == HC - 1 and n == 2)
                if p == 3:
                    ins.then_inc(s_y, 1)

            pe.wait_ge(s_xl[0], 16)
            transpose(0)
            pe.wait_ge(s_xl[1], 16)
            pe.wait_ge(s_xlo, 1)
            transpose(1)
            pe.wait_ge(s_w1h, 1)
            pe.wait_ge(s_w1l, 1)
            for p in range(4):
                fc(0, p, 0, 1)
            pe.wait_ge(s_w2h, 1)
            pe.wait_ge(s_w2l, 1)

            def step(U, s, shared, left):
                m = U * 2 + s
                (slot1, n1), (slot2, n2) = slot_of(U, s, shared, 1), slot_of(U, s, shared, 0)
                if left >= 1:
                    pe.wait_ge(s_xlo, m + 2)
                    pe.wait_ge(s_w1h, n1)
                    pe.wait_ge(s_w1l, n1)
                for p in range(4):
                    if left >= 1:
                        fc(m + 1, p, 1 - s, slot1)
                    if p == 0:
                        pe.wait_ge(s_yv, m)
                        pe.wait_ge(s_w2h, n2)
                        pe.wait_ge(s_w2l, n2)
                    proj(m, p, s, slot2)
                    if p == 2 and left >= 2:
                        pe.wait_ge(s_xl[s], U * 16 + 32)
                        transpose(s)

            loops(pe, step)

        @block.scalar
        def _(act):
            def upper_w1(slot):
                act.activation(w1_hi[:, slot], w1[:, slot].rearrange("p k (m c) -> p k c m", c=HC), ACT.Copy).then_inc(s_w1h, 1)
                act.activation(b1_use[:, slot], b1[:, slot], ACT.Copy).then_inc(s_b1, 1)

            def upper_w2(slot):
                act.activation(w2_hi[:, slot], w2[:, slot], ACT.Copy).then_inc(s_w2h, 1)

            def upper_x(tile, parity):
                act.wait_ge(s_xt, tile + 1)
                act.activation(xT_hi[:, parity], ps_t[:, :, :], ACT.Copy).then_inc(s_xh, 1)

            def gelu(m, p, slot, n):
                act.wait_ge(s_h, m * 4 + (p + 1))
                act.wait_ge(s_hl[p], m)
                if p == 0:
                    act.wait_ge(s_b1, n)
                for i in range(2):
                    c = 2 * p + i
                    ins = act.activation(ht[:, p, i, :], ps_h[:, p, i, :], ACT.Gelu_apprx_tanh, bias=b1_use[:, slot, c:c + 1])
                ins.then_inc(s_g[p], 1)

            act.wait_ge(s_raw1[1], 32)
            upper_w1(1)
            upper_x(0, 0)
            upper_x(1, 1)
            act.wait_ge(s_raw2[1], 32)
            upper_w2(1)
            for p in range(4):
                gelu(0, p, 1, 1)
            act.wait_ge(s_raw1[0], 32)
            upper_w1(0)
            act.wait_ge(s_raw2[0], 32)
            upper_w2(0)

            def step(U, s, shared, left):
                m = U * 2 + s
                slot, n = slot_of(U, s, shared, 1)
                if not shared and left >= 1:
                    act.wait_ge(s_raw2[1 - s], (U - S2) * 32 + 64)
                    act.wait_ge(s_y, m)
                    upper_w2(1 - s)
                for p in range(4):
                    if left >= 1:
                        gelu(m + 1, p, slot, n)
                    if p == 1 and left >= 2 and (not shared or last_shared(U, s)):
                        act.wait_ge(s_raw1[s], (U - S2) * 32 + 32 * (2 + s))
                        upper_w1(s)
                    if p == 2 and left >= 2:
                        upper_x(m + 2, s)

            loops(act, step)

        @block.vector
        def _(dve):
            v = nc.vector

            def lower_w1(slot, n):
                dve.wait_ge(s_w1h, n)
                v.tensor_tensor(w1_lo[:, slot], w1[:, slot].rearrange("p k (m c) -> p k c m", c=HC),
                                w1_hi[:, slot].bitcast(F32), ALU.subtract).then_inc(s_w1l, 1)

            def bias_2(slot, n):
                dve.wait_ge(s_w2h, n)
                v.tensor_copy(b2_use[:, slot], b2[:, slot]).then_inc(s_b2, 1)

            def lower_x(tile, parity):
                dve.wait_ge(s_xh, tile + 1)
                v.tensor_tensor(xT_lo[:, parity], ps_t[:, :, :], xT_hi[:, parity].bitcast(F32), ALU.subtract).then_inc(s_xlo, 1)

            def hidden(m, p, parity):
                dve.wait_ge(s_g[p], m + 1)
                v.tensor_copy(h_hi[:, parity, 2 * p:2 * p + 2, :], ht[:, p]).then_inc(s_hh[p], 1)
                dve.wait_ge(s_hh[p], m + 1)
                v.tensor_tensor(h_lo[:, parity, 2 * p:2 * p + 2, :], ht[:, p], h_hi[:, parity, 2 * p:2 * p + 2, :].bitcast(F32),
                                ALU.subtract).then_inc(s_hl[p], 1)

            lower_w1(1, 1)
            lower_x(0, 0)
            lower_x(1, 1)
            bias_2(1, 1)
            for p in range(4):
                hidden(0, p, 0)
            lower_w1(0, 2)
            bias_2(0, 2)

            def step(U, s, shared, left):
                m = U * 2 + s
                slot, n = slot_of(U, s, shared, 0)
                if not shared and left >= 1:
                    dve.wait_ge(s_yv, m)
                    bias_2(1 - s, m - (SHARED - 3))
                for p in range(4):
                    if left >= 1:
                        hidden(m + 1, p, 1 - s)
                    if p == 1 and left >= 2 and (not shared or last_shared(U, s)):
                        lower_w1(s, m - (SHARED - 4))
                    if p == 2 and left >= 2:
                        lower_x(m + 2, s)
                dve.wait_ge(s_b2, n)
                dve.wait_ge(s_y, m + 1)
                if not shared:
                    dve.wait_ge(s_ys[s], (U - S2) * 16)
                v.tensor_tensor(y[:, s], ps_y[:, :, 0:D], b2_use[:, slot].unsqueeze(1).broadcast_to([P, 2, D]),
                                ALU.add).then_inc(s_yv, 1)
                if shared:
                    dve.wait_ge(s_yv, m + 1)
                    x2_tile = x2[:, bass.ds(U * 4 + 2 * s, 2), :]
                    v.tensor_tensor(x2_tile, x2_tile, y[:, s], ALU.add).then_inc(s_sum, 1)

            loops(dve, step, first=1)


def combine(nc, x2, slots, gates, ys, out):
    NB, PAIRS = 4, TT // 2
    with ExitStack() as ctx:
        t = Tools(nc, ctx)
        y = t.sb("c_y", [P, NB, 2, 2, D])
        s_y = [t.sem("c_y%d" % i) for i in range(NB)]
        s_half, s_sum, s_out = t.sem("c_half"), t.sem("c_sum"), t.sem("c_out")
        block = ctx.enter_context(nc.Block())
        out_v = out.rearrange("b (g t p) d -> (b g) p t d", t=2, p=P)

        @block.gpsimd
        def _(pool):
            for k in range(PAIRS):
                i = k % NB
                if k >= NB:
                    pool.wait_ge(s_y[i], 64 * (k // NB))
                    pool.wait_ge(s_sum, 2 * (k - NB + 1))
                for tile in range(2):
                    for j in range(2):
                        pool.indirect_dma_start(out=y[:, i, tile, j, :], out_offset=None, in_=ys[:, :],
                                                in_offset=bass.IndirectOffsetOnAxis(ap=slots[:, j, 2 * k + tile:2 * k + tile + 1], axis=0)
                                                ).then_inc(s_y[i], 16)

        @block.vector
        def _(dve):
            for k in range(PAIRS):
                i = k % NB
                dve.wait_ge(s_y[i], 64 * (k // NB + 1))
                for j, done in enumerate((s_half, s_sum)):
                    if j:
                        dve.wait_ge(s_half, 2 * k + 2)
                    for tile in range(2):
                        n = 2 * k + tile
                        nc.vector.scalar_tensor_tensor(x2[:, n, :], y[:, i, tile, j, :], gates[:, n, j:j + 1], x2[:, n, :],
                                                       ALU.mult, ALU.add).then_inc(done, 1)

        @block.sync
        def _(sp):
            for k in range(PAIRS):
                sp.wait_ge(s_sum, 2 * k + 2)
                sp.dma_start(out_v[k], x2[:, 2 * k:2 * k + 2, :]).then_inc(s_out, 16)
            sp.wait_ge(s_out, 16 * PAIRS)


NAMES = ["x", "ctx_1024", "mask_BxS2_bf1"] + ["L0_xattn_" + n for n in (
    "ln_x_g", "ln_x_b", "ln_l_g", "ln_l_b", "qn_g", "kn_g", "Wq", "Wkv", "Wout", "bout")] + ["L0_ffn_" + n for n in (
    "Wfc_s", "bfc_s", "Wproj_s", "bproj_s", "Wr", "Wfc", "bfc", "Wproj", "bproj")]


def cross_attention_moe(nc, x, ctx_in, mask, ln_x_g, ln_x_b, ln_l_g, ln_l_b, qn_g, kn_g, Wq, Wkv, Wout, bout,
                        Wfc_s, bfc_s, Wproj_s, bproj_s, Wr, Wfc, bfc, Wproj, bproj, out):
    def dram(name, *shape):
        return nc.dram_tensor(name + "_dram", shape, F32, kind="Internal").ap()

    lnT = dram("lnT", B, P, 2, C, KEYS)
    wHead = dram("wHead", H, P, 2, C, 3 * DH)
    maskRow, maskCol = dram("maskRow", B, P), dram("maskCol", P, B)
    attT = dram("attT", HEADS, DH + 1, N)
    rden = dram("rden", HEADS, N)
    tokens = dram("tokens", TOKENS, D)
    routed = dram("routed", ROWS, D)
    ys = dram("ys", ROUTED * TS, D)
    prepare(nc, x, ctx_in, mask, ln_x_g, ln_x_b, ln_l_g, ln_l_b, Wq, Wkv, lnT, wHead, maskRow, maskCol)
    attention(nc, qn_g, kn_g, lnT, wHead, maskRow, maskCol, attT, routed)
    with ExitStack() as ctx:
        t = Tools(nc, ctx)
        x2 = t.sb("x2", [P, TT, D])
        slots = t.sb("slots", [P, 2, TT], U32)
        gates = t.sb("gates", [P, TT, 2])
        expert = t.sb("expert", [P, ROUTED + 2], I32)
        with nc.sbuf_tensor("l2", [P, TT, D], F32) as l2:
            project_out(nc, x, Wout, bout, attT, rden, tokens, x2, l2)
            route(nc, Wr, l2, slots, gates, expert)
        experts(nc, [Wfc_s, bfc_s, Wproj_s, bproj_s], [Wfc, bfc, Wproj, bproj], expert, slots, tokens, routed, x2, ys)
        combine(nc, x2, slots, gates, ys, out)


def kernel(**inputs):
    import numpy as np
    import concourse.bacc as bacc
    from concourse.bass_utils import run_bass_kernel_spmd

    nc = bacc.Bacc("TRN2", target_bir_lowering=False, num_devices=1)
    arrays, args = {}, []
    for name in NAMES:
        a = np.ascontiguousarray(inputs[name])
        if a.dtype == np.bool_:
            a = a.view(np.uint8)
        arrays["in_" + name] = a
        args.append(nc.dram_tensor("in_" + name, a.shape, mybir.dt.from_np(a.dtype), kind="ExternalInput").ap())
    args.append(nc.dram_tensor("out_dram", (B, N, D), F32, kind="ExternalOutput").ap())
    cross_attention_moe(nc, *args)
    r = run_bass_kernel_spmd(nc, [arrays], core_ids=[0])
    return r.results[0]["out_dram"]
```

```python
from contextlib import ExitStack

import concourse.bass as bass
from concourse import mybir

F32 = mybir.dt.float32
F32R = mybir.dt.float32r
I32 = mybir.dt.int32
U32 = mybir.dt.uint32
U8 = mybir.dt.uint8
ALU = mybir.AluOpType
ACT = mybir.ActivationFunctionType
AX = mybir.AxisListType

P = 128
B, N, D = 4, 1024, 256
CTX = 77
H, DH = 16, 64
C = D // P
NT = N // P
KT = NT + 1
KEYS = KT * P
QB = N // 512
HEADS = B * H
LN_EPS, RMS_EPS = 1e-5, 1e-8
NEG = -1e30
TOKENS = B * N
TT = TOKENS // P
GT = 2
E = 8
HID = 4 * D
HC = HID // P
TS = 2 * P
SHARED = TOKENS // TS
ROUTED = (2 * TOKENS + E * (TS - 1)) // TS
ROUTED += ROUTED % 2
ROWS = (ROUTED + 1) * TS


class Tools:

    def __init__(self, nc, ctx):
        self.nc, self.ctx = nc, ctx

    def sb(self, name, shape, dt=F32):
        return self.ctx.enter_context(self.nc.sbuf_tensor(name, shape, dt))

    def ps(self, name, shape):
        return self.ctx.enter_context(self.nc.psum_tensor(name, shape, F32))

    def sem(self, name):
        return self.ctx.enter_context(self.nc.semaphore(name))


def step(eng, sem, count, ins):
    ins.then_inc(sem, 1)
    count[0] += 1
    eng.wait_ge(sem, count[0])


def prepare(nc, x, ctx_in, mask, ln_x_g, ln_x_b, ln_l_g, ln_l_b, Wq, Wkv, lnT, wHead, maskRow, maskCol):
    with ExitStack() as ctx:
        t = Tools(nc, ctx)
        ident = t.sb("ident", [P, P])
        xin = t.sb("xin", [P, 2, NT, D])
        z = t.sb("z", [P, NT, D])
        cz = t.sb("cz", [CTX, B, D])
        stats = t.sb("stats", [P, NT, 6])
        mv = t.sb("mv", [P, NT, 2])
        var_eps = t.sb("var_eps", [P, NT])
        rstd = t.sb("rstd", [P, NT])
        half = t.sb("half", [P, NT])
        gain = t.sb("gain", [P, 4, C])
        full = t.sb("full", [P, 2, 512])
        out = t.sb("out", [P, 2, 2, C, KEYS], F32R)
        w = t.sb("w", [P, C, 3 * H * DH])
        wh = t.sb("wh", [P, H, 2, C, 3 * DH], F32R)
        mk8 = t.sb("mk8", [P, B], U8)
        mkf = t.sb("mkf", [P, B])
        mr8 = t.sb("mr8", [B, P], U8)
        mrf = t.sb("mrf", [B, P], F32R)
        tp = t.ps("tp", [P, 2, 512])
        s_x = [t.sem("s_x0"), t.sem("s_x1")]
        s_c, s_w, s_g, s_m = t.sem("s_c"), t.sem("s_w"), t.sem("s_g"), t.sem("s_m")
        s_id, s_ve, s_rs, s_z, s_cz = t.sem("s_id"), t.sem("s_ve"), t.sem("s_rs"), t.sem("s_z"), t.sem("s_cz")
        s_tp, s_full, s_fullfree, s_split = t.sem("s_tp"), t.sem("s_full"), t.sem("s_fullfree"), t.sem("s_split")
        s_out, s_whi, s_wlo, s_mk, s_wout = t.sem("s_out"), t.sem("s_whi"), t.sem("s_wlo"), t.sem("s_mk"), t.sem("s_wout")
        s_v = t.sem("s_v")
        s_lnT = [t.sem("s_lnT0"), t.sem("s_lnT1")]
        block = ctx.enter_context(nc.Block())
        x_v = x.rearrange("b (t p) d -> b p t d", p=P)
        GROUPS = [(c, g) for c in range(C) for g in range(2)]
        JOBS = len(GROUPS) + C

        @block.sync
        def _(sp):
            sp.dma_start(xin[:, 0], x_v[0]).then_inc(s_x[0], 16)
            sp.dma_start(w[:, :, 0:H * DH], Wq.rearrange("(c p) n -> p c n", p=P)).then_inc(s_w, 16)
            sp.dma_start(w[:, :, H * DH:], Wkv.rearrange("(c p) n -> p c n", p=P)).then_inc(s_w, 16)
            sp.dma_start(xin[:, 1], x_v[1]).then_inc(s_x[1], 16)
            for b in range(B):
                if b + 2 < B:
                    sp.wait_ge(s_z, b + 1)
                    sp.dma_start(xin[:, b % 2], x_v[b + 2]).then_inc(s_x[b % 2], 16)
                sp.wait_ge(s_split, 2 * JOBS * (b + 1))
                sp.dma_start(lnT[b], out[:, b % 2].bitcast(F32)).then_inc(s_lnT[b % 2], 16)
                if b == 0:
                    sp.wait_ge(s_mk, 2)
                    sp.dma_start(maskRow, mrf[:, :].bitcast(F32)).then_inc(s_out, 16)
                    sp.dma_start(maskCol, mkf[:, :]).then_inc(s_out, 16)
                    sp.wait_ge(s_whi, 6)
                    sp.wait_ge(s_wlo, 6)
                    sp.dma_start(wHead.rearrange("h p s c n -> p h s c n"), wh[:, :, :, :, :].bitcast(F32)).then_inc(s_out, 16)
            for k in range(2):
                sp.wait_ge(s_lnT[k], 16 * B // 2)
            sp.wait_ge(s_out, 48)

        @block.gpsimd
        def _(pool):
            pool.dma_start(cz[:, :, :], ctx_in.rearrange("b k d -> k b d")).then_inc(s_c, 16)
            pool.memset(ident[:, :], 0.0).then_inc(s_id, 1)
            pool.memset(half[:, :], -0.5).then_inc(s_id, 1)
            pool.memset(mk8[:, :], 0).then_inc(s_id, 1)
            pool.memset(mr8[:, :], 0).then_inc(s_id, 1)
            pool.wait_ge(s_id, 4)
            pool.dma_start(mk8[0:CTX, :], mask.rearrange("b k -> k b"), allow_slow_non_contiguous=True).then_inc(s_m, 16)
            pool.dma_start(mr8[:, 0:CTX], mask).then_inc(s_m, 16)
            for i, v in enumerate((ln_l_g, ln_l_b, ln_x_g, ln_x_b)):
                pool.dma_start(gain[:, i, :], v.rearrange("(c p) -> p c", p=P), allow_slow_non_contiguous=True).then_inc(s_g, 16)
            pool.affine_select(out=ident[:, :], in_=ident[:, :], compare_op=ALU.not_equal, fill=1.0,
                               base=0, pattern=[[-1, P]], channel_multiplier=1).then_inc(s_id, 1)
            pool.wait_ge(s_ve, 1)
            pool.tensor_tensor(rstd[0:CTX, 0:B], var_eps[0:CTX, 0:B], half[0:CTX, 0:B], ALU.pow).then_inc(s_rs, 1)
            for b in range(B):
                pool.wait_ge(s_ve, b + 2)
                pool.tensor_tensor(rstd[:, :], var_eps[:, :], half[:, :], ALU.pow).then_inc(s_rs, 1)

        @block.vector
        def _(dve):
            n = [0]
            v = nc.vector

            def statistics(src, rows, tiles, scale, add):
                for i in range(tiles):
                    v.bn_stats(stats[0:rows, i, :], src(i)).then_inc(s_v, 1)
                n[0] += tiles
                dve.wait_ge(s_v, n[0])
                for i in range(tiles):
                    v.bn_aggr(mv[0:rows, i, :], stats[0:rows, i, :]).then_inc(s_v, 1)
                n[0] += tiles
                dve.wait_ge(s_v, n[0])
                v.tensor_scalar(var_eps[0:rows, 0:tiles], mv[0:rows, 0:tiles, 1], scale, add, ALU.mult, ALU.add).then_inc(s_ve, 1)

            def normalise(dst, src, rows, tiles, k, done):
                dve.wait_ge(s_rs, k)
                for i in range(tiles):
                    ins = v.tensor_scalar(dst(i), src(i), mv[0:rows, i, 0:1], rstd[0:rows, i:i + 1],
                                          ALU.subtract, ALU.mult)
                    if i == tiles - 1:
                        ins.then_inc(done, 1)
                    else:
                        ins.then_inc(s_v, 1)
                        n[0] += 1
                dve.wait_ge(s_v, n[0])

            dve.wait_ge(s_c, 16)
            statistics(lambda b: cz[:, b, :], CTX, B, 1.0, LN_EPS)
            normalise(lambda b: cz[:, b, :], lambda b: cz[:, b, :], CTX, B, 1, s_cz)
            dve.wait_ge(s_m, 32)
            dve.wait_ge(s_id, 4)
            v.tensor_scalar(mkf[:, :], mk8[:, :], -NEG, NEG, ALU.mult, ALU.add).then_inc(s_mk, 1)
            v.tensor_scalar(mrf[:, :], mr8[:, :], -NEG, NEG, ALU.mult, ALU.add).then_inc(s_mk, 1)
            v.memset(out[:, :, :, :, N + CTX:KEYS].bitcast(F32), 0.0).then_inc(s_v, 1)
            n[0] += 1
            dve.wait_ge(s_g, 64)

            def load(b):
                dve.wait_ge(s_x[b % 2], 16 * (b // 2 + 1))
                statistics(lambda i: xin[:, b % 2, i, :], P, NT, 1.0 + LN_EPS, LN_EPS ** 2)

            load(0)
            for b in range(B):
                if b:
                    dve.wait_ge(s_tp, JOBS * b)
                normalise(lambda i: z[:, i, :], lambda i: xin[:, b % 2, i, :], P, NT, b + 2, s_z)
                if b + 1 < B:
                    load(b + 1)
                if b >= 2:
                    dve.wait_ge(s_lnT[b % 2], 16 * (b // 2))
                for j in range(JOBS):
                    jj = JOBS * b + j
                    c = GROUPS[j][0] if j < 4 else j - 4
                    lo, n_ = (512 * GROUPS[j][1], 512) if j < 4 else (N, CTX)
                    dve.wait_ge(s_full, jj + 1)
                    f = full[:, jj % 2, 0:n_]
                    v.tensor_copy(out[:, b % 2, 0, c, lo:lo + n_], f).then_inc(s_split, 1)
                    dve.wait_ge(s_split, 2 * jj + 1)
                    v.tensor_tensor(out[:, b % 2, 1, c, lo:lo + n_], f, out[:, b % 2, 0, c, lo:lo + n_].bitcast(F32),
                                    ALU.subtract).then_inc(s_split, 1)
                if b == 0:
                    for k in range(6):
                        c, part = k // 3, k % 3
                        hi, lo_ = (wh[:, :, s, c, part * DH:(part + 1) * DH] for s in range(2))
                        src_w = w[:, c, part * H * DH:(part + 1) * H * DH].rearrange("p (h d) -> p h d", d=DH)
                        dve.wait_ge(s_whi, k + 1)
                        v.tensor_tensor(lo_, src_w, hi.bitcast(F32), ALU.subtract).then_inc(s_wlo, 1)

        @block.tensor
        def _(pe):
            pe.wait_ge(s_id, 5)
            for b in range(B):
                pe.wait_ge(s_z, b + 1)
                if b == 0:
                    pe.wait_ge(s_cz, 1)
                for j in range(JOBS):
                    jj = JOBS * b + j
                    if jj >= 2:
                        pe.wait_ge(s_full, jj - 1)
                    if j < 4:
                        c, g = GROUPS[j]
                        for i in range(4):
                            ins = nc.tensor.transpose(tp[:, jj % 2, i * P:(i + 1) * P],
                                                      z[:, 4 * g + i, c * P:(c + 1) * P], ident[:, :])
                    else:
                        c = j - 4
                        ins = nc.tensor.transpose(tp[:, jj % 2, 0:CTX], cz[:, b, c * P:(c + 1) * P],
                                                  ident[0:CTX, 0:CTX])
                    ins.then_inc(s_tp, 1)

        @block.scalar
        def _(act):
            act.wait_ge(s_w, 32)
            for k in range(6):
                c, part = k // 3, k % 3
                act.activation(wh[:, :, 0, c, part * DH:(part + 1) * DH],
                               w[:, c, part * H * DH:(part + 1) * H * DH].rearrange("p (h d) -> p h d", d=DH),
                               ACT.Copy).then_inc(s_whi, 1)
            act.wait_ge(s_g, 64)
            for jj in range(B * JOBS):
                j = jj % JOBS
                c = GROUPS[j][0] if j < 4 else j - 4
                n_, kind = (512, 0) if j < 4 else (CTX, 2)
                act.wait_ge(s_tp, jj + 1)
                if jj >= 2:
                    act.wait_ge(s_split, 2 * (jj - 1))
                act.activation(full[:, jj % 2, 0:n_], tp[:, jj % 2, 0:n_], ACT.Identity,
                               scale=gain[:, kind, c:c + 1], bias=gain[:, kind + 1, c:c + 1]).then_inc(s_full, 1)


RING = 3
LAG = 2
UNITS = QB * KT
BANKS = 3
MOST = 70.0


class Plan:

    def __init__(self, hi, values, squares, units):
        self.hi, self.values, self.squares = hi, values, squares
        self.units = [u.split() for u in units.split(",")]
        self.jobs = [j for u in self.units for j in u]
        self.reduced = [j for j in self.jobs if j[0] in "MC"]
        self.copies = [j for j in self.jobs if j[0] not in "MC"]
        assert len(self.units) == UNITS and len(self.jobs) % BANKS == 0 and KT % BANKS == 0
        jobs, reduced, copies = len(self.jobs), len(self.reduced), len(self.copies)
        self.per = {"misc": jobs, "copy": copies, "reduce": reduced, "unit": UNITS, "proj": 1, "split": 1, "one": 1}
        self.pre = {"misc": jobs + KT, "copy": copies + KT, "reduce": reduced, "unit": 0, "proj": 2, "split": 1, "one": 0}


WITH_MAXIMA = Plan(0, 4, 12, "P0,P1 P2,P3 K10,P4 K11,P5 KK Q10,P6 Q11,P7 M00,P8 M01,M10 M11,C0 M20,"
                             "M21 M30,M31 K20,M40 M41,K21 M50,M51 Q20,M60 M61,C1 M70 M71,Q21")
BOUNDED = Plan(3, 7, 12, ",P0,P1,P2,P3,P4,P5,P6,P7,P8,K10,KK,K11,K20,K21 Q10,Q11,Q20 Q21,")


class Window:

    def __init__(self, plan, v, s):
        self.plan, self.v, self.s = plan, v, s
        self.slot, self.other = s % 2, (s + 1) % 2
        self.attend = v is not None
        self.turn = v is not None or s == -1
        self.first = v is not None and isinstance(v, int) and v == 0 and s == 0

    def count(self, kind, k=0, times=1):
        per, pre = self.plan.per[kind], self.plan.pre[kind]
        if self.v is None:
            before = 0 if self.s == -2 else {"misc": KT, "copy": KT, "proj": 1}.get(kind, 0)
            return times * (before + k)
        return self.v * (2 * per * times) + times * (pre + self.s * per + k)

    def here(self):
        return self.plan.jobs if self.turn else [j for j in self.plan.jobs if j[0] == "P"]

    def taken(self, name):
        reduced = self.plan.reduced
        kind = "reduce" if name in reduced else "copy"
        mine = [j for j in self.here() if (j in reduced) == (name in reduced)]
        return kind, self.count(kind, mine.index(name) + 1)

    def copied(self, name):
        return self.taken(name)[1]

    def freed(self, m):
        if m >= BANKS:
            return self.taken(self.here()[m - BANKS])
        if self.v is None and self.s == -2:
            return None
        jobs, reduced = self.plan.jobs, self.plan.reduced
        before = [j for j in jobs if j[0] == "P"] if self.v is None else jobs
        name, after = before[m - BANKS], before[len(before) + m - BANKS + 1:]
        kind = "reduce" if name in reduced else "copy"
        return kind, self.count(kind, -sum((j in reduced) == (name in reduced) for j in after))

    def jobs(self, u):
        here = self.here()
        return [(j, here.index(j)) for j in self.plan.units[u] if j in here]


def windows(eng, plan, body, last=None):
    body(Window(plan, None, -2))
    body(Window(plan, None, -1))
    for s in range(2):
        body(Window(plan, 0, s))
    with eng.Fori(1, HEADS // 2) as v:
        for s in range(2):
            body(Window(plan, v, s))
    if last is not None:
        last(Window(plan, HEADS // 2, 0))


def attention(nc, qn_g, kn_g, lnT, wHead, maskRow, maskCol, attT, routed):
    with ExitStack() as ctx:
        t = Tools(nc, ctx)
        ident = t.sb("a_ident", [P, P])
        lnT_sb = t.sb("lnT_sb", [P, 2, C, KEYS], F32R)
        w_sb = t.sb("w_sb", [P, 2, 2, C, 3 * DH], F32R)
        raw = t.sb("raw", [P, 2, KT, 3 * DH])
        sq = t.sb("sq", [P, KT, 2 * DH])
        ss = t.sb("ss", [P, 2 * KT])
        rs = t.sb("rs", [P, 2 * KT])
        minus_half = t.sb("minus_half", [P, 2 * KT])
        nrm = t.sb("nrm", [P, KT, 2, DH])
        gq = t.sb("gq", [P, DH])
        gk = t.sb("gk", [P, DH])
        gqk = t.sb("gqk", [P, DH])
        k_st = t.sb("k_st", [P, 2, KT, 2 * DH + 2], F32R)
        q_st = t.sb("q_st", [P, 2, NT, 3 * DH + 2], F32R)
        kT1 = t.sb("kT1", [P, 2, KEYS], F32R)
        kT2 = t.sb("kT2", [P, 2, KEYS], F32R)
        qT1 = t.sb("qT1", [P, 2, N], F32R)
        qT2 = t.sb("qT2", [P, 2, N], F32R)
        vA = t.sb("vA", [P, 2, KT, 2 * DH], F32R)
        vC = t.sb("vC", [P, 2, KT, 2 * DH], F32R)
        one_row = t.sb("one_row", [P, P], F32R)
        mrow = t.sb("mrow", [P, 2, P], F32R)
        mcol = t.sb("mcol", [P, 2])
        pr = t.sb("pr", [P, RING, 512])
        pr_hi = t.sb("pr_hi", [P, RING, 512], F32R)
        pr_lo = t.sb("pr_lo", [P, RING, 512], F32R)
        maxima = t.sb("maxima", [P, NT, 3])
        o_sb = t.sb("o_sb", [DH + 1, 2, 512])
        zero = t.sb("zero", [P, D])
        gain2 = t.sb("gain2", [P, DH])
        most2 = t.sb("most2", [P, 1])
        bounded_f = t.sb("bounded_f", [P, 1])
        bounded = t.sb("bounded", [P, 1], I32)
        ps_s = t.ps("ps_s", [P, RING, 512])
        ps_o = t.ps("ps_o", [P, QB, 512])
        ps_m = t.ps("ps_m", [P, BANKS, 512])
        s_id, s_g, s_const = t.sem("a_id"), t.sem("a_g"), t.sem("a_const")
        s_ln, s_lnready = t.sem("a_ln"), t.sem("a_lnready")
        s_w = [t.sem("a_w0"), t.sem("a_w1")]
        s_mask = [t.sem("a_mask0"), t.sem("a_mask1")]
        s_misc, s_copy, s_reduce, s_negmax = t.sem("a_misc"), t.sem("a_copy"), t.sem("a_reduce"), t.sem("a_negmax")
        s_sq, s_ss, s_nrm, s_hi, s_lo = t.sem("a_sq"), t.sem("a_ss"), t.sem("a_nrm"), t.sem("a_hi"), t.sem("a_lo")
        s_vhi, s_vlo, s_pool = t.sem("a_vhi"), t.sem("a_vlo"), t.sem("a_pool")
        s_scores, s_exp, s_prlo, s_pv = t.sem("a_scores"), t.sem("a_exp"), t.sem("a_prlo"), t.sem("a_pv")
        s_o = [t.sem("a_o0"), t.sem("a_o1")]
        s_store = [t.sem("a_store0"), t.sem("a_store1")]
        s_zero, s_clear = t.sem("a_zero"), t.sem("a_clear")
        s_bound = t.sem("a_bound")
        block = ctx.enter_context(nc.Block())

        def either(eng, body):
            eng.wait_ge(s_bound, 4)
            with eng.If(eng.value_load(bounded[0:1, 0:1], min_val=0, max_val=1) > 0):
                body(BOUNDED)
            with eng.Else():
                body(WITH_MAXIMA)

        @block.sync
        def _(sp):
            def load_ln(b):
                sp.dma_start(lnT_sb[:, :, :, :].bitcast(F32).unsqueeze(1),
                             lnT[bass.ds(b, 1)].rearrange("b p s c k -> p b s c k")).then_inc(s_ln, 16)

            def load_w(head, slot):
                sp.dma_start(w_sb[:, slot:slot + 1].bitcast(F32),
                             wHead[bass.ds(head, 1)].rearrange("h p s c n -> p h s c n")).then_inc(s_w[slot], 16)

            def load_mask(b, slot):
                sp.dma_start(mrow[0:1, slot, :].bitcast(F32), maskRow[bass.ds(b, 1), :]).then_inc(s_mask[slot], 16)
                sp.dma_start(mcol[:, slot:slot + 1], maskCol[:, bass.ds(b, 1)], allow_slow_non_contiguous=True).then_inc(s_mask[slot], 16)

            def store(head, q):
                sp.wait_ge(s_o[q], head + 1)
                sp.dma_start(attT[bass.ds(head, 1), :, q * 512:(q + 1) * 512].rearrange("h d n -> d h n"),
                             o_sb[:, q:q + 1, :]).then_inc(s_store[q], 16)

            load_ln(0)
            load_w(0, 0)
            load_w(1, 1)
            sp.wait_ge(s_ln, 16)
            sp.sem_inc(s_lnready, 1)

            def attend(plan):
                sp.wait_ge(s_copy, KT)
                load_w(2, 0)
                sp.wait_ge(s_const, 4)
                load_mask(0, 0)
                sp.wait_ge(s_copy, Window(plan, None, -1).copied("P8"))
                load_w(3, 1)

                def pair(v, b=None):
                    if b is not None:
                        sp.wait_ge(s_ln, b * 16 + 16)
                    sp.sem_inc(s_lnready, 1)
                    for s in range(2):
                        w = Window(plan, v, s)
                        mb, head = (v + s) // 8 % B, (v * 2 + s + 4) % H
                        sp.wait_ge(s_exp, w.count("unit"))
                        load_mask(mb, w.other)
                        if not w.first:
                            store(v * 2 + s - 1, 1)
                        sp.wait_ge(s_copy, w.copied("P8"))
                        load_w(head, w.slot)
                        store(v * 2 + s, 0)

                pair(0)
                with sp.Fori(1, 7) as v:
                    pair(v)
                with sp.Fori(1, B) as b:
                    load_ln(b)
                    with sp.Fori(0, 8) as k:
                        pair(b * 8 + k - 1, b)
                pair(HEADS // 2 - 1)
                store(HEADS - 1, 1)

            either(sp, attend)
            sp.wait_ge(s_clear, 16)
            for q in range(QB):
                sp.wait_ge(s_store[q], 16 * HEADS)
            for s in range(2):
                sp.wait_ge(s_w[s], 16 * (HEADS // 2 + 2))
                sp.wait_ge(s_mask[s], 32 * (HEADS // 2 + (s == 0)))

        @block.gpsimd
        def _(pool):
            g = nc.gpsimd
            pool.memset(ident[:, :], 0.0).then_inc(s_id, 1)
            pool.wait_ge(s_id, 1)
            pool.affine_select(out=ident[:, :], in_=ident[:, :], compare_op=ALU.not_equal, fill=1.0,
                               base=0, pattern=[[-1, P]], channel_multiplier=1).then_inc(s_id, 1)
            pool.memset(minus_half[:, :], -0.5).then_inc(s_pool, 1)
            pool.dma_start(gq[:, :], qn_g.rearrange("(a d) -> a d", a=1).broadcast_to([P, DH])).then_inc(s_g, 16)
            pool.dma_start(gk[:, :], kn_g.rearrange("(a d) -> a d", a=1).broadcast_to([P, DH])).then_inc(s_g, 16)
            pool.wait_ge(s_const, 5)

            def window(w):
                if w.turn:
                    pool.wait_ge(s_hi, w.count("split", 1, 2))
                    g.tensor_tensor(k_st[:, w.other, :, 0:DH], nrm[:, :, 1, :],
                                    k_st[:, w.other, :, DH:2 * DH].bitcast(F32), ALU.subtract).then_inc(s_lo, 1)
                    g.tensor_tensor(q_st[:, w.other, :, 2 * DH:3 * DH], nrm[:, 0:NT, 0, :],
                                    q_st[:, w.other, :, 0:DH].bitcast(F32), ALU.subtract).then_inc(s_lo, 1)
                    pool.wait_ge(s_vhi, w.count("split", 1))
                    g.tensor_tensor(vC[:, w.other, :, 0:DH], raw[:, w.other, :, 2 * DH:3 * DH],
                                    vA[:, w.other, :, 0:DH].bitcast(F32), ALU.subtract).then_inc(s_vlo, 1)
                pool.wait_ge(s_copy, w.copied("P8"))
                qk = raw[:, w.slot, :, 0:2 * DH]
                g.tensor_tensor(sq[:, :, :], qk, qk, ALU.mult).then_inc(s_sq, 1)
                pool.wait_ge(s_ss, w.count("proj", 1, 2))
                g.tensor_tensor(rs[:, :], ss[:, :], minus_half[:, :], ALU.pow).then_inc(s_pool, 1)
                pool.wait_ge(s_pool, w.count("proj", 0, 2) + 2)
                g.tensor_tensor(nrm[:, :, :, :], qk.rearrange("p t (j d) -> p t j d", d=DH),
                                rs[:, :].rearrange("p (t j) -> p t j", j=2).unsqueeze(3).broadcast_to([P, KT, 2, DH]),
                                ALU.mult).then_inc(s_pool, 1)
                pool.wait_ge(s_pool, w.count("proj", 0, 2) + 3)
                g.tensor_tensor(nrm[:, 0:NT, 0, :], nrm[:, 0:NT, 0, :],
                                gqk[:, :].unsqueeze(1).broadcast_to([P, NT, DH]), ALU.mult).then_inc(s_nrm, 1)

            either(pool, lambda plan: windows(pool, plan, window))

        @block.vector
        def _(dve):
            v = nc.vector
            v.memset(zero[:, :], 0.0).then_inc(s_zero, 1)
            v.memset(q_st[:, :, :, 3 * DH:3 * DH + 2].bitcast(F32), 0.0).then_inc(s_const, 1)
            v.memset(k_st[:, :, :, 2 * DH:2 * DH + 2].bitcast(F32), 1.0).then_inc(s_const, 1)
            v.memset(one_row[:, :].bitcast(F32), 0.0).then_inc(s_const, 1)
            v.memset(mrow[:, :, :].bitcast(F32), 0.0).then_inc(s_const, 1)
            dve.wait_ge(s_g, 32)
            dve.wait_ge(s_const, 4)
            v.scalar_tensor_tensor(gqk[:, :], gq[:, :], DH ** 0.5, gk[:, :], ALU.mult, ALU.mult).then_inc(s_const, 1)
            v.memset(one_row[0:1, :].bitcast(F32), 1.0).then_inc(s_const, 1)
            v.memset(vA[:, :, :, DH:2 * DH].bitcast(F32), 1.0).then_inc(s_const, 1)
            v.memset(vC[:, :, :, DH:2 * DH].bitcast(F32), 0.0).then_inc(s_const, 1)
            dve.wait_ge(s_const, 8)
            compared = [0]
            step(dve, s_bound, compared, v.tensor_tensor(gain2[:, :], gqk[:, :], gqk[:, :], ALU.mult))
            step(dve, s_bound, compared, v.tensor_reduce(most2[:, :], gain2[:, :], AX.X, ALU.max))
            step(dve, s_bound, compared, v.tensor_scalar(bounded_f[:, :], most2[:, :], MOST ** 2, None, ALU.is_le))
            step(dve, s_bound, compared, v.tensor_copy(bounded[:, :], bounded_f[:, :]))

            def negmax(w, half):
                a = slice(4 * half, 4 * half + 4)
                dve.wait_ge(s_reduce, w.taken("M71" if half else "M31")[1])
                v.tensor_reduce(q_st[:, w.other, a, 3 * DH], maxima[:, a, :], AX.X, ALU.min).then_inc(s_negmax, 1)

            def output(w, q, before=0):
                dve.wait_ge(s_pv, w.count("unit", KT * (q + 1) - before * UNITS))
                dve.wait_ge(s_store[q], w.count("one", -before, 16))
                v.tensor_copy(o_sb[:, q, :], ps_o[0:DH + 1, q, :]).then_inc(s_o[q], 1)

            def window(w):
                for u in range(UNITS):
                    for name, m in w.jobs(u):
                        if name not in w.plan.reduced:
                            continue
                        dve.wait_ge(s_misc, w.count("misc", m + 1))
                        j, bank = int(name[1]), ps_m[:, m % BANKS, :]
                        if name[0] == "M":
                            g = int(name[2])
                            v.tensor_reduce(maxima[:, j, g:g + 1], bank, AX.X, ALU.max, negate=True).then_inc(s_reduce, 1)
                        else:
                            v.tensor_reduce(maxima[:, 4 * j:4 * j + 4, 2], bank.rearrange("p (t k) -> p t k", k=P),
                                            AX.X, ALU.max, negate=True).then_inc(s_reduce, 1)
                        if name in ("M31", "M71"):
                            negmax(w, name == "M71")
                    if w.attend:
                        dve.wait_ge(s_exp, w.count("unit", u + 1))
                        v.tensor_tensor(pr_lo[:, u % RING, :], pr[:, u % RING, :], pr_hi[:, u % RING, :].bitcast(F32),
                                        ALU.subtract).then_inc(s_prlo, 1)
                    if u == w.plan.hi and w.turn:
                        dve.wait_ge(s_nrm, w.count("proj"))
                        v.tensor_copy(k_st[:, w.other, :, DH:2 * DH], nrm[:, :, 1, :]).then_inc(s_hi, 1)
                        v.tensor_copy(q_st[:, w.other, :, 0:2 * DH].rearrange("p t (j d) -> p t j d", d=DH),
                                      nrm[:, 0:NT, 0, :].unsqueeze(2).broadcast_to([P, NT, 2, DH])).then_inc(s_hi, 1)
                    if u == w.plan.values and w.turn:
                        if w.attend:
                            dve.wait_ge(s_pv, w.count("unit"))
                        dve.wait_ge(s_copy, w.count("copy"))
                        v.tensor_copy(vA[:, w.other, :, 0:DH], raw[:, w.other, :, 2 * DH:3 * DH]).then_inc(s_vhi, 1)
                    if u == w.plan.squares:
                        dve.wait_ge(s_sq, w.count("proj", 1))
                        v.tensor_reduce(ss[:, :], sq[:, :, :].rearrange("p t (j d) -> p (t j) d", d=DH),
                                        AX.X, ALU.add).then_inc(s_ss, 1)
                        dve.wait_ge(s_ss, w.count("proj", 0, 2) + 1)
                        v.tensor_scalar(ss[:, :], ss[:, :], DH * RMS_EPS ** 2, None, ALU.max).then_inc(s_ss, 1)
                    if u == LAG and w.attend and not w.first:
                        output(w, 1, 1)
                    if u == KT + LAG and w.attend:
                        output(w, 0)

            either(dve, lambda plan: windows(dve, plan, window, lambda w: output(w, 1, 1)))

        @block.scalar
        def _(act):
            def window(w):
                for u in range(UNITS):
                    if w.attend:
                        q, k = u // KT, u % KT
                        act.wait_ge(s_scores, w.count("unit", u + 1))
                        if k == KT - 1:
                            if q == 0:
                                act.wait_ge(s_mask[w.slot], w.v * 32 + 32)
                            bias = mcol[:, w.slot:w.slot + 1]
                        else:
                            bias = 0.0
                        act.activation(pr[:, u % RING, :], ps_s[:, u % RING, :], ACT.Exp, bias=bias)
                        act.activation(pr_hi[:, u % RING, :], ps_s[:, u % RING, :], ACT.Exp, bias=bias).then_inc(s_exp, 1)
                    for name, m in w.jobs(u):
                        if name in w.plan.reduced:
                            continue
                        act.wait_ge(s_misc, w.count("misc", m + 1))
                        src = ps_m[:, m % BANKS, :]
                        if name[0] == "P":
                            if name == "P0" and w.attend:
                                act.wait_ge(s_vlo, w.count("split"))
                                act.wait_ge(s_nrm, w.count("proj"))
                            ins = act.activation(raw[:, w.slot, int(name[1]), :], src[:, 0:3 * DH], ACT.Copy)
                        elif name == "KK":
                            act.activation(kT1[:, w.other, N:KEYS], src[:, 0:P], ACT.Copy)
                            ins = act.activation(kT2[0:DH + 1, w.other, N:KEYS], src[0:DH + 1, P:2 * P], ACT.Copy)
                        else:
                            rows, dst = {"K1": (P, kT1), "K2": (DH + 1, kT2), "Q1": (P, qT1), "Q2": (DH + 1, qT2)}[name[:2]]
                            g = int(name[2])
                            ins = act.activation(dst[0:rows, w.other, 512 * g:512 * g + 512], src[0:rows, :], ACT.Copy)
                        ins.then_inc(s_copy, 1)

            act.wait_ge(s_zero, 1)
            act.dma_start(routed.rearrange("(t p) d -> p t d", p=P),
                          zero[:, :].unsqueeze(1).broadcast_to([P, ROWS // P, D])).then_inc(s_clear, 16)
            either(act, lambda plan: windows(act, plan, window))

        @block.tensor
        def _(pe):
            mm = nc.tensor.matmul
            pe.wait_ge(s_id, 2)
            pe.wait_ge(s_const, 8)

            def project(w, tile, out):
                for k, (a, b, c) in enumerate((a, b, c) for a, b in ((0, 0), (0, 1), (1, 0)) for c in range(C)):
                    ins = mm(out[:, 0:3 * DH], lnT_sb[:, a, c, tile * P:(tile + 1) * P], w_sb[:, w.slot, b, c, :],
                             start=k == 0, stop=k == 3 * C - 1)
                return ins

            def values(w, u):
                slot = w.slot if u >= 0 else w.other
                q, k, r = u % UNITS // KT, u % KT, u % RING
                if k == 0:
                    pe.wait_ge(s_o[q], w.count("one"))
                pe.wait_ge(s_prlo, w.count("unit", u + 1))
                last = k == KT - 1
                mm(ps_o[:, q, :], vA[:, slot, k, :], pr_hi[:, r, :], start=k == 0, stop=False)
                mm(ps_o[:, q, :], vC[:, slot, k, :], pr_hi[:, r, :], start=False, stop=False)
                mm(ps_o[:, q, :], vA[:, slot, k, :], pr_lo[:, r, :], start=False, stop=last).then_inc(s_pv, 1)

            def transposes(w, out, src, tiles, lo, n_):
                for i, tile in enumerate(tiles):
                    ins = nc.tensor.transpose(out[0:n_, i * P:(i + 1) * P],
                                              src[:, w.other, tile, lo:lo + n_].bitcast(F32), ident[:, :])
                return ins

            def job(w, name, m):
                out = ps_m[:, m % BANKS, :]
                if w.freed(m):
                    kind, value = w.freed(m)
                    pe.wait_ge({"copy": s_copy, "reduce": s_reduce}[kind], value)
                if name[0] == "P":
                    if name == "P0":
                        if w.attend:
                            pe.wait_ge(s_lnready, w.v + 2)
                            pe.wait_ge(s_w[w.slot], w.v * 16 + 32)
                        else:
                            pe.wait_ge(s_lnready, 1)
                            pe.wait_ge(s_w[w.slot], 16)
                    ins = project(w, int(name[1]), out)
                elif name[0] == "M":
                    j, g = int(name[1]), int(name[2])
                    if name in ("M00", "M40"):
                        pe.wait_ge(s_copy, w.copied("Q10" if j == 0 else "Q11"))
                    ins = mm(out, qT1[:, w.other, j * P:(j + 1) * P], kT1[:, w.other, 512 * g:512 * g + 512],
                             start=True, stop=True)
                elif name[0] == "C":
                    j = int(name[1])
                    if j == 0:
                        if w.attend:
                            pe.wait_ge(s_mask[w.other], w.v * 32 + (32 if w.s == 0 else 64))
                        else:
                            pe.wait_ge(s_mask[w.other], 32)
                    pe.wait_ge(s_copy, w.copied("Q1%d" % j))
                    for i in range(4):
                        mm(out[:, i * P:(i + 1) * P], qT1[:, w.other, (4 * j + i) * P:(4 * j + i + 1) * P],
                           kT1[:, w.other, N:KEYS], start=True, stop=False)
                        ins = mm(out[:, i * P:(i + 1) * P], one_row[:, :], mrow[:, w.other, :], start=False, stop=True)
                elif name == "KK":
                    transposes(w, out, k_st, [KT - 1], 0, 2 * DH)
                    ins = transposes(w, out[:, P:2 * P], k_st, [KT - 1], DH, DH + 1)
                else:
                    g = int(name[2])
                    tiles = range(4 * g, 4 * g + 4)
                    if name in ("K10", "Q10"):
                        pe.wait_ge(s_lo, w.count("split", 1, 2) - (name == "K10"))
                    if name[:2] == "Q2" and w.plan.reduced:
                        pe.wait_ge(s_negmax, w.count("split", 0, 2) + g + 1)
                    src, lo, n_ = {"K1": (k_st, 0, 2 * DH), "K2": (k_st, DH, DH + 1),
                                   "Q1": (q_st, 0, 2 * DH), "Q2": (q_st, 2 * DH, DH + 1)}[name[:2]]
                    ins = transposes(w, out, src, tiles, lo, n_)
                ins.then_inc(s_misc, 1)

            def window(w):
                for u in range(UNITS):
                    if w.attend:
                        q, k = u // KT, u % KT
                        if u == 0:
                            pe.wait_ge(s_copy, w.count("copy"))
                            pe.wait_ge(s_vlo, w.count("split"))
                        mm(ps_s[:, u % RING, :], kT1[:, w.slot, k * P:(k + 1) * P],
                           qT1[:, w.slot, q * 512:(q + 1) * 512], start=True, stop=False)
                        mm(ps_s[:, u % RING, :], kT2[0:DH + 1, w.slot, k * P:(k + 1) * P],
                           qT2[0:DH + 1, w.slot, q * 512:(q + 1) * 512], start=False, stop=True).then_inc(s_scores, 1)
                    here = w.jobs(u)
                    for name, m in here[:1]:
                        job(w, name, m)
                    if w.attend and (u >= LAG or not w.first):
                        values(w, u - LAG)
                    for name, m in here[1:]:
                        job(w, name, m)

            def last(w):
                for u in range(LAG):
                    values(w, u - LAG)

            either(pe, lambda plan: windows(pe, plan, window, last))


def project_out(nc, x, Wout, bout, Wr, attT, rden, tokens, x2, logit):
    HP, G = H // 2, 4
    W = GT * P
    with ExitStack() as ctx:
        t = Tools(nc, ctx)
        dn = t.sb("dn", [HEADS, N])
        wo = t.sb("wo", [P, HP, D])
        wo_hi = t.sb("wo_hi", [P, HP, D], F32R)
        wo_lo = t.sb("wo_lo", [P, HP, D], F32R)
        bo = t.sb("bo", [P, D])
        a = t.sb("a", [P, 2, HP, W])
        rb = t.sb("rb", [P, 2, HP, W])
        a_hi = t.sb("a_hi", [P, 2, HP, W], F32R)
        a_lo = t.sb("a_lo", [P, 2, HP, W], F32R)
        xg = t.sb("xg", [P, G, GT, D])
        stats = t.sb("o_stats", [P, GT, 6])
        mv = t.sb("o_mv", [P, GT, 2])
        var_eps = t.sb("o_var", [P, GT])
        rstd = t.sb("o_rstd", [P, GT])
        half = t.sb("o_half", [P, GT])
        marker = t.sb("marker", [P, 1])
        ident = t.sb("o_ident", [P, P])
        wr = t.sb("wr", [P, C, E])
        l2 = t.sb("l2", [P, G, GT, D])
        l2T = t.sb("l2T", [P, 2, GT, C, P])
        ps_y = t.ps("ps_y", [P, G, GT, D])
        ps_t = t.ps("o_ps_t", [P, 2, GT, C, P])
        ps_l = t.ps("o_ps_l", [P, 512])
        s_dn, s_rd, s_w, s_whi, s_wlo, s_bo, s_half = (t.sem("o_" + n) for n in ("dn", "rd", "w", "whi", "wlo", "bo", "half"))
        s_prod, s_xb = t.sem("o_prod"), t.sem("o_xb")
        s_a, s_x, s_st = ([t.sem("o_%s_%d" % (n, q)) for q in range(G)] for n in ("a", "x", "st"))
        s_y, s_l2, s_lov, s_lop, s_id, s_wr, s_t, s_tc, s_lg = (t.sem("o_" + n) for n in (
            "y", "l2", "lov", "lop", "id", "wr", "t", "tc", "lg"))
        s_hi, s_x2, s_v, s_ve, s_rs = (t.sem("o_" + n) for n in ("hi", "x2", "v", "ve", "rs"))
        block = ctx.enter_context(nc.Block())
        att_v = attT.rearrange("(b k r) d n -> b r d k n", b=B, r=2)
        rden_v = rden.rearrange("(b k r) n -> b r k n", b=B, r=2)
        x_v = x.rearrange("b (g t p) d -> (b g) p t d", t=GT, p=P)
        tokens_v = tokens.rearrange("(g t p) d -> g p t d", t=GT, p=P)
        HH = HP // 2

        def free(eng, sem, count):
            if not isinstance(count, int) or count > 0:
                eng.wait_ge(sem, count)

        def earlier(b, q, k):
            if q >= k:
                return b, q - k
            return None if isinstance(b, int) and b == 0 else (b - 1, q - k + G)

        def batches(eng, batch):
            batch(0)
            with eng.Fori(1, B) as b:
                batch(b)

        def ahead(eng, batch):
            batch(0)
            with eng.Fori(1, B - 1) as b:
                batch(b)
            batch(B - 1, last=True)

        @block.sync
        def _(sp):
            sp.dma_start(dn[:, :], attT[:, DH, :]).then_inc(s_dn, 16)
            sp.dma_start(wo[:, :, :], Wout.rearrange("(k p) n -> p k n", p=P)).then_inc(s_w, 16)
            sp.wait_ge(s_rd, 1)
            sp.dma_start(rden, dn[:, :]).then_inc(s_dn, 16)
            sp.wait_ge(s_dn, 32)
            def batch(b):
                for q in range(G):
                    free(sp, s_lov, b * G + q - 1)
                    free(sp, s_lop, b * G + q - 1)
                    cols = slice(W * q, W * q + W)
                    for r in range(2):
                        p = slice(DH * r, DH * r + DH)
                        sp.dma_start(a[p, q % 2:q % 2 + 1], att_v[bass.ds(b, 1), r, 0:DH, :, cols]
                                     .rearrange("b d k n -> d b k n")).then_inc(s_a[q], 16)
                        sp.dma_start(rb[p, q % 2:q % 2 + 1], rden_v[bass.ds(b, 1), r, :, cols]
                                     .unsqueeze(0).broadcast_to([DH, 1, HP, W])).then_inc(s_a[q], 16)
                    free(sp, s_l2, b * G + q - 3)
                    sp.dma_start(xg[:, q:q + 1], x_v[bass.ds(b * G + q, 1)]
                                 .rearrange("g p t d -> p g t d")).then_inc(s_x[q], 16)

            batches(sp, batch)

        @block.gpsimd
        def _(pool):
            pool.dma_start(bo[:, :], bout.rearrange("(a d) -> a d", a=1).broadcast_to([P, D])).then_inc(s_bo, 16)
            pool.memset(half[:, :], -0.5).then_inc(s_half, 1)
            pool.dma_start(wr[:, :, :], Wr.rearrange("(c p) e -> p c e", p=P)).then_inc(s_wr, 16)
            pool.memset(ident[:, :], 0.0).then_inc(s_id, 1)
            pool.wait_ge(s_id, 1)
            pool.affine_select(out=ident[:, :], in_=ident[:, :], compare_op=ALU.not_equal, fill=1.0,
                               base=0, pattern=[[-1, P]], channel_multiplier=1).then_inc(s_id, 1)
            pool.wait_ge(s_half, 1)
            pool.wait_ge(s_bo, 16)

            def lower(b, q):
                pool.wait_ge(s_hi, b * (2 * G) + 2 * q + 2)
                nc.gpsimd.tensor_tensor(a_lo[:, q % 2, HH:, :], a[:, q % 2, HH:, :],
                                        a_hi[:, q % 2, HH:, :].bitcast(F32), ALU.subtract).then_inc(s_lop, 1)

            lower(0, 0)

            def batch(b, last=False):
                for q in range(G):
                    pool.wait_ge(s_x[q], b * 16 + 16)
                    nc.gpsimd.tensor_tensor(xg[:, q], xg[:, q], bo[:, :].unsqueeze(1).broadcast_to([P, GT, D]),
                                            ALU.add).then_inc(s_xb, 1)
                    if q + 1 < G:
                        lower(b, q + 1)
                    elif not last:
                        lower(b + 1, 0)
                    pool.wait_ge(s_ve, b * G + q + 1)
                    nc.gpsimd.tensor_tensor(rstd[:, :], var_eps[:, :], half[:, :], ALU.pow).then_inc(s_rs, 1)
                    pool.wait_ge(s_l2, b * G + q + 1)
                    pool.dma_start(tokens_v[bass.ds(b * G + q, 1)].rearrange("g p t d -> p g t d"),
                                   l2[:, q:q + 1]).then_inc(s_st[q], 16)

            ahead(pool, batch)
            for q in range(G):
                pool.wait_ge(s_st[q], 16 * B)

        @block.scalar
        def _(act):
            act.wait_ge(s_w, 16)
            act.activation(wo_hi[:, :, :], wo[:, :, :], ACT.Copy).then_inc(s_whi, 1)
            def batch(b):
                for q in range(G):
                    free(act, s_y, b * G + q - 1)
                    for k in range(2):
                        act.wait_ge(s_prod, b * (2 * G) + 2 * q + k + 1)
                        h = slice(HH * k, HH * k + HH)
                        act.activation(a_hi[:, q % 2, h, :], a[:, q % 2, h, :], ACT.Copy).then_inc(s_hi, 1)
                    if earlier(b, q, 2):
                        transposed(*earlier(b, q, 2))

            def transposed(b, q):
                act.wait_ge(s_t, b * G + q + 1)
                free(act, s_lg, b * G + q - 1)
                act.activation(l2T[:, q % 2], ps_t[:, q % 2], ACT.Copy).then_inc(s_tc, 1)

            batches(act, batch)
            transposed(B - 1, G - 2)
            transposed(B - 1, G - 1)
            act.wait_ge(s_lg, B * G)
            act.activation(logit[:, :, :], ps_l[:, 0:TT * E].rearrange("p (t e) -> p t e", e=E), ACT.Copy)

        @block.vector
        def _(dve):
            v = nc.vector
            dve.wait_ge(s_dn, 16)
            v.reciprocal(dn[:, :], dn[:, :]).then_inc(s_rd, 1)
            dve.wait_ge(s_whi, 1)
            v.tensor_tensor(wo_lo[:, :, :], wo[:, :, :], wo_hi[:, :, :].bitcast(F32), ALU.subtract).then_inc(s_wlo, 1)

            def product(b, q):
                dve.wait_ge(s_a[q], b * 64 + 64)
                for k in range(2):
                    h = slice(HH * k, HH * k + HH)
                    v.tensor_tensor(a[:, q % 2, h, :], a[:, q % 2, h, :], rb[:, q % 2, h, :], ALU.mult).then_inc(s_prod, 1)
                dve.wait_ge(s_hi, b * (2 * G) + 2 * q + 1)
                v.tensor_tensor(a_lo[:, q % 2, 0:HH, :], a[:, q % 2, 0:HH, :], a_hi[:, q % 2, 0:HH, :].bitcast(F32),
                                ALU.subtract).then_inc(s_lov, 1)

            product(0, 0)

            def batch(b, last=False):
                for q in range(G):
                    if q + 1 < G:
                        product(b, q + 1)
                    elif not last:
                        product(b + 1, 0)
                    dve.wait_ge(s_xb, b * G + q + 1)
                    group = b * G + q
                    dve.wait_ge(s_y, group + 1)
                    v.tensor_tensor(x2[:, bass.ds(group * GT, GT), :], ps_y[:, q], xg[:, q], ALU.add).then_inc(s_x2, 1)
                    dve.wait_ge(s_x2, group * (1 + GT) + 1)
                    v.memset(marker[:, :], 0.0)
                    for i in range(GT):
                        v.bn_stats(stats[:, i, :], x2[:, bass.ds(group * GT + i, 1), :].rearrange("p a d -> p (a d)")).then_inc(s_x2, 1)
                    dve.wait_ge(s_x2, group * (1 + GT) + 1 + GT)
                    v.memset(marker[:, :], 0.0)
                    for i in range(GT):
                        ins = v.bn_aggr(mv[:, i, :], stats[:, i, :])
                    ins.then_inc(s_v, 1)
                    dve.wait_ge(s_v, group + 1)
                    v.tensor_scalar(var_eps[:, :], mv[:, :, 1], LN_EPS, None, ALU.add).then_inc(s_ve, 1)
                    dve.wait_ge(s_rs, group + 1)
                    free(dve, s_st[q], b * 16)
                    free(dve, s_t, group - 3)
                    for i in range(GT):
                        tile = bass.ds(group * GT + i, 1)
                        ins = v.tensor_scalar(l2[:, q, i:i + 1, :], x2[:, tile, :], mv[:, i, 0:1], rstd[:, i:i + 1],
                                              ALU.subtract, ALU.mult)
                    ins.then_inc(s_l2, 1)

            ahead(dve, batch)

        @block.tensor
        def _(pe):
            def product(b, q):
                pe.wait_ge(s_lov, b * G + q + 1)
                pe.wait_ge(s_lop, b * G + q + 1)
                free(pe, s_l2, b * G + q - 3)
                for i in range(GT):
                    n = 0
                    for k in range(HP):
                        for lhs, rhs in ((a_hi, wo_hi), (a_hi, wo_lo), (a_lo, wo_hi)):
                            ins = nc.tensor.matmul(ps_y[:, q, i, :], lhs[:, q % 2, k, i * P:(i + 1) * P],
                                                   rhs[:, k, :], start=n == 0, stop=n == 3 * HP - 1)
                            n += 1
                ins.then_inc(s_y, 1)

            def transpose(b, q):
                pe.wait_ge(s_l2, b * G + q + 1)
                free(pe, s_tc, b * G + q - 1)
                for i in range(GT):
                    for c in range(C):
                        ins = nc.tensor.transpose(ps_t[:, q % 2, i, c, :], l2[:, q, i, c * P:(c + 1) * P], ident[:, :])
                ins.then_inc(s_t, 1)

            def logits(b, q):
                pe.wait_ge(s_tc, b * G + q + 1)
                for i in range(GT):
                    for c in range(C):
                        ins = nc.tensor.matmul(ps_l[:, bass.ds((b * G + q) * (GT * E) + i * E, E)], l2T[:, q % 2, i, c, :],
                                               wr[:, c, :], start=c == 0, stop=c == C - 1)
                ins.then_inc(s_lg, 1)

            def batch(b):
                for q in range(G):
                    product(b, q)
                    if earlier(b, q, 1):
                        transpose(*earlier(b, q, 1))
                    if earlier(b, q, 2):
                        logits(*earlier(b, q, 2))

            pe.wait_ge(s_wlo, 1)
            pe.wait_ge(s_id, 2)
            pe.wait_ge(s_wr, 16)
            batches(pe, batch)
            transpose(B - 1, G - 1)
            logits(B - 1, G - 2)
            logits(B - 1, G - 1)


def route(nc, logit, slots, gates, expert):
    with ExitStack() as ctx:
        t = Tools(nc, ctx)
        before = t.sb("before", [P, P])
        ones = t.sb("ones", [P, P])
        eight = t.sb("eight", [P, TT, E])
        tiles = t.sb("tiles", [P, ROUTED + 2, E])
        top = t.sb("top", [P, TT])
        prob = t.sb("prob", [P, TT, E])
        total = t.sb("total", [P, TT])
        best = t.sb("best", [P, TT, 8])
        index = t.sb("index", [P, TT, 8], U32)
        index_f = t.sb("index_f", [P, TT, 2])
        hot = t.sb("hot", [P, 2, TT, E])
        both = t.sb("both", [P, TT, E])
        cum = t.sb("cum", [P, 2, TT, E])
        base = t.sb("base", [P, TT, E])
        filled = t.sb("filled", [P, E])
        filled_i = t.sb("filled_i", [P, E], I32)
        end = t.sb("end", [P, E])
        start = t.sb("start", [P, E])
        pick = t.sb("pick", [P, 2, TT, E])
        slot_f = t.sb("slot_f", [P, 2, TT])
        reached = t.sb("reached", [P, ROUTED + 2, E])
        expert_f = t.sb("expert_f", [P, ROUTED + 2])
        ps_c = t.ps("r_ps_c", [P, 2, 512])
        s_c, s_v, s_e, s_cnt = (t.sem("r_" + n) for n in ("c", "v", "e", "cnt"))
        s_in = t.sem("r_in")
        block = ctx.enter_context(nc.Block())

        @block.gpsimd
        def _(pool):
            pool.memset(before[:, :], 1.0).then_inc(s_c, 1)
            pool.memset(ones[:, :], 1.0).then_inc(s_c, 1)
            pool.iota(eight[:, :, :], pattern=[[0, TT], [1, E]], base=0, channel_multiplier=0,
                      allow_small_or_imprecise_dtypes=True).then_inc(s_c, 1)
            pool.iota(tiles[:, :, :], pattern=[[1, ROUTED + 2], [0, E]], base=0, channel_multiplier=0,
                      allow_small_or_imprecise_dtypes=True).then_inc(s_c, 1)
            pool.wait_ge(s_c, 4)
            pool.affine_select(out=before[:, :], in_=before[:, :], compare_op=ALU.is_gt, fill=0.0,
                               base=0, pattern=[[1, P]], channel_multiplier=-1).then_inc(s_c, 1)

        @block.tensor
        def _(pe):
            pe.wait_ge(s_c, 5)
            pe.wait_ge(s_cnt, 1)
            nc.tensor.matmul(ps_c[:, 0, 0:TT * E], before[:, :], both[:, :, :], start=True, stop=True)
            nc.tensor.matmul(ps_c[:, 1, 0:TT * E], ones[:, :], both[:, :, :], start=True, stop=True).then_inc(s_cnt, 1)

        @block.scalar
        def _(act):
            act.wait_ge(s_in, 1)
            act.activation(prob[:, :, :], logit[:, :, :], ACT.Exp).then_inc(s_e, 1)

        @block.vector
        def _(dve):
            v = nc.vector
            n = [0]

            def do(ins):
                step(dve, s_v, n, ins)

            tb = lambda ap: ap.unsqueeze(2).broadcast_to([P, TT, E])
            do(v.tensor_reduce(top[:, :], logit[:, :, :], AX.X, ALU.max))
            v.tensor_tensor(logit[:, :, :], logit[:, :, :], tb(top[:, :]), ALU.subtract).then_inc(s_in, 1)
            dve.wait_ge(s_e, 1)
            do(v.tensor_reduce(total[:, :], prob[:, :, :], AX.X, ALU.add))
            do(v.reciprocal(total[:, :], total[:, :]))
            do(v.tensor_tensor(prob[:, :, :], prob[:, :, :], tb(total[:, :]), ALU.mult))
            for i in range(TT):
                v.max(best[:, i, :], prob[:, i, :]).then_inc(s_v, 1)
            n[0] += TT
            dve.wait_ge(s_v, n[0])
            for i in range(TT):
                v.max_index(index[:, i, :], best[:, i, :], prob[:, i, :]).then_inc(s_v, 1)
            n[0] += TT
            dve.wait_ge(s_v, n[0])
            do(v.tensor_tensor(total[:, :], best[:, :, 0], best[:, :, 1], ALU.add))
            do(v.reciprocal(total[:, :], total[:, :]))
            do(v.tensor_tensor(gates[:, :, :], best[:, :, 0:2], total[:, :].unsqueeze(2).broadcast_to([P, TT, 2]), ALU.mult))
            do(v.tensor_copy(index_f[:, :, :], index[:, :, 0:2]))
            dve.wait_ge(s_c, 5)
            for k in range(2):
                do(v.tensor_tensor(hot[:, k], eight[:, :, :], tb(index_f[:, :, k]), ALU.is_equal))
            v.tensor_tensor(both[:, :, :], hot[:, 0], hot[:, 1], ALU.add).then_inc(s_cnt, 1)
            dve.wait_ge(s_cnt, 2)
            do(v.tensor_copy(cum[:, 0], ps_c[:, 1, 0:TT * E].rearrange("p (t e) -> p t e", e=E)))
            k, s = 0, 1
            while s < TT:
                do(v.tensor_copy(cum[:, 1 - k, 0:s, :], cum[:, k, 0:s, :]))
                do(v.tensor_tensor(cum[:, 1 - k, s:, :], cum[:, k, s:, :], cum[:, k, 0:TT - s, :], ALU.add))
                k, s = 1 - k, 2 * s
            do(v.tensor_scalar(filled[:, :], cum[:, k, TT - 1, :], float(TS - 1), None, ALU.add))
            do(v.tensor_copy(filled_i[:, :], filled[:, :]))
            do(v.tensor_scalar(filled_i[:, :], filled_i[:, :], TS.bit_length() - 1, None, ALU.logical_shift_right))
            do(v.tensor_copy(filled[:, :], filled_i[:, :]))
            do(v.tensor_copy(end[:, 0:1], filled[:, 0:1]))
            for e in range(1, E):
                do(v.tensor_tensor(end[:, e:e + 1], end[:, e - 1:e], filled[:, e:e + 1], ALU.add))
            do(v.tensor_tensor(start[:, :], end[:, :], filled[:, :], ALU.subtract))
            do(v.tensor_scalar(start[:, :], start[:, :], float(TS), None, ALU.mult))
            do(v.tensor_tensor(base[:, :, :], ps_c[:, 0, 0:TT * E].rearrange("p (t e) -> p t e", e=E),
                               start[:, :].unsqueeze(1).broadcast_to([P, TT, E]), ALU.add))
            do(v.tensor_tensor(base[:, 1:, :], base[:, 1:, :], cum[:, k, 0:TT - 1, :], ALU.add))
            for j in range(2):
                do(v.tensor_tensor(pick[:, j], hot[:, j], base[:, :, :], ALU.mult))
            do(v.tensor_reduce(slot_f[:, :, :], pick[:, :, :, :], AX.X, ALU.add))
            do(v.tensor_copy(slots[:, :, :], slot_f[:, :, :]))
            do(v.tensor_tensor(reached[:, :, :], tiles[:, :, :], end[:, :].unsqueeze(1).broadcast_to([P, ROUTED + 2, E]), ALU.is_ge))
            do(v.tensor_reduce(expert_f[:, :], reached[:, :, :], AX.X, ALU.add))
            do(v.tensor_scalar(expert_f[:, :], expert_f[:, :], float(E - 1), None, ALU.min))
            do(v.tensor_copy(expert[:, :], expert_f[:, :]))


def experts(nc, weights_s, weights, expert, slots, tokens, routed, x2, ys):
    Wfc, bfc, Wproj, bproj = weights
    with ExitStack() as ctx:
        t = Tools(nc, ctx)
        ident = t.sb("f_ident", [P, P])
        moved = t.sb("moved", [P, 4, D])
        xt = t.sb("xt", [P, 2, 2, D])
        xT_hi = t.sb("xT_hi", [P, 2, C, TS], F32R)
        xT_lo = t.sb("xT_lo", [P, 2, C, TS], F32R)
        w1 = t.sb("w1", [P, 2, C, HID])
        w2 = t.sb("w2", [P, 2, HC, D])
        b1 = t.sb("b1", [P, 2, HC])
        b2 = t.sb("b2", [P, 2, D])
        w1_hi = t.sb("w1_hi", [P, 2, C, HC, P], F32R)
        w1_lo = t.sb("w1_lo", [P, 2, C, HC, P], F32R)
        w2_hi = t.sb("w2_hi", [P, 2, HC, D], F32R)
        w2_lo = t.sb("w2_lo", [P, 2, HC, D], F32R)
        b1_use = t.sb("b1_use", [P, 2, HC])
        b2_use = t.sb("b2_use", [P, 2, D])
        ht = t.sb("ht", [P, 4, 2, TS])
        h_hi = t.sb("h_hi", [P, 2, HC, TS], F32R)
        h_lo = t.sb("h_lo", [P, 2, HC, TS], F32R)
        y = t.sb("y", [P, 2, 2, D])
        ps_t = t.ps("f_ps_t", [P, C, TS])
        ps_h = t.ps("f_ps_h", [P, 4, 2, TS])
        ps_y = t.ps("f_ps_y", [P, 2, 512])
        s_id = t.sem("f_id")
        s_xl, s_raw1, s_raw2, s_ys = ([t.sem("f_%s_%d" % (n, i)) for i in range(2)] for n in ("xl", "raw1", "raw2", "ys"))
        s_w1h, s_w1l, s_b1, s_w2h, s_w2l, s_b2 = (t.sem("f_" + n) for n in ("w1h", "w1l", "b1", "w2h", "w2l", "b2"))
        s_xt, s_xh, s_xlo, s_h, s_y, s_yv = (t.sem("f_" + n) for n in ("xt", "xh", "xlo", "h", "y", "yv"))
        s_g, s_hh, s_hl = ([t.sem("f_%s_%d" % (n, i)) for i in range(4)] for n in ("g", "hh", "hl"))
        s_mv, s_sc = ([t.sem("f_%s_%d" % (n, i)) for i in range(4)] for n in ("mv", "sc"))
        block = ctx.enter_context(nc.Block())
        tokens_v = tokens.rearrange("(t r p) d -> t p r d", r=2, p=P)
        routed_v = routed.rearrange("(t r p) d -> t p r d", r=2, p=P)
        ys_v = ys.rearrange("(t r p) d -> t p r d", r=2, p=P)
        S2, LAST = SHARED // 2, (SHARED + ROUTED) // 2 - 1

        def loops(eng, step, first=0):
            def pair(U, shared, left=9):
                for s in range(2):
                    step(U, s, shared, left - s)

            pair(0, True)
            with eng.Fori(1, S2 - 1) as u:
                pair(u, True)
            pair(S2 - 1, True)
            for u in range(first):
                pair(S2 + u, False)
            with eng.Fori(S2 + first, LAST) as u:
                pair(u, False)
            pair(LAST, False, 1)

        def slot_of(U, s, shared, ahead):
            m = U * 2 + (s + ahead)
            if shared and not (isinstance(U, int) and m >= SHARED):
                return 1, 1
            return (s + ahead) % 2, m - (SHARED - 2)

        def last_shared(U, s):
            return isinstance(U, int) and U * 2 + s == SHARED - 1

        @block.sync
        def _(sp):
            def load1(slot, e):
                if e is None:
                    f, bf = weights_s[:2]
                    sp.dma_start(w1[:, slot], f.rearrange("(c p) n -> p c n", p=P)).then_inc(s_raw1[slot], 16)
                    sp.dma_start(b1[:, slot], bf.rearrange("(p c) -> p c", c=HC)).then_inc(s_raw1[slot], 16)
                else:
                    sp.dma_start(w1[:, slot:slot + 1], Wfc[bass.ds(e, 1)].rearrange("e (c p) n -> p e c n", p=P)).then_inc(s_raw1[slot], 16)
                    sp.dma_start(b1[:, slot:slot + 1], bfc[bass.ds(e, 1)].rearrange("e (p c) -> p e c", c=HC)).then_inc(s_raw1[slot], 16)

            def load2(slot, e):
                if e is None:
                    pr, bp = weights_s[2:]
                    sp.dma_start(w2[:, slot], pr.rearrange("(p c) n -> p c n", c=HC)).then_inc(s_raw2[slot], 16)
                    sp.dma_start(b2[:, slot], bp.rearrange("(a n) -> a n", a=1).broadcast_to([P, D])).then_inc(s_raw2[slot], 16)
                else:
                    sp.dma_start(w2[:, slot:slot + 1], Wproj[bass.ds(e, 1)].rearrange("e (p c) n -> p e c n", c=HC)).then_inc(s_raw2[slot], 16)
                    sp.dma_start(b2[:, slot], bproj[bass.ds(e, 1)].broadcast_to([P, D])).then_inc(s_raw2[slot], 16)

            def expert_of(j):
                return sp.value_load(expert[0:1, bass.ds(j, 1)], min_val=0, max_val=E - 1)

            def split1(n):
                sp.wait_ge(s_w1h, n)
                sp.wait_ge(s_w1l, n)
                sp.wait_ge(s_b1, n)

            def split2(n):
                sp.wait_ge(s_w2h, n)
                sp.wait_ge(s_w2l, n)
                sp.wait_ge(s_b2, n)

            def load_x(src, tile, parity):
                sp.dma_start(xt[:, parity:parity + 1], src[bass.ds(tile, 1)].rearrange("t p r d -> p t r d")).then_inc(s_xl[parity], 16)

            load1(1, None)
            load_x(tokens_v, 0, 0)
            load_x(tokens_v, 1, 1)
            load2(1, None)
            e0, e1, e2 = expert_of(0), expert_of(1), expert_of(2)
            load1(0, e0)
            load2(0, e0)
            split1(1)
            load1(1, e1)
            split2(1)
            load2(1, e1)
            split1(2)
            load1(0, e2)

            def step(U, s, shared, left):
                m = U * 2 + s
                if left >= 2:
                    sp.wait_ge(s_xt, m + 1)
                    if shared and isinstance(U, int) and m + 2 >= SHARED:
                        if s == 0:
                            for i in range(4):
                                sp.wait_ge(s_sc[i], 16 * 2 * TT // 4)
                        load_x(routed_v, m + 2 - SHARED, s)
                    elif shared:
                        load_x(tokens_v, m + 2, s)
                    else:
                        load_x(routed_v, m + (2 - SHARED), s)
                if not shared and left >= 2:
                    e = expert_of(m + (2 - SHARED))
                    split2(m - (SHARED - 2))
                    load2(s, e)
                    if left >= 3:
                        e = expert_of(m + (3 - SHARED))
                        split1(m - (SHARED - 3))
                        load1(1 - s, e)
                if not shared:
                    sp.wait_ge(s_yv, m + 1)
                    sp.dma_start(ys_v[bass.ds(m - SHARED, 1)].rearrange("t p r d -> p t r d"), y[:, s:s + 1]).then_inc(s_ys[s], 16)

            loops(sp, step)
            for s in range(2):
                sp.wait_ge(s_ys[s], 16 * ROUTED // 2)

        @block.gpsimd
        def _(pool):
            g = nc.gpsimd
            pool.memset(ident[:, :], 0.0).then_inc(s_id, 1)
            pool.wait_ge(s_id, 1)
            pool.affine_select(out=ident[:, :], in_=ident[:, :], compare_op=ALU.not_equal, fill=1.0,
                               base=0, pattern=[[-1, P]], channel_multiplier=1).then_inc(s_id, 1)

            def lower_w2(slot):
                g.tensor_tensor(w2_lo[:, slot], w2[:, slot], w2_hi[:, slot].bitcast(F32), ALU.subtract).then_inc(s_w2l, 1)

            pool.wait_ge(s_w2h, 1)
            lower_w2(1)
            pool.wait_ge(s_w2h, 2)
            lower_w2(0)
            moved_v = tokens.rearrange("(t p) d -> t p d", p=P)
            for tile in range(TT + 3):
                if tile < TT:
                    i = tile % 4
                    if tile >= 4:
                        pool.wait_ge(s_sc[i], 32 * (tile // 4))
                    pool.dma_start(moved[:, i, :], moved_v[tile]).then_inc(s_mv[i], 16)
                if tile >= 3:
                    back = tile - 3
                    i = back % 4
                    pool.wait_ge(s_mv[i], 16 * (back // 4 + 1))
                    for k in range(2):
                        pool.indirect_dma_start(out=routed[:, :], out_offset=bass.IndirectOffsetOnAxis(ap=slots[:, k, back:back + 1], axis=0),
                                                in_=moved[:, i, :], in_offset=None).then_inc(s_sc[i], 16)

            def pair(U, last=False):
                for s in range(1 if last else 2):
                    pool.wait_ge(s_w2h, U * 2 + (s + 3 - SHARED))
                    lower_w2(1 - s)

            with pool.Fori(S2, LAST) as u:
                pair(u)
            pair(LAST, True)

        @block.tensor
        def _(pe):
            mm = nc.tensor.matmul
            pe.wait_ge(s_id, 2)

            def transpose(parity):
                for r in range(2):
                    for c in range(C):
                        ins = nc.tensor.transpose(ps_t[:, c, r * P:(r + 1) * P], xt[:, parity, r, c * P:(c + 1) * P], ident[:, :])
                ins.then_inc(s_xt, 1)

            def fc(m, p, parity, slot):
                pe.wait_ge(s_g[p], m)
                for i in range(2):
                    n = 0
                    for k in range(C):
                        for w, x_ in ((w1_hi, xT_hi), (w1_hi, xT_lo), (w1_lo, xT_hi)):
                            ins = mm(ps_h[:, p, i, :], w[:, slot, k, 2 * p + i, :], x_[:, parity, k, :],
                                     start=n == 0, stop=n == 3 * C - 1)
                            n += 1
                ins.then_inc(s_h, 1)

            def proj(m, p, parity, slot):
                pe.wait_ge(s_hl[p], m + 1)
                for c in (2 * p, 2 * p + 1):
                    for r in range(2):
                        for n, (h, w) in enumerate(((h_hi, w2_hi), (h_hi, w2_lo), (h_lo, w2_hi))):
                            ins = mm(ps_y[:, r, 0:D], h[:, parity, c, r * P:(r + 1) * P], w[:, slot, c, :],
                                     start=c == 0 and n == 0, stop=c == HC - 1 and n == 2)
                if p == 3:
                    ins.then_inc(s_y, 1)

            pe.wait_ge(s_xl[0], 16)
            transpose(0)
            pe.wait_ge(s_xl[1], 16)
            pe.wait_ge(s_xlo, 1)
            transpose(1)
            pe.wait_ge(s_w1h, 1)
            pe.wait_ge(s_w1l, 1)
            for p in range(4):
                fc(0, p, 0, 1)
            pe.wait_ge(s_w2h, 1)
            pe.wait_ge(s_w2l, 1)

            def step(U, s, shared, left):
                m = U * 2 + s
                (slot1, n1), (slot2, n2) = slot_of(U, s, shared, 1), slot_of(U, s, shared, 0)
                if left >= 1:
                    pe.wait_ge(s_xlo, m + 2)
                    pe.wait_ge(s_w1h, n1)
                    pe.wait_ge(s_w1l, n1)
                for p in range(4):
                    if left >= 1:
                        fc(m + 1, p, 1 - s, slot1)
                    if p == 0:
                        pe.wait_ge(s_yv, m)
                        pe.wait_ge(s_w2h, n2)
                        pe.wait_ge(s_w2l, n2)
                    proj(m, p, s, slot2)
                    if p == 2 and left >= 2:
                        pe.wait_ge(s_xl[s], U * 16 + 32)
                        transpose(s)

            loops(pe, step)

        @block.scalar
        def _(act):
            def upper_w1(slot):
                act.activation(w1_hi[:, slot], w1[:, slot].rearrange("p k (m c) -> p k c m", c=HC), ACT.Copy).then_inc(s_w1h, 1)
                act.activation(b1_use[:, slot], b1[:, slot], ACT.Copy).then_inc(s_b1, 1)

            def upper_w2(slot):
                act.activation(w2_hi[:, slot], w2[:, slot], ACT.Copy).then_inc(s_w2h, 1)

            def upper_x(tile, parity):
                act.wait_ge(s_xt, tile + 1)
                act.activation(xT_hi[:, parity], ps_t[:, :, :], ACT.Copy).then_inc(s_xh, 1)

            def gelu(m, p, slot, n):
                act.wait_ge(s_h, m * 4 + (p + 1))
                act.wait_ge(s_hl[p], m)
                if p == 0:
                    act.wait_ge(s_b1, n)
                for i in range(2):
                    c = 2 * p + i
                    ins = act.activation(ht[:, p, i, :], ps_h[:, p, i, :], ACT.Gelu_apprx_tanh, bias=b1_use[:, slot, c:c + 1])
                ins.then_inc(s_g[p], 1)

            act.wait_ge(s_raw1[1], 32)
            upper_w1(1)
            upper_x(0, 0)
            upper_x(1, 1)
            act.wait_ge(s_raw2[1], 32)
            upper_w2(1)
            for p in range(4):
                gelu(0, p, 1, 1)
            act.wait_ge(s_raw1[0], 32)
            upper_w1(0)
            act.wait_ge(s_raw2[0], 32)
            upper_w2(0)

            def step(U, s, shared, left):
                m = U * 2 + s
                slot, n = slot_of(U, s, shared, 1)
                if not shared and left >= 1:
                    act.wait_ge(s_raw2[1 - s], (U - S2) * 32 + 64)
                    act.wait_ge(s_y, m)
                    upper_w2(1 - s)
                for p in range(4):
                    if left >= 1:
                        gelu(m + 1, p, slot, n)
                    if p == 1 and left >= 2 and (not shared or last_shared(U, s)):
                        act.wait_ge(s_raw1[s], (U - S2) * 32 + 32 * (2 + s))
                        upper_w1(s)
                    if p == 2 and left >= 2:
                        upper_x(m + 2, s)

            loops(act, step)

        @block.vector
        def _(dve):
            v = nc.vector

            def lower_w1(slot, n):
                dve.wait_ge(s_w1h, n)
                v.tensor_tensor(w1_lo[:, slot], w1[:, slot].rearrange("p k (m c) -> p k c m", c=HC),
                                w1_hi[:, slot].bitcast(F32), ALU.subtract).then_inc(s_w1l, 1)

            def bias_2(slot, n):
                dve.wait_ge(s_w2h, n)
                v.tensor_copy(b2_use[:, slot], b2[:, slot]).then_inc(s_b2, 1)

            def lower_x(tile, parity):
                dve.wait_ge(s_xh, tile + 1)
                v.tensor_tensor(xT_lo[:, parity], ps_t[:, :, :], xT_hi[:, parity].bitcast(F32), ALU.subtract).then_inc(s_xlo, 1)

            def hidden(m, p, parity):
                dve.wait_ge(s_g[p], m + 1)
                v.tensor_copy(h_hi[:, parity, 2 * p:2 * p + 2, :], ht[:, p]).then_inc(s_hh[p], 1)
                dve.wait_ge(s_hh[p], m + 1)
                v.tensor_tensor(h_lo[:, parity, 2 * p:2 * p + 2, :], ht[:, p], h_hi[:, parity, 2 * p:2 * p + 2, :].bitcast(F32),
                                ALU.subtract).then_inc(s_hl[p], 1)

            lower_w1(1, 1)
            lower_x(0, 0)
            lower_x(1, 1)
            bias_2(1, 1)
            for p in range(4):
                hidden(0, p, 0)
            lower_w1(0, 2)
            bias_2(0, 2)

            def step(U, s, shared, left):
                m = U * 2 + s
                slot, n = slot_of(U, s, shared, 0)
                if not shared and left >= 1:
                    dve.wait_ge(s_yv, m)
                    bias_2(1 - s, m - (SHARED - 3))
                for p in range(4):
                    if left >= 1:
                        hidden(m + 1, p, 1 - s)
                    if p == 1 and left >= 2 and (not shared or last_shared(U, s)):
                        lower_w1(s, m - (SHARED - 4))
                    if p == 2 and left >= 2:
                        lower_x(m + 2, s)
                dve.wait_ge(s_b2, n)
                dve.wait_ge(s_y, m + 1)
                if not shared:
                    dve.wait_ge(s_ys[s], (U - S2) * 16)
                v.tensor_tensor(y[:, s], ps_y[:, :, 0:D], b2_use[:, slot].unsqueeze(1).broadcast_to([P, 2, D]),
                                ALU.add).then_inc(s_yv, 1)
                if shared:
                    dve.wait_ge(s_yv, m + 1)
                    x2_tile = x2[:, bass.ds(U * 4 + 2 * s, 2), :]
                    v.tensor_tensor(x2_tile, x2_tile, y[:, s], ALU.add)

            loops(dve, step, first=1)


def combine(nc, x2, slots, gates, ys, out):
    NB, PAIRS = 4, TT // 2
    with ExitStack() as ctx:
        t = Tools(nc, ctx)
        y = t.sb("c_y", [P, NB, 2, 2, D])
        s_y = [t.sem("c_y%d" % i) for i in range(NB)]
        s_half, s_sum, s_out = t.sem("c_half"), t.sem("c_sum"), t.sem("c_out")
        block = ctx.enter_context(nc.Block())
        out_v = out.rearrange("b (g t p) d -> (b g) p t d", t=2, p=P)

        @block.gpsimd
        def _(pool):
            for k in range(PAIRS):
                i = k % NB
                if k >= NB:
                    pool.wait_ge(s_y[i], 64 * (k // NB))
                    pool.wait_ge(s_sum, 2 * (k - NB + 1))
                for tile in range(2):
                    for j in range(2):
                        pool.indirect_dma_start(out=y[:, i, tile, j, :], out_offset=None, in_=ys[:, :],
                                                in_offset=bass.IndirectOffsetOnAxis(ap=slots[:, j, 2 * k + tile:2 * k + tile + 1], axis=0)
                                                ).then_inc(s_y[i], 16)

        @block.vector
        def _(dve):
            for k in range(PAIRS):
                i = k % NB
                dve.wait_ge(s_y[i], 64 * (k // NB + 1))
                for j, done in enumerate((s_half, s_sum)):
                    if j:
                        dve.wait_ge(s_half, 2 * k + 2)
                    for tile in range(2):
                        n = 2 * k + tile
                        nc.vector.scalar_tensor_tensor(x2[:, n, :], y[:, i, tile, j, :], gates[:, n, j:j + 1], x2[:, n, :],
                                                       ALU.mult, ALU.add).then_inc(done, 1)

        @block.sync
        def _(sp):
            for k in range(PAIRS):
                sp.wait_ge(s_sum, 2 * k + 2)
                sp.dma_start(out_v[k], x2[:, 2 * k:2 * k + 2, :]).then_inc(s_out, 16)
            sp.wait_ge(s_out, 16 * PAIRS)


NAMES = ["x", "ctx_1024", "mask_BxS2_bf1"] + ["L0_xattn_" + n for n in (
    "ln_x_g", "ln_x_b", "ln_l_g", "ln_l_b", "qn_g", "kn_g", "Wq", "Wkv", "Wout", "bout")] + ["L0_ffn_" + n for n in (
    "Wfc_s", "bfc_s", "Wproj_s", "bproj_s", "Wr", "Wfc", "bfc", "Wproj", "bproj")]


def cross_attention_moe(nc, x, ctx_in, mask, ln_x_g, ln_x_b, ln_l_g, ln_l_b, qn_g, kn_g, Wq, Wkv, Wout, bout,
                        Wfc_s, bfc_s, Wproj_s, bproj_s, Wr, Wfc, bfc, Wproj, bproj, out):
    def dram(name, *shape):
        return nc.dram_tensor(name + "_dram", shape, F32, kind="Internal").ap()

    lnT = dram("lnT", B, P, 2, C, KEYS)
    wHead = dram("wHead", H, P, 2, C, 3 * DH)
    maskRow, maskCol = dram("maskRow", B, P), dram("maskCol", P, B)
    attT = dram("attT", HEADS, DH + 1, N)
    rden = dram("rden", HEADS, N)
    tokens = dram("tokens", TOKENS, D)
    routed = dram("routed", ROWS, D)
    ys = dram("ys", ROUTED * TS, D)
    prepare(nc, x, ctx_in, mask, ln_x_g, ln_x_b, ln_l_g, ln_l_b, Wq, Wkv, lnT, wHead, maskRow, maskCol)
    attention(nc, qn_g, kn_g, lnT, wHead, maskRow, maskCol, attT, routed)
    with ExitStack() as ctx:
        t = Tools(nc, ctx)
        x2 = t.sb("x2", [P, TT, D])
        slots = t.sb("slots", [P, 2, TT], U32)
        gates = t.sb("gates", [P, TT, 2])
        expert = t.sb("expert", [P, ROUTED + 2], I32)
        logit = t.sb("logit", [P, TT, E])
        project_out(nc, x, Wout, bout, Wr, attT, rden, tokens, x2, logit)
        route(nc, logit, slots, gates, expert)
        experts(nc, [Wfc_s, bfc_s, Wproj_s, bproj_s], [Wfc, bfc, Wproj, bproj], expert, slots, tokens, routed, x2, ys)
        combine(nc, x2, slots, gates, ys, out)


def kernel(**inputs):
    import numpy as np
    import concourse.bacc as bacc
    from concourse.bass_utils import run_bass_kernel_spmd

    nc = bacc.Bacc("TRN2", target_bir_lowering=False, num_devices=1)
    arrays, args = {}, []
    for name in NAMES:
        a = np.ascontiguousarray(inputs[name])
        if a.dtype == np.bool_:
            a = a.view(np.uint8)
        arrays["in_" + name] = a
        args.append(nc.dram_tensor("in_" + name, a.shape, mybir.dt.from_np(a.dtype), kind="ExternalInput").ap())
    args.append(nc.dram_tensor("out_dram", (B, N, D), F32, kind="ExternalOutput").ap())
    cross_attention_moe(nc, *args)
    r = run_bass_kernel_spmd(nc, [arrays], core_ids=[0])
    return r.results[0]["out_dram"]
```
